# Optimizing a Trainium2 kernel written in Bass

```python
import numpy as np
import jax
import jax.numpy as jnp

def _softmax(x, axis=-1):
    return jax.nn.softmax(x, axis=axis)

def _gelu(x):
    return jax.nn.gelu(x, approximate=True)

def _silu(x):
    return jax.nn.silu(x)

def _sigmoid(x):
    return jax.nn.sigmoid(x)

def _layernorm(x, axis=-1, eps=1e-05):
    m = jnp.mean(x, axis=axis, keepdims=True)
    v = jnp.var(x, axis=axis, keepdims=True)
    return (x - m) / jnp.sqrt(v + eps)

def _scatter_add(tgt, idx, src, axis=0):
    return tgt.at[idx].add(src)

def _segment_sum(src, seg, n):
    return jax.ops.segment_sum(src, seg, n)
kernel_name = 'mk_flamingo_gated_d2_seqx_r4_d2841c'

def setup_inputs(seed: int=0):
    np.random.seed(seed)
    _w = jnp.asarray

    def _rec_inputs():
        import jax
        import jax.numpy as jnp
        _rk = jax.random.key(seed)
        x = 7.22e-05 + 1 * jax.random.normal(jax.random.fold_in(_rk, 1), (8, 256, 256), jnp.float32)
        _lenS = 256 - jax.random.randint(jax.random.fold_in(_rk, 7), (8,), 0, max(1, 256 // 4) + 1, jnp.int32)
        _lenS2 = 256 - jax.random.randint(jax.random.fold_in(_rk, 8), (8,), 0, max(1, 256 // 4) + 1, jnp.int32)
        _ctx_768P = jax.random.normal(jax.random.fold_in(_rk, 11), (8, 16, 192), jnp.float32)
        _ctx_768c = jax.random.dirichlet(jax.random.fold_in(_rk, 511), 0.3 * jnp.ones((16,), jnp.float32), (8, 256))
        _ctx_768t = jnp.einsum('bsk,bkd->bsd', _ctx_768c, _ctx_768P)
        _ctx_768t = _ctx_768t * jax.lax.rsqrt(jnp.mean(jnp.square(_ctx_768t)) + 1e-12) * 0.953939
        ctx_768 = 2.09791e-05 + 1.00001 * (_ctx_768t + 0.3 * jax.random.normal(jax.random.fold_in(_rk, 611), (8, 256, 192), jnp.float32))
        _g = jax.random.normal(jax.random.fold_in(_rk, 9001), (2, 2), jnp.float32)
        _g = jnp.sign(_g) * jnp.maximum(jnp.abs(_g), 1.0) + (_g == 0) * 1.0
        g_xattn = _g[0]
        g_ffn = _g[1]
        return (x, ctx_768, g_xattn, g_ffn)
    x, ctx_768, g_xattn, g_ffn = _rec_inputs()

    def _L0_xattn_setup():
        import jax, jax.numpy as jnp
        import numpy as np
        NUM_HEADS = 16
        key = jax.random.key(seed)
        ks = jax.random.split(key, 8)
        dim, cond_dim = (256, 192)
        B, N, condN = (4, 512, 256)
        s = lambda k, shp, fan: jax.random.normal(k, shp, dtype=jnp.float32) * fan ** (-0.5)
        return {'x': jax.random.normal(ks[0], (B, N, dim), dtype=jnp.float32), 'cond': jax.random.normal(ks[1], (B, condN, cond_dim), dtype=jnp.float32), 'q_w': s(ks[2], (dim, dim), dim), 'q_b': jnp.zeros((dim,), jnp.float32), 'kv_w': s(ks[3], (cond_dim, 2 * dim), cond_dim), 'kv_b': jnp.zeros((2 * dim,), jnp.float32), 'proj_w': s(ks[4], (dim, dim), dim), 'proj_b': jnp.zeros((dim,), jnp.float32)}
    _L0_xattn_all = _L0_xattn_setup()
    _L0_xattn_in = {k: v for k, v in _L0_xattn_all.items() if k in ('q_w', 'q_b', 'kv_w', 'kv_b', 'proj_w', 'proj_b')}
    del _L0_xattn_all

    def _L0_ffn_setup():
        import jax, jax.numpy as jnp
        import numpy as np
        E, H, I = (8, 256, 128)
        NG, TKG, TOPK = (4, 2, 4)
        SCALE = 2.5

        def _mlp(x, wg, wu, wd):
            return jax.nn.silu(x @ wg) * (x @ wu) @ wd
        key = jax.random.key(seed)
        ks = jax.random.split(key, 8)
        s = 0.02
        return {'hidden_states': jax.random.normal(ks[0], (32, 64, H), jnp.float32), 'gate_w': jax.random.normal(ks[1], (E, H), jnp.float32) * np.float32(np.sqrt(2.0 / H)), 'correction_bias': jnp.zeros((E,), jnp.float32), 'Wg': jax.random.normal(ks[2], (E, H, I), jnp.float32) * s, 'Wu': jax.random.normal(ks[3], (E, H, I), jnp.float32) * s, 'Wd': jax.random.normal(ks[4], (E, I, H), jnp.float32) * s, 'Wg_s': jax.random.normal(ks[5], (H, I), jnp.float32) * s, 'Wu_s': jax.random.normal(ks[6], (H, I), jnp.float32) * s, 'Wd_s': jax.random.normal(ks[7], (I, H), jnp.float32) * s}
    _L0_ffn_all = _L0_ffn_setup()
    _L0_ffn_in = {k: v for k, v in _L0_ffn_all.items() if k in ('gate_w', 'correction_bias', 'Wg', 'Wu', 'Wd', 'Wg_s', 'Wu_s', 'Wd_s')}
    del _L0_ffn_all

    def _L1_xattn_setup():
        import jax, jax.numpy as jnp
        import numpy as np
        NUM_HEADS = 16
        CLAMP = 10000.0
        key = jax.random.key(seed)
        ks = jax.random.split(key, 8)
        B, Nq, Nkv, Cq, Ckv = (4, 512, 512, 256, 192)
        s_q = 1.0 / np.sqrt(Cq)
        s_kv = 1.0 / np.sqrt(Ckv)
        return {'query': jax.random.normal(ks[0], (B, Nq, Cq), jnp.float32), 'key_value': jax.random.normal(ks[1], (B, Nkv, Ckv), jnp.float32), 'Wq': jax.random.normal(ks[2], (Cq, Cq), jnp.float32) * s_q, 'bq': jnp.zeros((Cq,), jnp.float32), 'Wk': jax.random.normal(ks[3], (Ckv, Cq), jnp.float32) * s_kv, 'bk': jnp.zeros((Cq,), jnp.float32), 'Wv': jax.random.normal(ks[4], (Ckv, Cq), jnp.float32) * s_kv, 'bv': jnp.zeros((Cq,), jnp.float32), 'Wo': jax.random.normal(ks[5], (Cq, Cq), jnp.float32) * s_q, 'bo': jnp.zeros((Cq,), jnp.float32)}
    _L1_xattn_all = _L1_xattn_setup()
    _L1_xattn_in = {k: v for k, v in _L1_xattn_all.items() if k in ('Wq', 'bq', 'Wk', 'bk', 'Wv', 'bv', 'Wo', 'bo')}
    del _L1_xattn_all

    def _L1_ffn_setup():
        import jax, jax.numpy as jnp
        import numpy as np
        NEG_INF = jnp.float32(-1000000000.0)

        def _router(x, Wr, br, top_k=2):
            logits = jnp.einsum('bsd,de->bse', x, Wr) + br
            _, top_idx = jax.lax.top_k(logits, top_k)
            num_experts = logits.shape[-1]
            mask = jnp.any(top_idx[..., None] == jnp.arange(num_experts), axis=-2)
            sparse_logits = jnp.where(mask, logits, NEG_INF)
            weights = jax.nn.softmax(sparse_logits, axis=-1)
            return (weights, top_idx, mask)
        key = jax.random.key(seed)
        ks = jax.random.split(key, 8)
        B, S, D, E, H = (4, 512, 256, 8, 1024)
        sd = 1.0 / np.sqrt(D)
        sh = 1.0 / np.sqrt(H)
        x = jax.random.normal(ks[0], (B, S, D), dtype=jnp.float32)
        Wr = jax.random.normal(ks[1], (D, E), dtype=jnp.float32) * sd
        br = jnp.zeros((E,), dtype=jnp.float32)
        W1 = jax.random.normal(ks[2], (E, D, H), dtype=jnp.float32) * sd
        b1 = jnp.zeros((E, H), dtype=jnp.float32)
        W2 = jax.random.normal(ks[3], (E, H, D), dtype=jnp.float32) * sh
        b2 = jnp.zeros((E, D), dtype=jnp.float32)
        return {'x': x, 'Wr': Wr, 'br': br, 'W1': W1, 'b1': b1, 'W2': W2, 'b2': b2}
    _L1_ffn_all = _L1_ffn_setup()
    _L1_ffn_in = {k: v for k, v in _L1_ffn_all.items() if k in ('Wr', 'br', 'W1', 'b1', 'W2', 'b2')}
    del _L1_ffn_all
    return {'x': x, 'ctx_768': ctx_768, 'g_xattn': g_xattn, 'g_ffn': g_ffn, 'L0_xattn_q_w': _L0_xattn_in['q_w'], 'L0_xattn_q_b': _L0_xattn_in['q_b'], 'L0_xattn_kv_w': _L0_xattn_in['kv_w'], 'L0_xattn_kv_b': _L0_xattn_in['kv_b'], 'L0_xattn_proj_w': _L0_xattn_in['proj_w'], 'L0_xattn_proj_b': _L0_xattn_in['proj_b'], 'L0_ffn_gate_w': _L0_ffn_in['gate_w'], 'L0_ffn_correction_bias': _L0_ffn_in['correction_bias'], 'L0_ffn_Wg': _L0_ffn_in['Wg'], 'L0_ffn_Wu': _L0_ffn_in['Wu'], 'L0_ffn_Wd': _L0_ffn_in['Wd'], 'L0_ffn_Wg_s': _L0_ffn_in['Wg_s'], 'L0_ffn_Wu_s': _L0_ffn_in['Wu_s'], 'L0_ffn_Wd_s': _L0_ffn_in['Wd_s'], 'L1_xattn_Wq': _L1_xattn_in['Wq'], 'L1_xattn_bq': _L1_xattn_in['bq'], 'L1_xattn_Wk': _L1_xattn_in['Wk'], 'L1_xattn_bk': _L1_xattn_in['bk'], 'L1_xattn_Wv': _L1_xattn_in['Wv'], 'L1_xattn_bv': _L1_xattn_in['bv'], 'L1_xattn_Wo': _L1_xattn_in['Wo'], 'L1_xattn_bo': _L1_xattn_in['bo'], 'L1_ffn_Wr': _L1_ffn_in['Wr'], 'L1_ffn_br': _L1_ffn_in['br'], 'L1_ffn_W1': _L1_ffn_in['W1'], 'L1_ffn_b1': _L1_ffn_in['b1'], 'L1_ffn_W2': _L1_ffn_in['W2'], 'L1_ffn_b2': _L1_ffn_in['b2']}

def reference(x, ctx_768, g_xattn, g_ffn, L0_xattn_q_w, L0_xattn_q_b, L0_xattn_kv_w, L0_xattn_kv_b, L0_xattn_proj_w, L0_xattn_proj_b, L0_ffn_gate_w, L0_ffn_correction_bias, L0_ffn_Wg, L0_ffn_Wu, L0_ffn_Wd, L0_ffn_Wg_s, L0_ffn_Wu_s, L0_ffn_Wd_s, L1_xattn_Wq, L1_xattn_bq, L1_xattn_Wk, L1_xattn_bk, L1_xattn_Wv, L1_xattn_bv, L1_xattn_Wo, L1_xattn_bo, L1_ffn_Wr, L1_ffn_br, L1_ffn_W1, L1_ffn_b1, L1_ffn_W2, L1_ffn_b2):
    import jax
    import jax.numpy as jnp

    def _L0_xattn_ref(x, cond, q_w, q_b, kv_w, kv_b, proj_w, proj_b):
        import jax, jax.numpy as jnp
        import numpy as np
        NUM_HEADS = 16
        B, N, C = x.shape
        condN = cond.shape[1]
        H = NUM_HEADS
        hd = C // H
        scale = hd ** (-0.5)
        q = (x @ q_w + q_b).reshape(B, N, H, hd).transpose(0, 2, 1, 3)
        kv = (cond @ kv_w + kv_b).reshape(B, condN, 2, H, hd)
        k = kv[:, :, 0].transpose(0, 2, 1, 3)
        v = kv[:, :, 1].transpose(0, 2, 1, 3)
        attn = jnp.einsum('bhnd,bhmd->bhnm', q * scale, k)
        attn = jax.nn.softmax(attn, axis=-1)
        out = jnp.einsum('bhnm,bhmd->bhnd', attn, v)
        out = out.transpose(0, 2, 1, 3).reshape(B, N, C)
        return out @ proj_w + proj_b

    def _L0_ffn_ref(hidden_states, gate_w, correction_bias, Wg, Wu, Wd, Wg_s, Wu_s, Wd_s):
        import jax, jax.numpy as jnp
        import numpy as np
        E, H, I = (8, 256, 128)
        NG, TKG, TOPK = (4, 2, 4)
        SCALE = 2.5

        def _mlp(x, wg, wu, wd):
            return jax.nn.silu(x @ wg) * (x @ wu) @ wd
        B, T, _ = hidden_states.shape
        x = hidden_states.reshape(-1, H)
        N = x.shape[0]
        logits = x @ gate_w.T
        scores = jax.nn.sigmoid(logits)
        scores_c = scores + correction_bias
        grp = scores_c.reshape(N, NG, E // NG)
        group_scores = jnp.sum(jax.lax.top_k(grp, 2)[0], axis=-1)
        grp_idx = jax.lax.top_k(group_scores, TKG)[1]
        group_mask = jnp.zeros_like(group_scores).at[jnp.arange(N)[:, None], grp_idx].set(1.0)
        score_mask = jnp.repeat(group_mask, E // NG, axis=-1) > 0.5
        scores_for_choice = jnp.where(score_mask, scores_c, 0.0)
        topk_idx = jax.lax.top_k(scores_for_choice, TOPK)[1]
        topk_w = jnp.take_along_axis(scores, topk_idx, axis=-1)
        topk_w = topk_w / (jnp.sum(topk_w, axis=-1, keepdims=True) + 1e-20)
        topk_w = topk_w * SCALE
        cw = jnp.sum(jax.nn.one_hot(topk_idx, E, dtype=topk_w.dtype) * topk_w[..., None], axis=1)
        g = jnp.einsum('nh,ehi->eni', x, Wg)
        u = jnp.einsum('nh,ehi->eni', x, Wu)
        y = jnp.einsum('eni,eih->enh', jax.nn.silu(g) * u, Wd)
        routed = jnp.einsum('enh,ne->nh', y, cw)
        out = routed + _mlp(x, Wg_s, Wu_s, Wd_s)
        return out.reshape(B, T, H)

    def _L1_xattn_ref(query, key_value, Wq, bq, Wk, bk, Wv, bv, Wo, bo):
        import jax, jax.numpy as jnp
        import numpy as np
        NUM_HEADS = 16
        CLAMP = 10000.0
        B, Nq, Cq = query.shape
        Nkv = key_value.shape[1]
        H = NUM_HEADS
        D = Cq // H
        scale = D ** (-0.5)
        q = (query @ Wq + bq).reshape(B, Nq, H, D).transpose(0, 2, 1, 3)
        k = (key_value @ Wk + bk).reshape(B, Nkv, H, D).transpose(0, 2, 1, 3)
        v = (key_value @ Wv + bv).reshape(B, Nkv, H, D).transpose(0, 2, 1, 3)
        attn = jnp.einsum('bhqd,bhkd->bhqk', q, k) * scale
        attn = jnp.clip(attn, -CLAMP, CLAMP)
        attn = jax.nn.softmax(attn, axis=-1)
        attn = jnp.where(jnp.any(jnp.isnan(attn)), jnp.asarray(1.0 / Nkv, attn.dtype), attn)
        x = jnp.einsum('bhqk,bhkd->bqhd', attn, v).reshape(B, Nq, Cq)
        return x @ Wo + bo

    def _L1_ffn_ref(x, Wr, br, W1, b1, W2, b2):
        import jax, jax.numpy as jnp
        import numpy as np
        NEG_INF = jnp.float32(-1000000000.0)

        def _router(x, Wr, br, top_k=2):
            logits = jnp.einsum('bsd,de->bse', x, Wr) + br
            _, top_idx = jax.lax.top_k(logits, top_k)
            num_experts = logits.shape[-1]
            mask = jnp.any(top_idx[..., None] == jnp.arange(num_experts), axis=-2)
            sparse_logits = jnp.where(mask, logits, NEG_INF)
            weights = jax.nn.softmax(sparse_logits, axis=-1)
            return (weights, top_idx, mask)
        weights, top_idx, mask = _router(x, Wr, br, top_k=2)
        num_experts = W1.shape[0]
        out = jnp.zeros_like(x)
        for e in range(num_experts):
            h = jax.nn.relu(jnp.einsum('bsd,dh->bsh', x, W1[e]) + b1[e])
            y = jnp.einsum('bsh,hd->bsd', h, W2[e]) + b2[e]
            w = weights[:, :, e] * mask[:, :, e].astype(x.dtype)
            out = out + y * w[:, :, None]
        return out
    x = x + jnp.tanh(g_xattn[0]) * _L0_xattn_ref(_layernorm(x, axis=-1), ctx_768, L0_xattn_q_w, L0_xattn_q_b, L0_xattn_kv_w, L0_xattn_kv_b, L0_xattn_proj_w, L0_xattn_proj_b)
    x = x + jnp.tanh(g_ffn[0]) * _L0_ffn_ref(_layernorm(x, axis=-1), L0_ffn_gate_w, L0_ffn_correction_bias, L0_ffn_Wg, L0_ffn_Wu, L0_ffn_Wd, L0_ffn_Wg_s, L0_ffn_Wu_s, L0_ffn_Wd_s)
    x = x + jnp.tanh(g_xattn[1]) * _L1_xattn_ref(_layernorm(x, axis=-1), ctx_768, L1_xattn_Wq, L1_xattn_bq, L1_xattn_Wk, L1_xattn_bk, L1_xattn_Wv, L1_xattn_bv, L1_xattn_Wo, L1_xattn_bo)
    x = x + jnp.tanh(g_ffn[1]) * _L1_ffn_ref(_layernorm(x, axis=-1), L1_ffn_Wr, L1_ffn_br, L1_ffn_W1, L1_ffn_b1, L1_ffn_W2, L1_ffn_b2)
    return x

_drawn_inputs = setup_inputs


def setup_inputs(seed=0):
    import zlib

    import numpy as np

    out = dict(_drawn_inputs(seed))
    spreads = {'g_ffn': (-1.0, 0.599),
     'L0_xattn_q_b': (0.0, 0.1),
     'L0_xattn_kv_b': (0.0, 0.1),
     'L0_xattn_proj_b': (0.0, 0.1),
     'L0_ffn_correction_bias': (0.0, 0.513),
     'L1_xattn_bq': (0.0, 0.1),
     'L1_xattn_bk': (0.0, 0.8),
     'L1_xattn_bv': (0.0, 0.1),
     'L1_xattn_bo': (0.0, 0.1),
     'L1_ffn_br': (0.0, 0.1),
     'L1_ffn_b1': (0.0, 0.1),
     'L1_ffn_b2': (0.0, 0.1)}
    factors = {'L0_ffn_gate_w': 2.746}
    for name, (base, spread) in spreads.items():
        noise = np.random.default_rng([zlib.crc32(name.encode()), seed]).standard_normal(out[name].shape)
        drawn = base * np.exp(spread * noise) if base else spread * noise
        out[name] = jnp.asarray(drawn.astype(out[name].dtype))
    for name, factor in factors.items():
        out[name] = (out[name] * factor).astype(out[name].dtype)
    return out
```

```python
from contextlib import ExitStack
from functools import partial

import concourse.bass as bass
from concourse import mybir

F32 = mybir.dt.float32
F32R = mybir.dt.float32r
I32 = mybir.dt.int32
U32 = mybir.dt.uint32
ALU = mybir.AluOpType
ACT = mybir.ActivationFunctionType
AX = mybir.AxisListType.X

P = 128
NB, S, D = 8, 256, 256
CTX = 192
H, HD = 16, 16
TT = S // P
NT = NB * TT
KC = D // P
E0, I0 = 8, 128
NG, TKG, TOPK0 = 4, 2, 4
E1, H1, TOPK1 = 8, 1024, 2
JH = H1 // P
BLOCKS = NB * S * TOPK1 // P + E1 - 1
CLAMP = 10000.0
EPS = 1e-5
QSCALE = HD ** -0.5
NEG_INF = -1e9

STACK = 4 * HD
FULL = 96
ROWS = FULL + 2


class Queue:

    def __init__(self, eng, sem):
        self.eng, self.sem, self.ops, self.count, self.seen = eng, sem, [], 0, {}

    def wait(self, *marks):
        for mark in marks:
            if mark is None:
                continue
            sem, value = mark
            if self.seen.get(sem.name, 0) < value:
                self.seen[sem.name] = value
                self.ops.append(partial(self.eng.wait_ge, sem, value))

    def put(self, fn):
        self.ops.append(fn)

    def mark(self, fn):
        self.count += 1
        self.ops.append(lambda: fn().then_inc(self.sem, 1))
        return (self.sem, self.count)

    def load(self, sem, fn):
        sem.total += 16
        self.ops.append(lambda: fn().then_inc(sem.sem, 16))
        return (sem.sem, sem.total)

    def play(self):
        for op in self.ops:
            op()


class DmaSem:
    def __init__(self, sem):
        self.sem, self.total = sem, 0


class Slot:

    def __init__(self, t):
        self.t, self.free, self.held = t, [], False


class Ring:
    def __init__(self, slots):
        self.slots, self.n = slots, -1

    def take(self):
        self.n += 1
        while self.slots[self.n % len(self.slots)].held:
            self.n += 1
        return self.slots[self.n % len(self.slots)]


def weave(*stages):
    live = [[0, n, g] for g, n in stages]
    while live:
        s = min(live, key=lambda s: s[0] / s[1])
        s[0] += 1
        if next(s[2], "end") == "end":
            live.remove(s)


def build(nc, a, out):
    es = ExitStack()
    tens = ExitStack()

    def sem(name):
        return es.enter_context(nc.semaphore(name))

    def sb(name, shape, dt=F32, scope=None):
        return (scope or es).enter_context(nc.sbuf_tensor(name, shape, dt))

    def dma_sem(name):
        return DmaSem(sem(name))

    PE, DV, AC, PO, SP = (Queue(eng, sem(n)) for eng, n in (
        (nc.tensor, "pe_done"), (nc.vector, "dve_done"), (nc.scalar, "act_done"), (nc.gpsimd, "pool_done"),
        (nc.sync, "sp_done")))

    qk_dram = [nc.dram_tensor(f"qk_{l}", (NB, 4, D, S), F32).ap() for l in range(2)]
    max_dram = [nc.dram_tensor(f"max_{l}", (NB, 3 * H * TT, P), F32).ap() for l in range(2)]
    ctxT_dram = nc.dram_tensor("ctx_t", (NB, 2, P, S), F32).ap()
    z_dram = nc.dram_tensor("z_rows", (NB, S, D), F32).ap()
    vmean_dram = nc.dram_tensor("vmean", (NB, D), F32).ap()
    zalt_dram = nc.dram_tensor("zalt_rows", (NB, D), F32).ap()
    xs_dram = nc.dram_tensor("xs", (BLOCKS * P, D), F32).ap()
    ys_dram = nc.dram_tensor("ys", (BLOCKS * P, D), F32).ap()

    banks = [es.enter_context(nc.psum_tensor(f"bank{i}", [P, 512], F32)) for i in range(8)]
    score_banks = Ring([Slot(banks[0]), Slot(banks[1])])
    shifted_banks = Ring([Slot(banks[2]), Slot(banks[3])])
    value_bank = Slot(banks[4])
    work_banks = Ring([Slot(banks[i]) for i in (5, 6, 7)])

    x = sb("x", [P, NT, D])
    ident = sb("ident", [P, P])
    ones = sb("ones", [P, P])
    tg = sb("tg", [P, 4])
    zero_row = sb("zero_row", [P, D])
    g_raw = sb("g_raw", [P, 4])
    stats_ring = Ring([Slot(sb(f"stats{i}", [P, TT, 6])) for i in range(3)])
    moments_ring = Ring([Slot(sb(f"moments{i}", [P, TT, 2])) for i in range(3)])
    rstd_ring = Ring([Slot(sb(f"rstd{i}", [P, 4, TT])) for i in range(3)])
    minus_half = sb("minus_half", [P, TT])
    before = sb("before", [P, 8, 8])
    after = sb("after", [P, 8, 8])
    keep_row = sb("keep_row", [P, D], I32)
    x_free = [None] * NT

    wait_const = []

    def const(fn):
        PO.wait(*wait_const[-1:])
        m = PO.mark(fn)
        wait_const.append(m)
        return m

    const(partial(nc.gpsimd.memset, ident[:, :], 0.0))
    ident_ready = const(partial(nc.gpsimd.affine_select, out=ident[:, :], in_=ident[:, :], compare_op=ALU.not_equal,
                                                  fill=1.0, base=0, pattern=[[-1, P]], channel_multiplier=1))
    const(partial(nc.gpsimd.memset, ones[:, :], 1.0))
    zero_ready = const(partial(nc.gpsimd.memset, zero_row[:, :], 0.0))

    gates_in = dma_sem("gates_in")
    SP.load(gates_in, partial(nc.sync.dma_start, g_raw[:, 0:2], a["g_xattn"].partition_broadcast(P)))
    m = SP.load(gates_in, partial(nc.sync.dma_start, g_raw[:, 2:4], a["g_ffn"].partition_broadcast(P)))
    AC.wait(m)
    tg_ready = AC.mark(partial(nc.scalar.activation, tg[:, :], g_raw[:, :], ACT.Tanh))

    A = tens

    def sba(name, shape, dt=F32):
        return sb(name, shape, dt, A)

    x_in = [dma_sem(f"x_in{b}") for b in range(NB)]

    def load_x(b):
        m = SP.load(x_in[b], partial(nc.sync.dma_start, 
            x[:, TT * b:TT * b + TT, :], a["x"][b].rearrange("(t p) d -> p t d", p=P)))
        for t in range(TT):
            x_free[TT * b + t] = m

    ctx_tok = Ring([Slot(sba(f"ctx_tok{i}", [P, TT, CTX])) for i in range(2)])
    ctx_in = [dma_sem(f"ctx_in{i}") for i in range(2)]

    wq = [sba(f"wq{l}", [P, KC, D]) for l in range(2)]
    wkv = [sba(f"wkv{l}", [P, 2, 2 * D]) for l in range(2)]
    wo = [sba(f"wo{l}", [P, KC, D]) for l in range(2)]
    qkb = [sba(f"qkb{l}", [P, 2, KC]) for l in range(2)]
    vb = [sba(f"vb{l}", [P, D]) for l in range(2)]
    ob = [sba(f"ob{l}", [P, D]) for l in range(2)]
    attn_w_in = [dma_sem(f"attn_w_in{l}") for l in range(2)]
    attn_w = [None, None]

    def load_attention_weights(l):
        if l == 0:
            q_w, q_b, o_w, o_b = a["L0_xattn_q_w"], a["L0_xattn_q_b"], a["L0_xattn_proj_w"], a["L0_xattn_proj_b"]
            k_w, v_w = a["L0_xattn_kv_w"][:, 0:D], a["L0_xattn_kv_w"][:, D:2 * D]
            k_b, v_b = a["L0_xattn_kv_b"][0:D], a["L0_xattn_kv_b"][D:2 * D]
        else:
            q_w, q_b, o_w, o_b = a["L1_xattn_Wq"], a["L1_xattn_bq"], a["L1_xattn_Wo"], a["L1_xattn_bo"]
            k_w, v_w, k_b, v_b = a["L1_xattn_Wk"], a["L1_xattn_Wv"], a["L1_xattn_bk"], a["L1_xattn_bv"]
        q_col, k_col = q_b.rearrange("(k p) -> p k", p=P), k_b.rearrange("(k p) -> p k", p=P)
        for dst, src in (
            (wq[l][:, :, :], q_w.rearrange("(k p) n -> p k n", p=P)),
            (qkb[l][:, 0, :], q_col),
            (qkb[l][:, 1, :], k_col),
            (wkv[l][:, 0, 0:D], k_w[0:P, :]),
            (wkv[l][0:CTX - P, 1, 0:D], k_w[P:CTX, :]),
            (wkv[l][:, 0, D:2 * D], v_w[0:P, :]),
            (wkv[l][0:CTX - P, 1, D:2 * D], v_w[P:CTX, :]),
            (vb[l][:, :], v_b.partition_broadcast(P)),
            (wo[l][:, :, :], o_w.rearrange("(k p) n -> p k n", p=P)),
            (ob[l][:, :], o_b.partition_broadcast(P)),
        ):
            columns = src is q_col or src is k_col
            attn_w[l] = SP.load(attn_w_in[l], partial(nc.sync.dma_start, 
                dst, src, allow_slow_non_contiguous=columns))

    def load_ctx(b):
        slot = ctx_tok.take()
        SP.wait(*slot.free)
        slot.ready = SP.load(ctx_in[b % 2], partial(nc.sync.dma_start, 
            slot.t[:, :, :], a["ctx_768"][b].rearrange("(t p) d -> p t d", p=P)))
        return slot

    load_x(0)
    first_ctx = load_ctx(0)
    load_attention_weights(0)

    w_gate0 = sba("w_gate0", [P, KC, E0 + 1, I0])
    w_up0 = sba("w_up0", [P, KC, E0 + 1, I0])
    w_down0 = sba("w_down0", [P, E0 + 1, D])
    gate_rows = sba("gate_rows", [E0, D])
    gate_wT = sba("gate_wT", [P, KC, E0])
    corr = sba("corr", [P, E0])
    ffn0_in = dma_sem("ffn0_in")
    ffn0_w = None
    loads0 = [(gate_rows[:, :], a["L0_ffn_gate_w"]),
              (corr[:, :], a["L0_ffn_correction_bias"].partition_broadcast(P))]
    for k in range(KC):
        rows = slice(k * P, k * P + P)
        for t, w, shared in ((w_gate0, a["L0_ffn_Wg"], a["L0_ffn_Wg_s"]), (w_up0, a["L0_ffn_Wu"], a["L0_ffn_Wu_s"])):
            loads0.append((t[:, k, 0:E0, :], w[:, rows, :].rearrange("e p i -> p e i")))
            loads0.append((t[:, k, E0, :], shared[rows, :]))
    loads0.append((w_down0[:, 0:E0, :], a["L0_ffn_Wd"].rearrange("e i d -> i e d")))
    loads0.append((w_down0[:, E0, :], a["L0_ffn_Wd_s"]))

    def load_experts0():
        nonlocal ffn0_w
        for dst, src in loads0:
            ffn0_w = SP.load(ffn0_in, partial(nc.sync.dma_start, dst, src))

    stack_q = [Slot(sba(f"stack_q{l}", [ROWS, H, S], F32R)) for l in range(2)]
    stack_k = [Slot(sba(f"stack_k{l}", [ROWS, H, S], F32R)) for l in range(2)]
    values = [Slot(sba(f"values{l}", [P, 2, H, 2 * HD])) for l in range(2)]
    xn = Ring([Slot(sba(f"xn{i}", [P, TT, D])) for i in range(2)])
    xnT = Ring([Slot(sba(f"xnT{i}", [P, KC, S])) for i in range(2)])
    ctxT = Ring([Slot(sba(f"ctxT{i}", [P, 2, S])) for i in range(2)])
    full = Ring([Slot(sba(f"full{i}", [P, KC, S])) for i in range(1)])
    hi = Ring([Slot(sba(f"hi{i}", [P, KC, S], F32R)) for i in range(1)])
    lo = Ring([Slot(sba(f"lo{i}", [P, KC, S], F32R)) for i in range(1)])
    rowmax = Ring([Slot(sba(f"rowmax{i}", [P, H, TT])) for i in range(2)])
    shift = Slot(sba("shift", [P, 3, H * TT]))
    shiftT = Slot(sba("shiftT", [3 * H * TT, P]))
    clipped = Ring([Slot(sba(f"clipped{i}", [P, 2, S])) for i in range(2)])
    LB_HEADS = 2
    lower = Ring([Slot(sba(f"lower{i}", [P, LB_HEADS, S])) for i in range(2)])
    probs = Ring([Slot(sba(f"probs{i}", [P, 2, S])) for i in range(3)])
    weighted = Slot(sba("weighted", [P, 2, S]))
    recip = Slot(sba("recip", [P, TT, 8]))
    attn = Slot(sba("attn", [P, TT, D]))
    attnT = Slot(sba("attnT", [P, KC, S]))
    summed = Ring([Slot(sba(f"summed{i}", [P, TT, D])) for i in range(1)])
    nan_sum = sba("nan_sum", [P, 2 * NB])
    vmean_row = Slot(sba("vmean_row", [1, D]))
    inv_s = sba("inv_s", [P, 32])

    half_ready = const(partial(nc.gpsimd.memset, minus_half[:, :], -0.5))
    inv_ready = const(partial(nc.gpsimd.memset, inv_s[:, :], 1.0 / S))
    stacks_ready = []
    for l in range(2):
        for t in (stack_q[l].t, stack_k[l].t):
            DV.put(partial(nc.vector.memset, t[STACK:FULL, :, :].bitcast(F32), 0.0))
        stacks_ready.append(DV.mark(partial(nc.vector.memset, stack_k[l].t[FULL:ROWS, :, :].bitcast(F32), 1.0)))
    values_ready = [DV.mark(partial(nc.vector.memset, values[l].t[:, :, :, HD:2 * HD], 1.0)) for l in range(2)]

    hidden0 = Slot(sba("hidden0", [P, E0 + 1, S]))
    cw_sel_f = hidden0.t[0:2 * E0, 0:E0 * P // S, :].rearrange("p a (b n) -> p (a b) n", n=P)
    cw_sel = sba("cw_sel", [2 * E0, E0, P], F32R)
    const(partial(nc.gpsimd.memset, cw_sel_f, 0.0))
    for half in range(2):
        m = const(partial(nc.gpsimd.affine_select, 
            out=cw_sel_f, in_=cw_sel_f, compare_op=ALU.not_equal, fill=1.0,
            base=-half * E0, pattern=[[-1, E0], [0, P]], channel_multiplier=1))
    DV.wait(m)
    cw_sel_ready = DV.mark(partial(nc.vector.tensor_copy, cw_sel[:, :, :], cw_sel_f))
    const(partial(nc.gpsimd.memset, before[:, :, :], 1.0))
    const(partial(nc.gpsimd.affine_select, out=before[:, :, :], in_=before[:, :, :], compare_op=ALU.is_gt, fill=0.0,
                                    base=0, pattern=[[1, 8], [-1, 8]], channel_multiplier=0))
    const(partial(nc.gpsimd.memset, after[:, :, :], 1.0))
    order_ready = const(partial(nc.gpsimd.affine_select, out=after[:, :, :], in_=after[:, :, :], compare_op=ALU.is_gt,
                                                  fill=0.0, base=0, pattern=[[-1, 8], [1, 8]],
                                                  channel_multiplier=0))

    def dv(fn, *waits):
        DV.wait(*waits)
        return DV.mark(fn)

    def layer_norm(b, slot_n, slot_t):
        stats, moments, rstd = stats_ring.take(), moments_ring.take(), rstd_ring.take()
        DV.wait(*stats.free, *moments.free)
        for t in range(TT):
            m = dv(partial(nc.vector.bn_stats, stats.t[:, t, :], x[:, TT * b + t, :]), x_free[TT * b + t])
        stats.free = []
        for t in range(TT):
            m_mom = dv(partial(nc.vector.bn_aggr, moments.t[:, t, :], stats.t[:, t, :]), m)
        r = rstd.t
        PO.wait(m_mom, *rstd.free, half_ready)
        m = PO.mark(partial(nc.gpsimd.tensor_scalar, r[:, 0, :], moments.t[:, :, 1], EPS, None, ALU.add))
        for fn in (
            partial(nc.gpsimd.tensor_tensor, r[:, 1, :], r[:, 0, :], minus_half[:, :], ALU.pow),
            partial(nc.gpsimd.tensor_tensor, r[:, 2, :], r[:, 1, :], r[:, 1, :], ALU.mult),
            partial(nc.gpsimd.tensor_tensor, r[:, 2, :], r[:, 2, :], r[:, 0, :], ALU.mult),
            partial(nc.gpsimd.tensor_scalar, r[:, 2, :], r[:, 2, :], -0.5, 1.5, ALU.mult, ALU.add),
            partial(nc.gpsimd.tensor_tensor, r[:, 3, :], r[:, 1, :], r[:, 2, :], ALU.mult),
        ):
            PO.wait(m)
            m = PO.mark(fn)
        yield
        DV.wait(m, *slot_n.free)
        for t in range(TT):
            m_n = DV.mark(partial(nc.vector.tensor_scalar, 
                slot_n.t[:, t, :], x[:, TT * b + t, :], moments.t[:, t, 0:1], r[:, 3, t:t + 1],
                ALU.subtract, ALU.mult))
        stats.free, moments.free, rstd.free = [m_mom], [m_n], [m_n]
        slot_n.ready = m_n
        yield
        bank = work_banks.take()
        PE.wait(m_n, ident_ready, *bank.free)
        for k in range(KC):
            for t in range(TT):
                o = k * S + t * P
                tr = partial(nc.tensor.transpose, 
                    bank.t[:, o:o + P], slot_n.t[:, t, k * P:k * P + P], ident[:, :])
                m = PE.mark(tr) if (k, t) == (KC - 1, TT - 1) else PE.put(tr)
        slot_n.free = [m]
        AC.wait(m, *slot_t.free)
        slot_t.ready = AC.mark(partial(nc.scalar.activation, 
            slot_t.t[:, :, :].rearrange("p k s -> p (k s)"), bank.t[:, :], ACT.Copy))
        bank.free = [slot_t.ready]
        yield

    hilo_out = [[dma_sem(f"hilo_out{l}{w}") for w in range(2)] for l in range(2)]
    stack_in = [[dma_sem(f"stack_in{l}{w}") for w in range(2)] for l in range(2)]
    ctxT_out = [dma_sem(f"ctxT_out{i}") for i in range(NB)]
    ctxT_in = [dma_sem(f"ctxT_in{i}") for i in range(2)]
    shift_out = [dma_sem(f"shift_out{l}") for l in range(2)]
    shift_in = [dma_sem(f"shift_in{l}") for l in range(2)]
    lower_in = [dma_sem(f"lower_in{i}") for i in range(2)]
    z_out = [dma_sem(f"z_out{i}") for i in range(2)]
    vmean_out = dma_sem("vmean_out")
    ctxT_stored = [None] * NB
    z_stored = [None] * NB
    vmean_stored = [None] * NB
    nan_marks = []
    shifts_ready = {}
    lower_written = {}

    def project(b, l):
        cT = ctxT.take()
        if l == 0:
            slot = first_ctx if b == 0 else load_ctx(b)
            if b + 1 < NB:
                load_x(b + 1)
            bank = work_banks.take()
            PE.wait(slot.ready, ident_ready, *bank.free)
            for t in range(TT):
                PE.put(partial(nc.tensor.transpose, bank.t[:, t * P:t * P + P], slot.t[:, t, 0:P], ident[:, :]))
            for t in range(TT):
                tr = partial(nc.tensor.transpose, bank.t[0:CTX - P, S + t * P:S + t * P + P],
                                                slot.t[:, t, P:CTX], ident[:, :])
                m = PE.mark(tr) if t == TT - 1 else PE.put(tr)
            slot.free = [m]
            AC.wait(m, *cT.free)
            AC.mark(partial(nc.scalar.activation, cT.t[:, 0, :], bank.t[:, 0:S], ACT.Copy))
            cT.ready = AC.mark(partial(nc.scalar.activation, cT.t[0:CTX - P, 1, :], bank.t[0:CTX - P, S:2 * S], ACT.Copy))
            bank.free = [cT.ready]
            SP.wait(cT.ready)
            SP.load(ctxT_out[b], partial(nc.sync.dma_start, ctxT_dram[b, 0], cT.t[:, 0, :]))
            ctxT_stored[b] = SP.load(ctxT_out[b], partial(nc.sync.dma_start, 
                ctxT_dram[b, 1, 0:CTX - P], cT.t[0:CTX - P, 1, :]))
            extra_free = [ctxT_stored[b]]
        else:
            SP.wait(ctxT_stored[b], *cT.free)
            SP.load(ctxT_in[b % 2], partial(nc.sync.dma_start, cT.t[:, 0, :], ctxT_dram[b, 0]))
            cT.ready = SP.load(ctxT_in[b % 2], partial(nc.sync.dma_start, 
                cT.t[0:CTX - P, 1, :], ctxT_dram[b, 1, 0:CTX - P]))
            extra_free = []
        yield
        chunks = ((0, P), (1, CTX - P))

        def hi_lo(which, source, weights, rows):
            bank = work_banks.take()
            PE.wait(source.ready, attn_w[l], *bank.free)
            for mt in range(KC):
                for n, (k, r) in enumerate(rows):
                    mm = partial(nc.tensor.matmul, 
                        bank.t[:, mt * S:mt * S + S], weights[0:r, k, mt * P:mt * P + P], source.t[0:r, k, :],
                        start=n == 0, stop=n == len(rows) - 1)
                    m = PE.mark(mm) if mt == KC - 1 and n == len(rows) - 1 else PE.put(mm)
            f, hs, ls = full.take(), hi.take(), lo.take()
            flat = lambda t: t[:, :, :].rearrange("p k s -> p (k s)")
            DV.wait(m, *f.free)
            for mt in range(KC):
                bias = qkb[l][:, which, mt:mt + 1]
                m_f = DV.mark(partial(nc.vector.tensor_scalar, 
                    f.t[:, mt, :], bank.t[:, mt * S:mt * S + S], bias, QSCALE if which == 0 else 1.0,
                    ALU.add, ALU.mult))
            bank.free = [m_f]
            AC.wait(m_f, *hs.free)
            m_h = AC.mark(partial(nc.scalar.activation, flat(hs.t), flat(f.t), ACT.Copy))
            m_l = dv(partial(nc.vector.tensor_tensor, flat(ls.t), flat(f.t), flat(hs.t).bitcast(F32), ALU.subtract),
                     m_h, *ls.free)
            f.free = [m_h, m_l]
            SP.wait(m_h, m_l)
            dram = qk_dram[l][b]
            SP.load(hilo_out[l][which], partial(nc.sync.dma_start, 
                dram[2 * which].rearrange("(k p) s -> p k s", p=P), hs.t[:, :, :].bitcast(F32)))
            m_out = SP.load(hilo_out[l][which], partial(nc.sync.dma_start, 
                dram[2 * which + 1].rearrange("(k p) s -> p k s", p=P), ls.t[:, :, :].bitcast(F32)))
            hs.free, ls.free = [m_out, m_l], [m_out]
            if l == 1:
                AC.wait(m_l)
                m_nan = AC.mark(partial(nc.scalar.activation, 
                    flat(f.t), flat(ls.t).bitcast(F32), ACT.Copy,
                    accum_out=nan_sum[:, 2 * b + which:2 * b + which + 1]))
                nan_marks.append(m_nan)
                f.free = [m_nan]
                ls.free.append(m_nan)
            dst = (stack_q if which == 0 else stack_k)[l]
            SP.wait(m_out, stacks_ready[l], *dst.free)
            for blk in range(4):
                part = (blk // 2) if which == 0 else (blk % 2)
                src = dram[2 * which + part].rearrange("(h d) s -> d h s", d=HD)
                dst.ready = SP.load(stack_in[l][which], partial(nc.sync.dma_start, 
                    dst.t[blk * HD:blk * HD + HD, :, :].bitcast(F32), src))

        hi_lo(1, cT, wkv[l], chunks)
        yield
        xT = xnT.take()
        yield from layer_norm(b, xn.take(), xT)
        hi_lo(0, xT, wq[l], ((0, P), (1, P)))
        xT.free = [(PE.sem, PE.count)]
        yield
        bank = work_banks.take()
        PE.wait(cT.ready, attn_w[l], *bank.free)
        for kt in range(2):
            for k, r in chunks:
                mm = partial(nc.tensor.matmul, 
                    bank.t[:, kt * D:kt * D + D], cT.t[0:r, k, kt * P:kt * P + P], wkv[l][0:r, k, D:2 * D],
                    start=k == 0, stop=k == 1)
                m = PE.mark(mm) if (kt, k) == (1, 1) else PE.put(mm)
        cT.free = [m] + extra_free
        v = values[l]
        DV.wait(values_ready[l], m, attn_w[l], *v.free)
        for kt in range(2):
            v.ready = DV.mark(partial(nc.vector.tensor_tensor, 
                v.t[:, kt, :, 0:HD], bank.t[:, kt * D:kt * D + D].rearrange("p (h d) -> p h d", d=HD),
                vb[l][:, :].rearrange("p (h d) -> p h d", d=HD), ALU.add))
        bank.free = [v.ready]
        yield
        if l == 1:
            bank = work_banks.take()
            PE.wait(v.ready, inv_ready, *bank.free)
            for kt in range(2):
                mm = partial(nc.tensor.matmul, bank.t[0:32, 0:D].rearrange("p (h d) -> p h d", d=HD),
                                               inv_s[:, :], v.t[:, kt, :, 0:HD], start=kt == 0, stop=kt == 1)
                m = PE.mark(mm) if kt else PE.put(mm)
            AC.wait(m, *vmean_row.free)
            m = AC.mark(partial(nc.scalar.activation, vmean_row.t[0:1, :], bank.t[0:1, 0:D], ACT.Copy))
            bank.free = [m]
            SP.wait(m)
            vmean_stored[b] = SP.load(vmean_out, partial(nc.sync.dma_start, vmean_dram[b:b + 1, :], vmean_row.t[0:1, :]))
            vmean_row.free = [vmean_stored[b]]
        for _ in range(PAUSE):
            yield
        sq, sk, mx = stack_q[l], stack_k[l], rowmax.take()
        for h in range(H):
            bank = score_banks.take()
            PE.wait(sq.ready, sk.ready, *bank.free)
            for t in range(TT):
                mm = partial(nc.tensor.matmul, bank.t[:, t * S:t * S + S], sq.t[0:FULL, h, t * P:t * P + P],
                                                  sk.t[0:FULL, h, :], start=True, stop=True)
                m = PE.mark(mm) if t == TT - 1 else PE.put(mm)
            DV.wait(m, *mx.free)
            m_max = DV.mark(partial(nc.vector.tensor_reduce, 
                mx.t[:, h, :], bank.t[:, :].rearrange("p (t s) -> p t s", t=TT), AX, ALU.max))
            bank.free = [m_max]
            yield
        flat = mx.t[:, :, :].rearrange("p h t -> p (h t)")
        if l == 1:
            m_max = dv(partial(nc.vector.tensor_scalar, flat, flat, CLAMP, -CLAMP, ALU.min, ALU.max), m_max)
        DV.wait(m_max, *shift.free)
        m_h = DV.mark(partial(nc.vector.tensor_scalar, shift.t[:, 0, :].bitcast(F32R), flat, -1.0, None, ALU.mult))
        m_b = DV.mark(partial(nc.vector.tensor_scalar, shift.t[:, 2, :], flat, -1.0, -CLAMP, ALU.mult, ALU.add))
        m_l = dv(partial(nc.vector.scalar_tensor_tensor, shift.t[:, 1, :].bitcast(F32R), flat, -1.0, shift.t[:, 0, :],
                                                  ALU.mult, ALU.subtract), m_h)
        mx.free = [m_l]
        bank = work_banks.take()
        PE.wait(m_l, *bank.free)
        m = PE.mark(partial(nc.tensor.transpose, bank.t[0:3 * H * TT, 0:P],
                                          shift.t[:, :, :].rearrange("p j r -> p (j r)"), ident[:, :]))
        shift.free = [m]
        AC.wait(m, *shiftT.free)
        m = AC.mark(partial(nc.scalar.activation, shiftT.t[:, :], bank.t[0:3 * H * TT, 0:P], ACT.Copy))
        bank.free = [m]
        SP.wait(m)
        m = SP.load(shift_out[l], partial(nc.sync.dma_start, max_dram[l][b], shiftT.t[:, :]))
        shiftT.free = [m]
        lower_written[b, l] = m
        SP.wait(m)
        shifts_ready[b, l] = SP.load(shift_in[l], partial(nc.sync.dma_start, 
            sq.t[FULL:ROWS, :, :].bitcast(F32).rearrange("j h s -> j (h s)"),
            max_dram[l][b, 0:2 * H * TT].rearrange("(j r) q -> j (r q)", j=2)))
        yield

    def attend(b, l):
        sq, sk, v = stack_q[l], stack_k[l], values[l]
        for _ in range(HOLD[l]):
            yield
        DV.wait(*attn.free)
        for h in range(H):
            if l == 1 and h % LB_HEADS == 0:
                low = lower.take()
                SP.wait(lower_written[b, l], *low.free)
                low.ready = SP.load(lower_in[(h // LB_HEADS) % 2], partial(nc.sync.dma_start, 
                    low.t[:, :, :].rearrange("p h s -> p (h s)"),
                    max_dram[l][b, 2 * H * TT + h * TT:2 * H * TT + (h + LB_HEADS) * TT]
                    .rearrange("r q -> (r q)").partition_broadcast(P)))
            bank = shifted_banks.take()
            PE.wait(shifts_ready[b, l], *bank.free)
            for kt in range(2):
                mm = partial(nc.tensor.matmul, 
                    bank.t[:, kt * S:kt * S + S], sk.t[:, h, kt * P:kt * P + P], sq.t[:, h, :],
                    start=True, stop=True)
                m = PE.mark(mm) if kt else PE.put(mm)
            p = probs.take()
            two = lambda t: t[:, :].rearrange("p (k s) -> p k s", k=2)
            if l == 0:
                AC.wait(m, *p.free)
                p.ready = AC.mark(partial(nc.scalar.activation, p.t[:, :, :], two(bank.t), ACT.Exp))
                bank.free = [p.ready]
            else:
                c = clipped.take()
                DV.wait(m, low.ready, *c.free)
                i = h % LB_HEADS
                m = DV.mark(partial(nc.vector.scalar_tensor_tensor, 
                    c.t[:, :, :], two(bank.t), 0.0, low.t[:, i:i + 1, :].broadcast_to([P, 2, S]),
                    ALU.min, ALU.max))
                bank.free = [m]
                low.free = [m]
                AC.wait(m, *p.free)
                p.ready = AC.mark(partial(nc.scalar.activation, p.t[:, :, :], c.t[:, :, :], ACT.Exp))
                c.free = [p.ready]
            yield
            pending.append((h, p))
            if h:
                value_product(b, l, *pending.pop(0))
            if h == 8:
                value_out(b, l, 0)
        yield
        value_product(b, l, *pending.pop(0))
        yield
        value_out(b, l, 1)
        sq.free, sk.free = [(PE.sem, PE.count)], [(PE.sem, PE.count)]
        v.free = [(PE.sem, PE.count)]
        yield
        bank = work_banks.take()
        PE.wait(attn.ready, *bank.free)
        for k in range(KC):
            for t in range(TT):
                o = k * S + t * P
                tr = partial(nc.tensor.transpose, bank.t[:, o:o + P], attn.t[:, t, k * P:k * P + P],
                                                          ident[:, :])
                m = PE.mark(tr) if (k, t) == (KC - 1, TT - 1) else PE.put(tr)
        attn.free = [m]
        AC.wait(m, *attnT.free)
        attnT.ready = AC.mark(partial(nc.scalar.activation, attnT.t[:, :, :].rearrange("p k s -> p (k s)"), bank.t[:, :],
                                                     ACT.Copy))
        bank.free = [attnT.ready]
        yield
        bank = work_banks.take()
        PE.wait(attnT.ready, *bank.free)
        for t in range(TT):
            for k in range(KC):
                mm = partial(nc.tensor.matmul, 
                    bank.t[:, t * D:t * D + D], attnT.t[:, k, t * P:t * P + P], wo[l][:, k, :],
                    start=k == 0, stop=k == KC - 1)
                m = PE.mark(mm) if (t, k) == (TT - 1, KC - 1) else PE.put(mm)
        attnT.free = [m]
        s = summed.take()
        DV.wait(m, *s.free)
        m = DV.mark(partial(nc.vector.tensor_tensor, 
            s.t[:, :, :], bank.t[:, :].rearrange("p (t d) -> p t d", t=TT),
            ob[l][:, :].unsqueeze(1).broadcast_to([P, TT, D]), ALU.add))
        bank.free = [m]
        xs = x[:, TT * b:TT * b + TT, :]
        if l == 0:
            m = dv(partial(nc.vector.scalar_tensor_tensor, xs, s.t[:, :, :], tg[:, 0:1], xs, ALU.mult, ALU.add),
                   m, tg_ready)
            for t in range(TT):
                x_free[TT * b + t] = m
            s.free = [m]
        else:
            m = dv(partial(nc.vector.tensor_scalar, s.t[:, :, :], s.t[:, :, :], tg[:, 1:2], None, ALU.mult), m, tg_ready)
            SP.wait(m)
            z_stored[b] = SP.load(z_out[b % 2], partial(nc.sync.dma_start, 
                z_dram[b].rearrange("(t p) d -> p t d", p=P), s.t[:, :, :]))
            s.free = [z_stored[b]]
        yield

    pending = []

    def value_product(b, l, h, p):
        c, half = h % 4, (h // 4) % 2
        PE.wait(p.ready, *(value_bank.free if h % 8 == 0 else ()))
        for kt in range(2):
            mm = partial(nc.tensor.matmul, 
                value_bank.t[32 * c:32 * c + 32, half * S:half * S + S], values[l].t[:, kt, h, :], p.t[:, kt, :],
                start=kt == 0, stop=kt == 1)
            m = PE.mark(mm) if kt else PE.put(mm)
        p.free = [m]
        value_bank.ready = m

    def value_out(b, l, pair):
        AC.wait(value_bank.ready, *weighted.free)
        m = AC.mark(partial(nc.scalar.activation, weighted.t[:, :, :].rearrange("p g s -> p (g s)"), value_bank.t[:, :],
                                           ACT.Copy))
        value_bank.free = [m]
        bank = work_banks.take()
        PE.wait(m, *bank.free)
        for t in range(TT):
            for g in range(2):
                o = (t * 2 + g) * P
                tr = partial(nc.tensor.transpose, bank.t[:, o:o + P], weighted.t[:, g, t * P:t * P + P],
                                                          ident[:, :])
                m = PE.mark(tr) if (t, g) == (TT - 1, 1) else PE.put(tr)
        weighted.free = [m]
        view = bank.t[:, :].rearrange("p (t h e) -> p t h e", t=TT, e=2 * HD)
        DV.wait(m, *recip.free)
        m = DV.mark(partial(nc.vector.reciprocal, recip.t[:, :, :], view[:, :, :, HD]))
        m = dv(partial(nc.vector.tensor_tensor, 
            attn.t[:, :, pair * P:pair * P + P].rearrange("p t (h d) -> p t h d", d=HD), view[:, :, :, 0:HD],
            recip.t[:, :, :].unsqueeze(3).broadcast_to([P, TT, 8, HD]), ALU.mult), m)
        recip.free = [m]
        bank.free = [m]
        attn.ready = m

    act_gate = Ring([Slot(sba(f"act_gate{i}", [P, S])) for i in range(2)])
    act_t = Ring([Slot(sba(f"act_t{i}", [P, S])) for i in range(2)])
    cwT = Slot(sba("cwT", [2 * E0, S], F32R))
    rt = sba("rt", [P, 12, TT, 8])
    pair0 = sba("pair0", [P, 2, TT, 8, 8])
    cw_hl = Slot(sba("cw_hl", [P, TT, 2 * E0]))

    def rank_of(values_ap, ranks, n, tiles, pa, pb, m):
        j = values_ap.unsqueeze(2).broadcast_to([P, tiles, n, n])
        i = values_ap.unsqueeze(3).broadcast_to([P, tiles, n, n])
        bef = before[:, 0:n, 0:n].unsqueeze(1).broadcast_to([P, tiles, n, n])
        aft = after[:, 0:n, 0:n].unsqueeze(1).broadcast_to([P, tiles, n, n])
        DV.wait(m, order_ready)
        m1 = DV.mark(partial(nc.vector.tensor_tensor, pa, j, i, ALU.is_ge))
        m2 = DV.mark(partial(nc.vector.tensor_tensor, pb, j, i, ALU.is_gt))
        m1 = dv(partial(nc.vector.tensor_tensor, pa, pa, bef, ALU.mult), m1)
        m2 = dv(partial(nc.vector.tensor_tensor, pb, pb, aft, ALU.mult), m2)
        m1 = dv(partial(nc.vector.tensor_tensor, pa, pa, pb, ALU.add), m1, m2)
        return dv(partial(nc.vector.tensor_reduce, ranks, pa, AX, ALU.add), m1)

    gate_done = []

    def transpose_gate():
        bank = work_banks.take()
        PE.wait(ffn0_w, ident_ready, *bank.free)
        for k in range(KC):
            tr = partial(nc.tensor.transpose, bank.t[:, k * E0:k * E0 + E0], gate_rows[:, k * P:k * P + P],
                                            ident[0:E0, 0:E0])
            m = PE.mark(tr) if k else PE.put(tr)
        AC.wait(m)
        m = AC.mark(partial(nc.scalar.activation, gate_wT[:, :, :].rearrange("p k e -> p (k e)"),
                                           bank.t[:, 0:KC * E0], ACT.Copy))
        bank.free = [m]
        gate_done.append(m)

    def experts0(b):
        xT = xnT.take()
        yield from layer_norm(b, xn.take(), xT)
        if not gate_done:
            transpose_gate()
        bank = work_banks.take()
        PE.wait(xT.ready, gate_done[0], *bank.free)
        for t in range(TT):
            for k in range(KC):
                mm = partial(nc.tensor.matmul, 
                    bank.t[:, t * E0:t * E0 + E0], xT.t[:, k, t * P:t * P + P], gate_wT[:, k, :],
                    start=k == 0, stop=k == KC - 1)
                m = PE.mark(mm) if (t, k) == (TT - 1, KC - 1) else PE.put(mm)
        row = lambda i: rt[:, i, :, :]
        AC.wait(m, *rt_free)
        m = AC.mark(partial(nc.scalar.activation, row(0), bank.t[:, 0:TT * E0].rearrange("p (t e) -> p t e", t=TT),
                                           ACT.Exp, scale=-1.0))
        bank.free = [m]
        yield
        m = dv(partial(nc.vector.tensor_scalar, row(1), row(0), 1.0, None, ALU.add), m)
        m_s = dv(partial(nc.vector.reciprocal, row(2), row(1)), m)
        m = dv(partial(nc.vector.tensor_tensor, row(3), row(2), corr[:, :].unsqueeze(1).broadcast_to([P, TT, E0]),
                                         ALU.add), m_s, ffn0_w)
        grp = row(3).rearrange("p t (g i) -> p t g i", i=E0 // NG)
        m = dv(partial(nc.vector.tensor_tensor, row(4)[:, :, 0:NG], grp[:, :, :, 0], grp[:, :, :, 1], ALU.add), m)
        m = rank_of(row(4)[:, :, 0:NG], row(5)[:, :, 0:NG], NG, TT, pair0[:, 0, :, 0:NG, 0:NG],
                    pair0[:, 1, :, 0:NG, 0:NG], m)
        m = dv(partial(nc.vector.tensor_scalar, row(6)[:, :, 0:NG], row(5)[:, :, 0:NG], TKG - 0.5, None, ALU.is_lt), m)
        m = dv(partial(nc.vector.tensor_tensor, row(7).rearrange("p t (g i) -> p t g i", i=E0 // NG), grp,
                                         row(6)[:, :, 0:NG].unsqueeze(3).broadcast_to([P, TT, NG, E0 // NG]),
                                         ALU.mult), m)
        yield
        m = rank_of(row(7), row(8), E0, TT, pair0[:, 0], pair0[:, 1], m)
        m = dv(partial(nc.vector.scalar_tensor_tensor, row(9), row(8), TOPK0 - 0.5, row(2), ALU.is_lt, ALU.mult), m)
        m = dv(partial(nc.vector.tensor_reduce, row(10)[:, :, 0], row(9), AX, ALU.add), m)
        m = dv(partial(nc.vector.tensor_scalar, row(10)[:, :, 1], row(10)[:, :, 0], 1e-20, None, ALU.add), m)
        m = dv(partial(nc.vector.reciprocal, row(10)[:, :, 2], row(10)[:, :, 1]), m)
        m = dv(partial(nc.vector.scalar_tensor_tensor, row(11), row(9), 2.5 * 0.5,
                                                row(10)[:, :, 2:3].broadcast_to([P, TT, E0]), ALU.mult, ALU.mult),
               m)
        m = dv(partial(nc.vector.tensor_copy, cw_hl.t[:, :, 0:E0].bitcast(F32R), row(11)), m, *cw_hl.free)
        m = dv(partial(nc.vector.tensor_tensor, cw_hl.t[:, :, E0:2 * E0].bitcast(F32R), row(11), cw_hl.t[:, :, 0:E0],
                                         ALU.subtract), m)
        rt_free[:] = [m]
        yield
        bank = work_banks.take()
        PE.wait(m, *bank.free)
        for t in range(TT):
            tr = partial(nc.tensor.transpose, bank.t[0:2 * E0, t * P:t * P + P], cw_hl.t[:, t, :],
                                                       ident[:, :])
            m = PE.mark(tr) if t == TT - 1 else PE.put(tr)
        cw_hl.free = [m]
        AC.wait(m, *cwT.free)
        cwT.ready = AC.mark(partial(nc.scalar.activation, cwT.t[:, :], bank.t[0:2 * E0, 0:S], ACT.Copy))
        bank.free = [cwT.ready]
        yield
        DV.wait(*hidden0.free)
        for e_ in [E0] + list(range(E0)):
            gu = work_banks.take()
            PE.wait(*gu.free)
            for half, w in enumerate((w_gate0, w_up0)):
                for k in range(KC):
                    mm = partial(nc.tensor.matmul, 
                        gu.t[:, half * S:half * S + S], w[:, k, e_, :], xT.t[:, k, :], start=k == 0,
                        stop=k == KC - 1)
                    m_gu = PE.mark(mm) if (half, k) == (1, KC - 1) else PE.put(mm)
            if e_ == E0:
                scale = None
            else:
                scale = work_banks.take()
                PE.wait(cwT.ready, cw_sel_ready, *scale.free)
                m_w = PE.mark(partial(nc.tensor.matmul, scale.t[:, 0:S], cw_sel[:, e_, :], cwT.t[:, :],
                                                                     start=True, stop=True))
            th, tmp = act_gate.take(), act_t.take()
            AC.wait(m_gu, *th.free)
            m = AC.mark(partial(nc.scalar.activation, th.t[:, :], gu.t[:, 0:S], ACT.Tanh, scale=0.5))
            m = dv(partial(nc.vector.scalar_tensor_tensor, 
                tmp.t[:, :], th.t[:, :], 1.0, gu.t[:, 0:S], ALU.add, ALU.mult), m, *tmp.free)
            th.free = [m]
            if scale is not None:
                m = dv(partial(nc.vector.tensor_tensor, tmp.t[:, :], tmp.t[:, :], scale.t[:, 0:S],
                                                                       ALU.mult), m, m_w)
                scale.free = [m]
            half_ = 0.5 if scale is None else 1.0
            m_h = dv(partial(nc.vector.scalar_tensor_tensor, 
                hidden0.t[:, e_, :], tmp.t[:, :], half_, gu.t[:, S:2 * S], ALU.mult, ALU.mult), m)
            tmp.free, gu.free = [m_h], [m_h]
            yield
        xT.free = [(PE.sem, PE.count)]
        cwT.free = [(PE.sem, PE.count)]
        y = work_banks.take()
        y.held = True
        PE.wait(m_h, *y.free)
        for t in range(TT):
            for n, e_ in enumerate([E0] + list(range(E0))):
                mm = partial(nc.tensor.matmul, 
                    y.t[:, t * D:t * D + D], hidden0.t[:, e_, t * P:t * P + P], w_down0[:, e_, :], start=n == 0,
                    stop=n == E0)
                m = PE.mark(mm) if (t, n) == (TT - 1, E0) else PE.put(mm)
            yield
        hidden0.free = [m]
        xs = x[:, TT * b:TT * b + TT, :]
        m = dv(partial(nc.vector.scalar_tensor_tensor, xs, y.t[:, :].rearrange("p (t d) -> p t d", t=TT), tg[:, 2:3], xs,
                                                ALU.mult, ALU.add), m, tg_ready)
        y.free, y.held = [m], False
        for t in range(TT):
            x_free[TT * b + t] = m
        yield

    rt_free = []

    PAUSE = 5
    HOLD = (3, 0)
    SP.wait(zero_ready)
    xs_zero = dma_sem("xs_zero")

    def fill_slots():
        return SP.load(xs_zero, partial(nc.sync.dma_start, 
            xs_dram.rearrange("(p n) d -> p n d", p=P), zero_row[:, :].unsqueeze(1).broadcast_to([P, BLOCKS, D])))

    zero_filled = None
    for r in range(NB + 2):
        first = []
        if r < NB:
            first.append((project(r, 0), 28))
        if 0 <= r - 2:
            first.append((attend(r - 2, 1), 21))
        if 0 <= r - 1 < NB:
            if r == 1:
                load_attention_weights(1)
                zero_filled = fill_slots()
            first.append((experts0(r - 1), 18))
        if r == 0:
            load_experts0()
        weave(*first)
        second = []
        if r < NB:
            second.append((attend(r, 0), 24))
        if 0 <= r - 1 < NB:
            second.append((project(r - 1, 1), 28))
        weave(*second)

    flag = sba("flag", [P, 4])
    vm = sba("vm", [NB, D])
    vmT = sba("vmT", [P, KC, NB])
    zalt = sba("zalt", [NB, D])
    alt_in, zalt_out = dma_sem("alt_in"), dma_sem("zalt_out")
    m = dv(partial(nc.vector.tensor_reduce, flag[:, 0:1], nan_sum[:, :], AX, ALU.add), nan_marks[-1])
    m = dv(partial(nc.vector.tensor_tensor, flag[:, 1:2], flag[:, 0:1], flag[:, 0:1], ALU.is_equal), m)
    bank = work_banks.take()
    PE.wait(m, *bank.free)
    m = PE.mark(partial(nc.tensor.matmul, bank.t[:, 0:1], ones[:, :], flag[:, 1:2], start=True, stop=True))
    m = dv(partial(nc.vector.tensor_scalar, flag[:, 2:3], bank.t[:, 0:1], P - 0.5, None, ALU.is_lt), m)
    bank.free = [m]
    m_keep = dv(partial(nc.vector.tensor_scalar, keep_row[:, :], zero_row[:, :], flag[:, 2:3], None, ALU.add), m, zero_ready)
    SP.wait(*vmean_stored)
    m = SP.load(alt_in, partial(nc.sync.dma_start, vm[:, :], vmean_dram[:, :]))
    bank = work_banks.take()
    PE.wait(m, *bank.free)
    for k in range(KC):
        tr = partial(nc.tensor.transpose, bank.t[:, k * NB:k * NB + NB], vm[:, k * P:k * P + P],
                                                   ident[0:NB, 0:NB])
        m = PE.mark(tr) if k else PE.put(tr)
    AC.wait(m)
    m = AC.mark(partial(nc.scalar.activation, vmT[:, :, :].rearrange("p k b -> p (k b)"), bank.t[:, 0:KC * NB], ACT.Copy))
    bank.free = [m]
    bank2 = work_banks.take()
    PE.wait(m, *bank2.free)
    for k in range(KC):
        mm = partial(nc.tensor.matmul, bank2.t[0:NB, 0:D], vmT[:, k, :], wo[1][:, k, :], start=k == 0, stop=k == 1)
        m = PE.mark(mm) if k else PE.put(mm)
    m = dv(partial(nc.vector.tensor_tensor, zalt[:, :], bank2.t[0:NB, 0:D], ob[1][0:NB, :], ALU.add), m)
    bank2.free = [m]
    m = dv(partial(nc.vector.tensor_scalar, zalt[:, :], zalt[:, :], tg[0:NB, 1:2], None, ALU.mult), m)
    SP.wait(m)
    m_alt = SP.load(zalt_out, partial(nc.sync.dma_start, zalt_dram[:, :], zalt[:, :]))
    before_experts1 = [m_alt]

    C = es
    tail = [(q.sem, q.count) for q in (PE, DV, AC, PO)] + [m for m in z_stored if m] + [m_alt]
    tens.close()

    for q in (PE, DV, AC, PO, SP):
        q.wait(*tail)

    xn1 = sb("xn_all", [P, NT, D])
    z_in = Ring([Slot(sb(f"z_in{i}", [P, TT, D])) for i in range(2)])
    alt_row = Ring([Slot(sb(f"alt_row{i}", [P, D])) for i in range(2)])
    z_sem = [dma_sem(f"z_sem{i}") for i in range(2)]
    x1T = Ring([Slot(sb(f"x1T{i}", [P, KC, S])) for i in range(2)])
    wr = sb("wr", [P, KC, E1])
    br = sb("br", [P, E1])
    b1_rows = sb("b1_rows", [E1 * JH, P])
    b1T = sb("b1T", [P, E1, JH])
    b2 = sb("b2", [E1, D])
    lg = sb("lg", [P, NT, E1])
    W1S = 3
    w1 = Ring([Slot(sb(f"w1_{i}", [P, KC, H1])) for i in range(W1S)])
    w2 = Ring([Slot(sb(f"w2_{i}", [P, JH, D])) for i in range(W1S)])
    router_in = dma_sem("router_in")
    for dst, src in ((wr[:, :, :], a["L1_ffn_Wr"].rearrange("(k p) e -> p k e", p=P)),
                     (br[:, :], a["L1_ffn_br"].partition_broadcast(P)),
                     (b1_rows[:, :], a["L1_ffn_b1"].rearrange("e (j p) -> (e j) p", p=P)),
                     (b2[:, :], a["L1_ffn_b2"])):
        router_w = SP.load(router_in, partial(nc.sync.dma_start, dst, src))

    def finish_attention(b):
        z, alt = z_in.take(), alt_row.take()
        SP.wait(z_stored[b], m_alt, *z.free, *alt.free)
        SP.load(z_sem[b % 2], partial(nc.sync.dma_start, z.t[:, :, :], z_dram[b].rearrange("(t p) d -> p t d", p=P)))
        m = SP.load(z_sem[b % 2], partial(nc.sync.dma_start, alt.t[:, :], zalt_dram[b].partition_broadcast(P)))
        yield
        DV.wait(m)
        for t in range(TT):
            m = DV.mark(partial(nc.vector.copy_predicated, z.t[:, t, :], keep_row[:, :], alt.t[:, :]))
        alt.free = [m]
        xs = x[:, TT * b:TT * b + TT, :]
        m = dv(partial(nc.vector.tensor_tensor, xs, xs, z.t[:, :, :], ALU.add), m)
        z.free = [m]
        for t in range(TT):
            x_free[TT * b + t] = m
        yield
        n = Slot(xn1[:, TT * b:TT * b + TT, :])
        xT = x1T.take()
        yield from layer_norm(b, n, xT)
        xn_ready.append(n.ready)
        bank = work_banks.take()
        PE.wait(xT.ready, router_w, *bank.free)
        for t in range(TT):
            for k in range(KC):
                mm = partial(nc.tensor.matmul, 
                    bank.t[:, t * E1:t * E1 + E1], xT.t[:, k, t * P:t * P + P], wr[:, k, :],
                    start=k == 0, stop=k == KC - 1)
                m = PE.mark(mm) if (t, k) == (TT - 1, KC - 1) else PE.put(mm)
        xT.free = [m]
        m = dv(partial(nc.vector.tensor_tensor, 
            lg[:, TT * b:TT * b + TT, :], bank.t[:, 0:TT * E1].rearrange("p (t e) -> p t e", t=TT),
            br[:, :].unsqueeze(1).broadcast_to([P, TT, E1]), ALU.add), m, router_w)
        bank.free = [m]
        lg_ready.append(m)
        yield

    xn_ready, lg_ready = [], []
    for b in range(0, NB, 2):
        weave((finish_attention(b), 6), (finish_attention(b + 1), 6))

    q1 = sb("q1", [P, 8, NT, E1])
    pair1 = sb("pair1", [P, 2, NT, E1, E1])
    small = sb("small", [P, 8, NT])
    row = lambda i: q1[:, i, :, :]
    tok = lambda i: small[:, i, :]
    wide = lambda ap: ap.unsqueeze(2).broadcast_to([P, NT, E1])
    m_rank = rank_of(lg[:, :, :], row(0), E1, NT, pair1[:, 0], pair1[:, 1], lg_ready[-1])
    m_mask = dv(partial(nc.vector.tensor_scalar, row(1), row(0), TOPK1 - 0.5, None, ALU.is_lt), m_rank)

    tri = sb("tri", [P, P])
    const(partial(nc.gpsimd.memset, tri[:, :], 1.0))
    tri_ready = const(partial(nc.gpsimd.affine_select, out=tri[:, :], in_=tri[:, :], compare_op=ALU.is_gt, fill=0.0,
                                                base=0, pattern=[[1, P]], channel_multiplier=-1))
    bank = work_banks.take()
    PE.wait(m_mask, tri_ready, *bank.free)
    PE.put(partial(nc.tensor.matmul, bank.t[:, 0:NT * E1], tri[:, :], row(1).rearrange("p t e -> p (t e)"),
                              start=True, stop=False, skip_group_check=True))
    for t in range(NT):
        n = NT - 1 - t
        if n:
            PE.put(partial(nc.tensor.matmul, 
                bank.t[:, (t + 1) * E1:NT * E1].rearrange("p (t e) -> p t e", e=E1), ones[:, :],
                row(1)[:, t:t + 1, :].broadcast_to([P, n, E1]), start=False, stop=False, skip_group_check=True))
        mm = partial(nc.tensor.matmul, bank.t[:, NT * E1:NT * E1 + E1], ones[:, :], row(1)[:, t, :], start=False,
                                     stop=t == NT - 1, skip_group_check=True)
        m_count = PE.mark(mm) if t == NT - 1 else PE.put(mm)
    m_max = dv(partial(nc.vector.tensor_reduce, tok(0), lg[:, :, :], AX, ALU.max), m_mask)
    m = dv(partial(nc.vector.tensor_tensor, row(2), lg[:, :, :], row(1), ALU.mult), m_mask)
    m1 = dv(partial(nc.vector.tensor_scalar, row(3), row(1), -NEG_INF, NEG_INF, ALU.mult, ALU.add), m_mask)
    m = dv(partial(nc.vector.tensor_tensor, row(2), row(2), row(3), ALU.add), m, m1)
    m = dv(partial(nc.vector.tensor_tensor, row(2), row(2), wide(tok(0)), ALU.subtract), m, m_max)
    AC.wait(m)
    m = AC.mark(partial(nc.scalar.activation, row(3), row(2), ACT.Exp))
    m = dv(partial(nc.vector.tensor_reduce, tok(1), row(3), AX, ALU.add), m)
    m = dv(partial(nc.vector.reciprocal, tok(2), tok(1)), m)
    m = dv(partial(nc.vector.tensor_scalar, tok(2), tok(2), tg[:, 3:4], None, ALU.mult), m)
    m_w = dv(partial(nc.vector.tensor_tensor, row(4), row(3), wide(tok(2)), ALU.mult), m)
    TB = NB * S // P
    steps = sb("steps", [P, E1, TB])
    steps_ready = const(partial(nc.gpsimd.iota, steps[:, :, :], [[0, E1], [P, TB]], base=0, channel_multiplier=0,
                                         allow_small_or_imprecise_dtypes=True))
    cnt = sb("cnt", [P, 6, E1])
    c = lambda i: cnt[:, i, :]
    m = dv(partial(nc.vector.tensor_copy, c(0), bank.t[:, NT * E1:NT * E1 + E1]), m_count)
    m = dv(partial(nc.vector.tensor_tensor, steps[:, :, :], c(0).unsqueeze(2).broadcast_to([P, E1, TB]), steps[:, :, :],
                                     ALU.is_gt), m, steps_ready)
    m = dv(partial(nc.vector.tensor_reduce, c(1), steps[:, :, :], AX, ALU.add), m)
    cum = sb("cum", [P, E1, E1])
    m = dv(partial(nc.vector.tensor_tensor, cum[:, :, :], before[:, :, :], c(1).unsqueeze(1).broadcast_to([P, E1, E1]),
                                     ALU.mult), m)
    m = dv(partial(nc.vector.tensor_reduce, c(2), cum[:, :, :], AX, ALU.add), m)
    m_end = dv(partial(nc.vector.tensor_tensor, c(3), c(2), c(1), ALU.add), m)
    m = dv(partial(nc.vector.tensor_scalar, c(4), c(2), float(P), None, ALU.mult), m)
    m_slot = dv(partial(nc.vector.tensor_tensor, 
        row(5), bank.t[:, 0:NT * E1].rearrange("p (t e) -> p t e", e=E1),
        c(4).unsqueeze(1).broadcast_to([P, NT, E1]), ALU.add), m)
    bank.free = [m_slot]
    slot_i = sb("slot_i", [P, TOPK1, NT], I32)
    slot_ready = []
    for r in range(TOPK1):
        m = dv(partial(nc.vector.tensor_scalar, row(6), row(0), float(r), None, ALU.is_equal), m_rank, m_slot, m_w)
        m1 = dv(partial(nc.vector.tensor_tensor, row(7), row(6), row(5), ALU.mult), m)
        m1 = dv(partial(nc.vector.tensor_reduce, tok(3 + r), row(7), AX, ALU.add), m1)
        slot_ready.append(dv(partial(nc.vector.tensor_copy, slot_i[:, r, :], tok(3 + r)), m1))
        m1 = dv(partial(nc.vector.tensor_tensor, row(7), row(6), row(4), ALU.mult), m, m1)
        w_ready = dv(partial(nc.vector.tensor_reduce, tok(5 + r), row(7), AX, ALU.add), m1)
        m_slot = w_ready
    block_no = sb("block_no", [P, BLOCKS, E1])
    block_e = sb("block_e", [P, BLOCKS])
    block_i = sb("block_i", [P, BLOCKS], I32)
    m_no = const(partial(nc.gpsimd.iota, block_no[:, :, :], [[1, BLOCKS], [0, E1]], base=0, channel_multiplier=0,
                                  allow_small_or_imprecise_dtypes=True))
    m = dv(partial(nc.vector.tensor_tensor, block_no[:, :, :], block_no[:, :, :],
                                     c(3).unsqueeze(1).broadcast_to([P, BLOCKS, E1]), ALU.is_ge), m_end, m_no)
    m = dv(partial(nc.vector.tensor_reduce, block_e[:, :], block_no[:, :, :], AX, ALU.add), m)
    m_be = dv(partial(nc.vector.tensor_scalar, block_e[:, :], block_e[:, :], E1 - 1.0, None, ALU.min), m)
    block_ready = dv(partial(nc.vector.tensor_copy, block_i[:, :], block_e[:, :]), m_be)

    scatter_sem = dma_sem("scatter_sem")
    PO.wait(zero_filled, xn_ready[-1], *slot_ready)
    for r in range(TOPK1):
        for t in range(NT):
            scattered = PO.load(scatter_sem, partial(nc.gpsimd.indirect_dma_start, 
                xs_dram[:, :], bass.IndirectOffsetOnAxis(ap=slot_i[:, r, t:t + 1].bitcast(U32), axis=0),
                xn1[:, t, :], None))

    bank = work_banks.take()
    PE.wait(router_w, *bank.free)
    m = PE.mark(partial(nc.tensor.transpose, bank.t[:, 0:E1 * JH], b1_rows[:, :], ident[0:E1 * JH, 0:E1 * JH]))
    AC.wait(m)
    m_b1 = AC.mark(partial(nc.scalar.activation, b1T[:, :, :].rearrange("p e j -> p (e j)"), bank.t[:, 0:E1 * JH],
                                          ACT.Copy))
    bank.free = [m_b1]
    expert_no = sb("expert_no", [P, E1])
    part_no = sb("part_no", [P, 1])
    const(partial(nc.gpsimd.iota, expert_no[:, :], [[1, E1]], base=0, channel_multiplier=0,
                           allow_small_or_imprecise_dtypes=True))
    no_ready = const(partial(nc.gpsimd.iota, part_no[:, :], [[0, 1]], base=0, channel_multiplier=1,
                                      allow_small_or_imprecise_dtypes=True))
    onehot = sb("onehot", [P, BLOCKS, E1])
    onehotT = sb("onehotT", [P, BLOCKS])
    m = dv(partial(nc.vector.tensor_tensor, onehot[:, :, :], expert_no[:, :].unsqueeze(1).broadcast_to([P, BLOCKS, E1]),
                                     block_e[:, :].unsqueeze(2).broadcast_to([P, BLOCKS, E1]), ALU.is_equal),
           m_be, no_ready)
    onehotT_ready = dv(partial(nc.vector.tensor_scalar, onehotT[:, :], block_e[:, :], part_no[:, 0:1], None,
                                                 ALU.is_equal), m_be, no_ready)
    b1_all = sb("b1_all", [P, BLOCKS, JH])
    b1_tmp = sb("b1_tmp", [P, BLOCKS, JH])
    m = dv(partial(nc.vector.tensor_tensor, 
        b1_all[:, :, :], onehot[:, :, 0:1].broadcast_to([P, BLOCKS, JH]),
        b1T[:, 0:1, :].broadcast_to([P, BLOCKS, JH]), ALU.mult), m, m_b1)
    for ex in range(1, E1):
        m = dv(partial(nc.vector.tensor_tensor, 
            b1_tmp[:, :, :], onehot[:, :, ex:ex + 1].broadcast_to([P, BLOCKS, JH]),
            b1T[:, ex:ex + 1, :].broadcast_to([P, BLOCKS, JH]), ALU.mult), m)
        m = dv(partial(nc.vector.tensor_tensor, b1_all[:, :, :], b1_all[:, :, :], b1_tmp[:, :, :], ALU.add), m)
    b1_ready = m

    W_AHEAD = W1S - 1
    w_sem = [dma_sem(f"w_sem{i}") for i in range(W1S)]
    xs_in = Ring([Slot(sb(f"xs_in{i}", [P, D])) for i in range(3)])
    xs_sem = [dma_sem(f"xs_sem{i}") for i in range(3)]
    xsT = Ring([Slot(sb(f"xsT{i}", [P, KC, P])) for i in range(2)])
    hT = Ring([Slot(sb(f"hT{i}", [P, JH, P])) for i in range(2)])
    ysb = Ring([Slot(sb(f"ysb{i}", [P, D])) for i in range(2)])
    ys_sem = [dma_sem(f"ys_sem{i}") for i in range(2)]
    last = [m for s in (*score_banks.slots, *shifted_banks.slots, value_bank, *work_banks.slots) for m in s.free]
    PE.wait(*last)
    AC.wait(*last)
    DV.wait(*last)
    h_banks = Ring([Slot(banks[i]) for i in range(4)])
    y_banks = Ring([Slot(banks[4]), Slot(banks[5])])
    t_banks = Ring([Slot(banks[6]), Slot(banks[7])])
    weights = {}

    def load_weights(i):
        a1, a2 = w1.take(), w2.take()
        SP.wait(block_ready, *a1.free, *a2.free)

        def start():
            no = nc.sync.value_load(block_i[0:1, i:i + 1], min_val=0, max_val=E1 - 1)
            nc.sync.dma_start(a1.t[:, :, :], a["L1_ffn_W1"][bass.ds(no, 1)].rearrange("e (k p) n -> p (e k) n", p=P))\
                .then_inc(w_sem[i % W1S].sem, 16)
            return nc.sync.dma_start(a2.t[:, :, :],
                               a["L1_ffn_W2"][bass.ds(no, 1)].rearrange("e (j p) n -> p (e j) n", p=P))
        w_sem[i % W1S].total += 16
        weights[i] = (a1, a2, SP.load(w_sem[i % W1S], start))

    xs_slots = {}

    def load_slots(i):
        s = xs_in.take()
        SP.wait(scattered, *s.free)
        s.ready = SP.load(xs_sem[i % 3], partial(nc.sync.dma_start, s.t[:, :], xs_dram[i * P:i * P + P, :]))
        xs_slots[i] = s

    def up(i):
        s, xT, bank = xs_slots.pop(i), xsT.take(), t_banks.take()
        PE.wait(s.ready, *bank.free)
        for k in range(KC):
            tr = partial(nc.tensor.transpose, bank.t[:, k * P:k * P + P], s.t[:, k * P:k * P + P], ident[:, :])
            m = PE.mark(tr) if k else PE.put(tr)
        s.free = [m]
        AC.wait(m, *xT.free)
        m = AC.mark(partial(nc.scalar.activation, xT.t[:, :, :].rearrange("p k s -> p (k s)"), bank.t[:, 0:KC * P],
                                           ACT.Copy))
        bank.free = [m]
        xT.ready = m
        return xT

    def up2(i, xT):
        a1, _, w_ready_ = weights[i]
        hb, h = (h_banks.take(), h_banks.take()), hT.take()
        for half in range(2):
            PE.wait(xT.ready, w_ready_, *hb[half].free)
            for j in range(half * JH // 2, (half + 1) * JH // 2):
                o = (j % (JH // 2)) * P
                for k in range(KC):
                    mm = partial(nc.tensor.matmul, 
                        hb[half].t[:, o:o + P], a1.t[:, k, j * P:j * P + P], xT.t[:, k, :], start=k == 0,
                        stop=k == KC - 1)
                    m = PE.mark(mm) if k == KC - 1 and j % (JH // 2) == JH // 2 - 1 else PE.put(mm)
            q = AC if half == 0 else DV
            q.wait(m, b1_ready, *(h.free if True else ()))
            for j in range(half * JH // 2, (half + 1) * JH // 2):
                o = (j % (JH // 2)) * P
                if q is AC:
                    mh = q.mark(partial(nc.scalar.activation, 
                        h.t[:, j, :], hb[half].t[:, o:o + P], ACT.Relu, bias=b1_all[:, i, j:j + 1]))
                else:
                    mh = q.mark(partial(nc.vector.tensor_scalar, 
                        h.t[:, j, :], hb[half].t[:, o:o + P], b1_all[:, i, j:j + 1], 0.0, ALU.add, ALU.max))
            hb[half].free = [mh]
            h.ready = (h.ready if half else []) + [mh]
        xT.free = [m]
        a1.free = [m]
        return h

    ys_written = []

    def down(i, h):
        _, a2, w_ready_ = weights.pop(i)
        bank, y = y_banks.take(), ysb.take()
        PE.wait(onehotT_ready, router_w, w_ready_, *bank.free)
        PE.put(partial(nc.tensor.matmul, bank.t[:, 0:D], onehotT[0:E1, i:i + 1].broadcast_to([E1, P]), b2[:, :],
                                  start=True, stop=False))
        PE.wait(*h.ready)
        for j in range(JH):
            mm = partial(nc.tensor.matmul, bank.t[:, 0:D], h.t[:, j, :], a2.t[:, j, :], start=False,
                                         stop=j == JH - 1)
            m = PE.mark(mm) if j == JH - 1 else PE.put(mm)
        h.free, a2.free = [m], [m]
        DV.wait(m, *y.free)
        m = DV.mark(partial(nc.vector.tensor_copy, y.t[:, :], bank.t[:, 0:D]))
        bank.free = [m]
        SP.wait(m)
        m = SP.load(ys_sem[i % 2], partial(nc.sync.dma_start, ys_dram[i * P:i * P + P, :], y.t[:, :]))
        y.free = [m]
        ys_written.append(m)

    for i in range(W_AHEAD):
        load_weights(i)
    for i in range(2):
        load_slots(i)
    xTs = {0: up(0)}
    held = None
    for i in range(BLOCKS):
        if i + 2 < BLOCKS:
            load_slots(i + 2)
        if i + 1 < BLOCKS:
            xTs[i + 1] = up(i + 1)
        h = up2(i, xTs.pop(i))
        if held is not None:
            down(*held)
        if i + W_AHEAD < BLOCKS:
            load_weights(i + W_AHEAD)
        held = (i, h)
    down(*held)

    picked = Ring([Slot(sb(f"picked{i}", [P, TOPK1, D])) for i in range(4)])
    pick_sem = [dma_sem(f"pick_sem{i}") for i in range(4)]
    out_sem = dma_sem("out_sem")
    PO.wait(*ys_written[-2:])
    for t in range(NT):
        g = picked.take()
        PO.wait(*g.free)
        for r in range(TOPK1):
            m = PO.load(pick_sem[t % 4], partial(nc.gpsimd.indirect_dma_start, 
                g.t[:, r, :], None, ys_dram[:, :],
                bass.IndirectOffsetOnAxis(ap=slot_i[:, r, t:t + 1].bitcast(U32), axis=0)))
        for r in range(TOPK1):
            m = dv(partial(nc.vector.scalar_tensor_tensor, 
                x[:, t, :], g.t[:, r, :], small[:, 5 + r, t:t + 1], x[:, t, :], ALU.mult, ALU.add), m, w_ready)
        g.free = [m]
        SP.wait(m)
        done = SP.load(out_sem, partial(nc.sync.dma_start, 
            out[t // TT, (t % TT) * P:(t % TT) * P + P, :], x[:, t, :]))
    SP.wait(done)

    block = es.enter_context(nc.Block())

    @block.sync
    def _(_engine):
        SP.play()

    @block.tensor
    def _(_engine):
        PE.play()

    @block.vector
    def _(_engine):
        DV.play()

    @block.scalar
    def _(_engine):
        AC.play()

    @block.gpsimd
    def _(_engine):
        PO.play()

    es.close()


def kernel(**inputs):
    import numpy as np
    import concourse.bacc as bacc
    from concourse.bass_utils import run_bass_kernel_spmd

    nc = bacc.Bacc("TRN2", target_bir_lowering=False, num_devices=1)
    arrays, aps = {}, {}
    for name, value in inputs.items():
        v = np.ascontiguousarray(value)
        arrays[f"in_{name}"] = v
        aps[name] = nc.dram_tensor(f"in_{name}", v.shape, mybir.dt.from_np(v.dtype), kind="ExternalInput").ap()
    out = nc.dram_tensor("out_x", (NB, S, D), F32, kind="ExternalOutput").ap()
    build(nc, aps, out)
    r = run_bass_kernel_spmd(nc, [arrays], core_ids=[0])
    return r.results[0]["out_x"]
```

```python
from contextlib import ExitStack
from functools import partial
from math import prod

import concourse.bass as bass
from concourse import mybir

F32 = mybir.dt.float32
F32R = mybir.dt.float32r
I32 = mybir.dt.int32
U32 = mybir.dt.uint32
ALU = mybir.AluOpType
ACT = mybir.ActivationFunctionType
AX = mybir.AxisListType.X

P = 128
NB, S, D = 8, 256, 256
CTX = 192
H, HD = 16, 16
TT = S // P
NT = NB * TT
KC = D // P
E0, I0 = 8, 128
NG, TKG, TOPK0 = 4, 2, 4
E1, H1, TOPK1 = 8, 1024, 2
JH = H1 // P
BLOCKS = NB * S * TOPK1 // P + E1 - 1
CLAMP = 10000.0
EPS = 1e-5
QSCALE = HD ** -0.5
NEG_INF = -1e9

STACK = 4 * HD
FULL = 96
ROWS = FULL + 2


PE_COLUMN = 0.42
PASSES = 4
PE_STRIP = 32
DVE_NS, DVE_COLUMN = 60, 1.04
ACT_NS, ACT_COLUMN = 50, 0.83
POOL_NS, POOL_COLUMN = 100, 1.3
SP_NS, SP_COLUMN = 60, 0.0
SIGNAL_NS = 150
DMA_START, DMA_END, DMA_BYTE = 1400, 900, 1 / 360


def columns(fn):
    return max((prod(v.shape[1:]) for v in (*fn.args, *fn.keywords.values()) if isinstance(v, bass.AP)), default=0)


class Queue:

    due = {}
    dma_free = 0.0

    def __init__(self, eng, sem, fixed, per_column):
        self.eng, self.sem, self.ops, self.count, self.seen = eng, sem, [], 0, {}
        self.fixed, self.per_column, self.now = fixed, per_column, 0.0

    def wait(self, *marks):
        for mark in marks:
            if mark is None:
                continue
            sem, value = mark
            if self.seen.get(sem.name, 0) < value:
                self.seen[sem.name] = value
                self.ops.append(partial(self.eng.wait_ge, sem, value))
                self.now = max(self.now, when([mark]))

    def put(self, fn):
        self.ops.append(fn)
        self.now += self.cost(fn)

    def cost(self, fn):
        return self.fixed + self.per_column * columns(fn)

    def mark(self, fn):
        self.count += 1
        self.ops.append(lambda: fn().then_inc(self.sem, 1))
        self.now += self.cost(fn)
        self.due[self.sem.name, self.count] = self.now + SIGNAL_NS
        return (self.sem, self.count)

    def load(self, sem, fn):
        sem.total += 16
        self.ops.append(lambda: fn().then_inc(sem.sem, 16))
        self.now += self.fixed
        start = max(self.now + DMA_START, Queue.dma_free)
        ap = fn.args[0] if isinstance(fn, partial) else None
        Queue.dma_free = start + DMA_BYTE * (4 * prod(ap.shape) if ap is not None and isinstance(ap, bass.AP) else 0)
        self.due[sem.sem.name, sem.total] = Queue.dma_free + DMA_END
        return (sem.sem, sem.total)

    def play(self):
        for op in self.ops:
            op()


class TensorQueue(Queue):

    def cost(self, fn):
        out, weights = fn.args[0:2]
        n = prod(out.shape[1:]) * (PASSES if weights.dtype == F32 else 1)
        return self.fixed + self.per_column * n * (out.shape[0] / P if out.shape[0] == PE_STRIP else 1)


def when(marks):
    return max((Queue.due.get((m[0].name, m[1]), 0.0) for m in marks if m), default=0.0)


class DmaSem:
    def __init__(self, sem):
        self.sem, self.total = sem, 0


class Slot:

    def __init__(self, t):
        self.t, self.free, self.held, self.ready = t, [], False, None

    def release(self, *marks):
        self.free, self.held = list(marks), False


BUSY = "busy"


class Ring:

    def __init__(self, *tensors):
        self.slots = [Slot(t) for t in tensors]

    def take(self):
        while all(s.held for s in self.slots):
            yield BUSY
        slot = min((s for s in self.slots if not s.held), key=lambda s: when(s.free))
        slot.held = True
        return slot

    def grab(self):
        slot = min((s for s in self.slots if not s.held), key=lambda s: when(s.free))
        slot.held = True
        return slot


def weave(stages, clock):
    turn = {n: 0.0 for n in range(len(stages))}
    busy = set()
    while turn:
        n = min((n for n in turn if n not in busy), key=lambda n: max(turn[n], clock.now))
        marks = next(stages[n], None)
        if marks == BUSY:
            busy.add(n)
            continue
        if marks is None:
            del turn[n]
        else:
            turn[n] = when(marks)
        busy.clear()


def build(nc, a, out):
    es = ExitStack()
    tens = ExitStack()

    def sem(name):
        return es.enter_context(nc.semaphore(name))

    def sb(name, shape, dt=F32, scope=None):
        return (scope or es).enter_context(nc.sbuf_tensor(name, shape, dt))

    def dma_sem(name):
        return DmaSem(sem(name))

    PE = TensorQueue(nc.tensor, sem("pe_done"), 0, PE_COLUMN)
    DV = Queue(nc.vector, sem("dve_done"), DVE_NS, DVE_COLUMN)
    AC = Queue(nc.scalar, sem("act_done"), ACT_NS, ACT_COLUMN)
    PO = Queue(nc.gpsimd, sem("pool_done"), POOL_NS, POOL_COLUMN)
    SP = Queue(nc.sync, sem("sp_done"), SP_NS, SP_COLUMN)

    qk_dram = [nc.dram_tensor(f"qk_{l}", (NB, 4, D, S), F32).ap() for l in range(2)]
    max_dram = [nc.dram_tensor(f"max_{l}", (NB, 3 * H * TT, P), F32).ap() for l in range(2)]
    ctxT_dram = nc.dram_tensor("ctx_t", (NB, 2, P, S), F32).ap()
    z_dram = nc.dram_tensor("z_rows", (NB, S, D), F32).ap()
    vmean_dram = nc.dram_tensor("vmean", (NB, D), F32).ap()
    zalt_dram = nc.dram_tensor("zalt_rows", (NB, D), F32).ap()
    xs_dram = nc.dram_tensor("xs", (BLOCKS * P, D), F32).ap()
    ys_dram = nc.dram_tensor("ys", (BLOCKS * P, D), F32).ap()

    banks = [es.enter_context(nc.psum_tensor(f"bank{i}", [P, 512], F32)) for i in range(8)]
    value_banks = Ring(banks[0])
    work_banks = Ring(*banks[1:8])

    x = sb("x", [P, NT, D])
    ident = sb("ident", [P, P])
    ones = sb("ones", [P, P])
    tg = sb("tg", [P, 4])
    zero_row = sb("zero_row", [P, D])
    g_raw = sb("g_raw", [P, 4])
    norm_small = Ring(*[(sb(f"stats{i}", [P, TT, 6]), sb(f"moments{i}", [P, TT, 2]), sb(f"rstd{i}", [P, 4, TT]))
                        for i in range(3)])
    minus_half = sb("minus_half", [P, TT])
    before = sb("before", [P, 8, 8])
    after = sb("after", [P, 8, 8])
    keep_row = sb("keep_row", [P, D], I32)
    x_ready = [None] * NB

    wait_const = []

    def const(fn):
        PO.wait(*wait_const[-1:])
        m = PO.mark(fn)
        wait_const.append(m)
        return m

    const(partial(nc.gpsimd.memset, ident[:, :], 0.0))
    ident_ready = const(partial(nc.gpsimd.affine_select, out=ident[:, :], in_=ident[:, :], compare_op=ALU.not_equal,
                                                  fill=1.0, base=0, pattern=[[-1, P]], channel_multiplier=1))
    const(partial(nc.gpsimd.memset, ones[:, :], 1.0))
    zero_ready = const(partial(nc.gpsimd.memset, zero_row[:, :], 0.0))

    gates_in = dma_sem("gates_in")
    SP.load(gates_in, partial(nc.sync.dma_start, g_raw[:, 0:2], a["g_xattn"].partition_broadcast(P)))
    m = SP.load(gates_in, partial(nc.sync.dma_start, g_raw[:, 2:4], a["g_ffn"].partition_broadcast(P)))
    AC.wait(m)
    tg_ready = AC.mark(partial(nc.scalar.activation, tg[:, :], g_raw[:, :], ACT.Tanh))

    A = tens

    def sba(name, shape, dt=F32):
        return sb(name, shape, dt, A)

    x_in = [dma_sem(f"x_in{b}") for b in range(NB)]

    def load_x(b):
        m = SP.load(x_in[b], partial(nc.sync.dma_start, 
            x[:, TT * b:TT * b + TT, :], a["x"][b].rearrange("(t p) d -> p t d", p=P)))
        x_ready[b] = m

    ctx_tok = Ring(*[sba(f"ctx_tok{i}", [P, TT, CTX]) for i in range(2)])
    for i, slot in enumerate(ctx_tok.slots):
        slot.sem = dma_sem(f"ctx_in{i}")

    wq = [sba(f"wq{l}", [P, KC, D]) for l in range(2)]
    wkv = [sba(f"wkv{l}", [P, 2, 2 * D]) for l in range(2)]
    wo = [sba(f"wo{l}", [P, KC, D]) for l in range(2)]
    qkb = [sba(f"qkb{l}", [P, 2, KC]) for l in range(2)]
    vb = [sba(f"vb{l}", [P, D]) for l in range(2)]
    ob = [sba(f"ob{l}", [P, D]) for l in range(2)]
    attn_w_in = [dma_sem(f"attn_w_in{l}") for l in range(2)]
    attn_w_ready = [None, None]

    def load_attention_weights(l):
        if l == 0:
            q_w, q_b, o_w, o_b = a["L0_xattn_q_w"], a["L0_xattn_q_b"], a["L0_xattn_proj_w"], a["L0_xattn_proj_b"]
            k_w, v_w = a["L0_xattn_kv_w"][:, 0:D], a["L0_xattn_kv_w"][:, D:2 * D]
            k_b, v_b = a["L0_xattn_kv_b"][0:D], a["L0_xattn_kv_b"][D:2 * D]
        else:
            q_w, q_b, o_w, o_b = a["L1_xattn_Wq"], a["L1_xattn_bq"], a["L1_xattn_Wo"], a["L1_xattn_bo"]
            k_w, v_w, k_b, v_b = a["L1_xattn_Wk"], a["L1_xattn_Wv"], a["L1_xattn_bk"], a["L1_xattn_bv"]
        q_col, k_col = q_b.rearrange("(k p) -> p k", p=P), k_b.rearrange("(k p) -> p k", p=P)
        for dst, src in (
            (wq[l][:, :, :], q_w.rearrange("(k p) n -> p k n", p=P)),
            (qkb[l][:, 0, :], q_col),
            (qkb[l][:, 1, :], k_col),
            (wkv[l][:, 0, 0:D], k_w[0:P, :]),
            (wkv[l][0:CTX - P, 1, 0:D], k_w[P:CTX, :]),
            (wkv[l][:, 0, D:2 * D], v_w[0:P, :]),
            (wkv[l][0:CTX - P, 1, D:2 * D], v_w[P:CTX, :]),
            (vb[l][:, :], v_b.partition_broadcast(P)),
            (wo[l][:, :, :], o_w.rearrange("(k p) n -> p k n", p=P)),
            (ob[l][:, :], o_b.partition_broadcast(P)),
        ):
            columns = src is q_col or src is k_col
            m = SP.load(attn_w_in[l], partial(nc.sync.dma_start, 
                dst, src, allow_slow_non_contiguous=columns))
        DV.wait(m)
        DV.mark(partial(nc.vector.tensor_scalar, qkb[l][:, 0, :], qkb[l][:, 0, :], QSCALE, None, ALU.mult))
        attn_w_ready[l] = DV.mark(partial(nc.vector.tensor_scalar, wq[l][:, :, :], wq[l][:, :, :], QSCALE, None, ALU.mult))

    def load_ctx(b):
        slot = yield from ctx_tok.take()
        SP.wait(*slot.free)
        slot.ready = SP.load(slot.sem, partial(nc.sync.dma_start, 
            slot.t[:, :, :], a["ctx_768"][b].rearrange("(t p) d -> p t d", p=P)))
        return slot

    load_x(0)
    load_attention_weights(0)

    w_gate0 = sba("w_gate0", [P, KC, E0 + 1, I0])
    w_up0 = sba("w_up0", [P, KC, E0 + 1, I0])
    w_down0 = sba("w_down0", [P, E0 + 1, D])
    gate_rows = sba("gate_rows", [E0, D])
    gate_wT = sba("gate_wT", [P, KC, E0])
    corr = sba("corr", [P, E0])
    ffn0_in = dma_sem("ffn0_in")
    ffn0_w = None
    loads0 = [(gate_rows[:, :], a["L0_ffn_gate_w"]),
              (corr[:, :], a["L0_ffn_correction_bias"].partition_broadcast(P))]
    for k in range(KC):
        rows = slice(k * P, k * P + P)
        for t, w, shared in ((w_gate0, a["L0_ffn_Wg"], a["L0_ffn_Wg_s"]), (w_up0, a["L0_ffn_Wu"], a["L0_ffn_Wu_s"])):
            loads0.append((t[:, k, 0:E0, :], w[:, rows, :].rearrange("e p i -> p e i")))
            loads0.append((t[:, k, E0, :], shared[rows, :]))
    loads0.append((w_down0[:, 0:E0, :], a["L0_ffn_Wd"].rearrange("e i d -> i e d")))
    loads0.append((w_down0[:, E0, :], a["L0_ffn_Wd_s"]))

    def load_experts0():
        nonlocal ffn0_w
        SP.wait(cw_sel_ready)
        for dst, src in loads0:
            ffn0_w = SP.load(ffn0_in, partial(nc.sync.dma_start, dst, src))

    stack_q = [Slot(sba(f"stack_q{l}", [ROWS, H, S], F32R)) for l in range(2)]
    stack_k = [Slot(sba(f"stack_k{l}", [ROWS, H, S], F32R)) for l in range(2)]
    values = [Slot(sba(f"values{l}", [P, 2, H, 2 * HD])) for l in range(2)]
    xn = Ring(*[sba(f"xn{i}", [P, TT, D]) for i in range(2)])
    xnT = Ring(*[sba(f"xnT{i}", [P, KC, S]) for i in range(3)])
    ctxT = Ring(*[sba(f"ctxT{i}", [P, 2, S]) for i in range(2)])
    for i, slot in enumerate(ctxT.slots):
        slot.sem = dma_sem(f"ctxT_in{i}")
    split = Ring(*[(sba(f"hi{i}", [P, KC, S], F32R), sba(f"lo{i}", [P, KC, S], F32R)) for i in range(2)])
    rowmax = Ring(*[sba(f"rowmax{i}", [P, H, TT]) for i in range(2)])
    shift = Ring(sba("shift", [P, 3, H * TT]))
    shiftT = Ring(sba("shiftT", [3 * H * TT, P]))
    clipped = Ring(*[sba(f"clipped{i}", [P, 2, S]) for i in range(2)])
    LB_HEADS = 2
    lower = Ring(*[sba(f"lower{i}", [P, LB_HEADS, S]) for i in range(2)])
    for i, slot in enumerate(lower.slots):
        slot.sem = dma_sem(f"lower_in{i}")
    probs = Ring(*[sba(f"probs{i}", [P, 2, S]) for i in range(3)])
    weighted = Ring(sba("weighted", [P, 2, S]))
    recip = Ring(sba("recip", [P, TT, 8]))
    attn = Ring(sba("attn", [P, TT, D]))
    attnT = Ring(sba("attnT", [P, KC, S]))
    summed = Ring(*[sba(f"summed{i}", [P, TT, D]) for i in range(1)])
    nan_scratch = Ring(sba("nan_scratch", [P, KC * S]))
    attending = Ring(None)
    nan_sum = sba("nan_sum", [P, 2 * NB])
    vmean_row = Slot(sba("vmean_row", [1, D]))
    inv_s = sba("inv_s", [P, 32])

    half_ready = const(partial(nc.gpsimd.memset, minus_half[:, :], -0.5))
    inv_ready = const(partial(nc.gpsimd.memset, inv_s[:, :], 1.0 / S))
    stacks_ready = []
    for l in range(2):
        for t in (stack_q[l].t, stack_k[l].t):
            DV.put(partial(nc.vector.memset, t[STACK:FULL, :, :].bitcast(F32), 0.0))
        stacks_ready.append(DV.mark(partial(nc.vector.memset, stack_k[l].t[FULL:ROWS, :, :].bitcast(F32), 1.0)))
    values_ready = [DV.mark(partial(nc.vector.memset, values[l].t[:, :, :, HD:2 * HD], 1.0)) for l in range(2)]

    hidden0 = Ring(*[sba(f"hidden0_{i}", [P, S]) for i in range(3)])
    cw_sel_f = w_down0[0:2 * E0, 0:E0 * P // D, :].rearrange("p a (b n) -> p (a b) n", n=P)
    cw_sel = sba("cw_sel", [2 * E0, E0, P], F32R)
    const(partial(nc.gpsimd.memset, cw_sel_f, 0.0))
    for half in range(2):
        m = const(partial(nc.gpsimd.affine_select, 
            out=cw_sel_f, in_=cw_sel_f, compare_op=ALU.not_equal, fill=1.0,
            base=-half * E0, pattern=[[-1, E0], [0, P]], channel_multiplier=1))
    DV.wait(m)
    cw_sel_ready = DV.mark(partial(nc.vector.tensor_copy, cw_sel[:, :, :], cw_sel_f))
    const(partial(nc.gpsimd.memset, before[:, :, :], 1.0))
    const(partial(nc.gpsimd.affine_select, out=before[:, :, :], in_=before[:, :, :], compare_op=ALU.is_gt, fill=0.0,
                                    base=0, pattern=[[1, 8], [-1, 8]], channel_multiplier=0))
    const(partial(nc.gpsimd.memset, after[:, :, :], 1.0))
    order_ready = const(partial(nc.gpsimd.affine_select, out=after[:, :, :], in_=after[:, :, :], compare_op=ALU.is_gt,
                                                  fill=0.0, base=0, pattern=[[-1, 8], [1, 8]],
                                                  channel_multiplier=0))

    def dv(fn, *waits):
        DV.wait(*waits)
        return DV.mark(fn)

    finished = set()

    def until(*names):
        while not finished.issuperset(names):
            yield BUSY

    def layer_norm(b, slot_n, slot_t):
        yield [x_ready[b]]
        s = yield from norm_small.take()
        stats, moments, r = s.t
        DV.wait(*s.free, x_ready[b])
        for t in range(TT):
            m = DV.mark(partial(nc.vector.bn_stats, stats[:, t, :], x[:, TT * b + t, :]))
        DV.wait(m)
        for t in range(TT):
            m_mom = DV.mark(partial(nc.vector.bn_aggr, moments[:, t, :], stats[:, t, :]))
        PO.wait(m_mom, half_ready)
        m = PO.mark(partial(nc.gpsimd.tensor_scalar, r[:, 0, :], moments[:, :, 1], EPS, None, ALU.add))
        for fn in (
            partial(nc.gpsimd.tensor_tensor, r[:, 1, :], r[:, 0, :], minus_half[:, :], ALU.pow),
            partial(nc.gpsimd.tensor_tensor, r[:, 2, :], r[:, 1, :], r[:, 1, :], ALU.mult),
            partial(nc.gpsimd.tensor_tensor, r[:, 2, :], r[:, 2, :], r[:, 0, :], ALU.mult),
            partial(nc.gpsimd.tensor_scalar, r[:, 2, :], r[:, 2, :], -0.5, 1.5, ALU.mult, ALU.add),
            partial(nc.gpsimd.tensor_tensor, r[:, 3, :], r[:, 1, :], r[:, 2, :], ALU.mult),
        ):
            PO.wait(m)
            m = PO.mark(fn)
        yield [m, *slot_n.free]
        DV.wait(m, *slot_n.free)
        for t in range(TT):
            m_n = DV.mark(partial(nc.vector.tensor_scalar,
                slot_n.t[:, t, :], x[:, TT * b + t, :], moments[:, t, 0:1], r[:, 3, t:t + 1],
                ALU.subtract, ALU.mult))
        s.release(m_n)
        slot_n.ready = m_n
        yield [m_n]
        bank = yield from work_banks.take()
        PE.wait(m_n, ident_ready, *bank.free)
        for k in range(KC):
            for t in range(TT):
                o = k * S + t * P
                tr = partial(nc.tensor.transpose,
                    bank.t[:, o:o + P], slot_n.t[:, t, k * P:k * P + P], ident[:, :])
                m = PE.mark(tr) if (k, t) == (KC - 1, TT - 1) else PE.put(tr)
        slot_n.release(m)
        yield [m, *slot_t.free]
        AC.wait(m, *slot_t.free)
        slot_t.ready = AC.mark(partial(nc.scalar.activation,
            slot_t.t[:, :, :].rearrange("p k s -> p (k s)"), bank.t[:, :], ACT.Copy))
        bank.release(slot_t.ready)

    hilo_out = [[dma_sem(f"hilo_out{l}{w}") for w in range(2)] for l in range(2)]
    stack_in = [[dma_sem(f"stack_in{l}{w}") for w in range(2)] for l in range(2)]
    ctxT_out = [dma_sem(f"ctxT_out{i}") for i in range(NB)]
    shift_out = [dma_sem(f"shift_out{l}") for l in range(2)]
    shift_in = [dma_sem(f"shift_in{l}") for l in range(2)]
    z_out = [dma_sem(f"z_out{i}") for i in range(NB)]
    vmean_out = dma_sem("vmean_out")
    ctxT_stored = [None] * NB
    z_stored = [None] * NB
    vmean_stored = [None] * NB
    nan_marks = []
    shifts_ready = {}
    lower_written = {}

    def context(b, l):
        cT = yield from ctxT.take()
        if l == 0:
            slot = yield from load_ctx(b)
            yield [slot.ready]
            bank = yield from work_banks.take()
            PE.wait(slot.ready, ident_ready, *bank.free)
            for t in range(TT):
                PE.put(partial(nc.tensor.transpose, bank.t[:, t * P:t * P + P], slot.t[:, t, 0:P], ident[:, :]))
            for t in range(TT):
                tr = partial(nc.tensor.transpose, bank.t[0:CTX - P, S + t * P:S + t * P + P],
                                                slot.t[:, t, P:CTX], ident[:, :])
                m = PE.mark(tr) if t == TT - 1 else PE.put(tr)
            slot.release(m)
            yield [m, *cT.free]
            AC.wait(m, *cT.free)
            AC.mark(partial(nc.scalar.activation, cT.t[:, 0, :], bank.t[:, 0:S], ACT.Copy))
            cT.ready = AC.mark(partial(nc.scalar.activation, cT.t[0:CTX - P, 1, :], bank.t[0:CTX - P, S:2 * S], ACT.Copy))
            bank.release(cT.ready)
            yield [cT.ready]
            SP.wait(cT.ready)
            SP.load(ctxT_out[b], partial(nc.sync.dma_start, ctxT_dram[b, 0], cT.t[:, 0, :]))
            ctxT_stored[b] = SP.load(ctxT_out[b], partial(nc.sync.dma_start,
                ctxT_dram[b, 1, 0:CTX - P], cT.t[0:CTX - P, 1, :]))
        else:
            yield [ctxT_stored[b], *cT.free]
            SP.wait(ctxT_stored[b], *cT.free)
            SP.load(cT.sem, partial(nc.sync.dma_start, cT.t[:, 0, :], ctxT_dram[b, 0]))
            cT.ready = SP.load(cT.sem, partial(nc.sync.dma_start,
                cT.t[0:CTX - P, 1, :], ctxT_dram[b, 1, 0:CTX - P]))
        return cT

    CTX_CHUNKS = ((0, P), (1, CTX - P))

    def hi_lo(b, l, which, source, weights, rows):
        yield [source.ready, attn_w_ready[l]]
        bank = yield from work_banks.take()
        PE.wait(source.ready, attn_w_ready[l], *bank.free)
        for mt in range(KC):
            for n, (k, r) in enumerate(rows):
                mm = partial(nc.tensor.matmul,
                    bank.t[:, mt * S:mt * S + S], weights[0:r, k, mt * P:mt * P + P], source.t[0:r, k, :],
                    start=n == 0, stop=n == len(rows) - 1)
                m_mm = PE.mark(mm) if mt == KC - 1 and n == len(rows) - 1 else PE.put(mm)
        if which == 0:
            source.release(m_mm)
        else:
            finished.add(("k product", b, l))
        s = yield from split.take()
        hs, ls = s.t
        yield [m_mm, *s.free]
        AC.wait(m_mm, *s.free)
        for mt in range(KC):
            m_h = AC.mark(partial(nc.scalar.activation, hs[:, mt, :], bank.t[:, mt * S:mt * S + S], ACT.Identity,
                                  bias=qkb[l][:, which, mt:mt + 1]))
        yield [m_h]
        DV.wait(m_h, *s.free)
        for mt in range(KC):
            m_l = DV.mark(partial(nc.vector.scalar_tensor_tensor, ls[:, mt, :], bank.t[:, mt * S:mt * S + S],
                                  qkb[l][:, which, mt:mt + 1], hs[:, mt, :].bitcast(F32), ALU.add, ALU.subtract))
        bank.release(m_l)
        yield [m_l]
        dram = qk_dram[l][b]
        SP.wait(m_h, m_l)
        for part, t in enumerate((hs, ls)):
            m_out = SP.load(hilo_out[l][which], partial(nc.sync.dma_start,
                dram[2 * which + part].rearrange("(k p) s -> p k s", p=P), t[:, :, :].bitcast(F32)))
        m_nan = None
        if l == 1:
            yield from nan_scratch.take()
            lo_flat = ls[:, :, :].bitcast(F32).rearrange("p k s -> p (k s)")
            AC.wait(m_l, *nan_scratch.slots[0].free)
            m_nan = AC.mark(partial(nc.scalar.activation, nan_scratch.slots[0].t[:, :], lo_flat, ACT.Copy,
                                    accum_out=nan_sum[:, 2 * b + which:2 * b + which + 1]))
            nan_scratch.slots[0].release(m_nan)
            nan_marks.append(m_nan)
        s.release(m_out, m_nan)
        dst = (stack_q if which == 0 else stack_k)[l]
        if b:
            yield from until(("attend", b - 1, l))
        yield [m_out, *dst.free]
        SP.wait(m_out, stacks_ready[l], *dst.free)
        for blk in range(STACK // HD):
            part = (blk // 2) if which == 0 else (blk % 2)
            src = dram[2 * which + part].rearrange("(h d) s -> d h s", d=HD)
            finished.add(("stacking", which, b, l))
            dst.ready = SP.load(stack_in[l][which], partial(nc.sync.dma_start,
                dst.t[blk * HD:blk * HD + HD, :, :].bitcast(F32), src))

    contexts = {}

    def keys(b, l):
        yield from until(*([("keys", b - 1, l)] if b else []), *([("output", b, 0)] if l == 1 else []))
        cT = contexts[b, l] = yield from context(b, l)
        finished.add(("context", b, l))
        yield from hi_lo(b, l, 1, cT, wkv[l], CTX_CHUNKS)
        finished.add(("keys", b, l))

    def queries(b, l):
        yield from until(*([("queries", b - 1, l)] if b else []), *([("experts0", b)] if l == 1 else []))
        if l == 0 and b + 1 < NB:
            load_x(b + 1)
        slot_n = yield from xn.take()
        xT = yield from xnT.take()
        yield from layer_norm(b, slot_n, xT)
        yield from hi_lo(b, l, 0, xT, wq[l], ((0, P), (1, P)))
        finished.add(("queries", b, l))

    def value_rows(b, l):
        yield from until(("k product", b, l), *([("value rows", b - 1, l)] if b else []))
        cT = contexts[b, l]
        bank = yield from work_banks.take()
        PE.wait(cT.ready, attn_w_ready[l], *bank.free)
        for kt in range(2):
            for k, r in CTX_CHUNKS:
                mm = partial(nc.tensor.matmul,
                    bank.t[:, kt * D:kt * D + D], cT.t[0:r, k, kt * P:kt * P + P], wkv[l][0:r, k, D:2 * D],
                    start=k == 0, stop=k == 1)
                m = PE.mark(mm) if (kt, k) == (1, 1) else PE.put(mm)
        cT.release(m, ctxT_stored[b] if l == 0 else None)
        if b:
            yield from until(("attend", b - 1, l))
        v = values[l]
        yield [m, *v.free]
        DV.wait(values_ready[l], m, attn_w_ready[l], *v.free)
        v.ready = DV.mark(partial(nc.vector.tensor_tensor,
            v.t[:, :, :, 0:HD], bank.t[:, :].rearrange("p (k h d) -> p k h d", k=2, d=HD),
            vb[l][:, :].rearrange("p (h d) -> p h d", d=HD).unsqueeze(1).broadcast_to([P, 2, H, HD]), ALU.add))
        bank.release(v.ready)
        finished.add(("value rows", b, l))
        if l == 1:
            yield [v.ready]
            bank = yield from work_banks.take()
            PE.wait(v.ready, inv_ready, *bank.free)
            for kt in range(2):
                mm = partial(nc.tensor.matmul, bank.t[0:32, 0:D].rearrange("p (h d) -> p h d", d=HD),
                                               inv_s[:, :], v.t[:, kt, :, 0:HD], start=kt == 0, stop=kt == 1)
                m = PE.mark(mm) if kt else PE.put(mm)
            finished.add(("mean", b))
            yield [m, *vmean_row.free]
            AC.wait(m, *vmean_row.free)
            m = AC.mark(partial(nc.scalar.activation, vmean_row.t[0:1, :], bank.t[0:1, 0:D], ACT.Copy))
            bank.release(m)
            yield [m]
            SP.wait(m)
            vmean_stored[b] = SP.load(vmean_out, partial(nc.sync.dma_start, vmean_dram[b:b + 1, :], vmean_row.t[0:1, :]))
            vmean_row.free = [vmean_stored[b]]

    def maxima(b, l):
        yield from until(("keys", b, l), ("queries", b, l))
        sq, sk = stack_q[l], stack_k[l]
        mx = yield from rowmax.take()
        before_last = None
        for h in range(H + 1):
            yield [sq.ready, sk.ready]
            if h < H:
                bank = yield from work_banks.take()
                PE.wait(sq.ready, sk.ready, *bank.free)
                for t in range(TT):
                    mm = partial(nc.tensor.matmul, bank.t[:, t * S:t * S + S], sq.t[0:FULL, h, t * P:t * P + P],
                                                      sk.t[0:FULL, h, :], start=True, stop=True)
                    m = PE.mark(mm) if t == TT - 1 else PE.put(mm)
            if h:
                last_bank, last_m = before_last
                DV.wait(last_m, *mx.free)
                m_max = DV.mark(partial(nc.vector.tensor_reduce,
                    mx.t[:, h - 1, :], last_bank.t[:, :].rearrange("p (t s) -> p t s", t=TT), AX, ALU.max))
                last_bank.release(m_max)
            before_last = (bank, m)
        flat = mx.t[:, :, :].rearrange("p h t -> p (h t)")
        if l == 1:
            m_max = dv(partial(nc.vector.tensor_scalar, flat, flat, CLAMP, -CLAMP, ALU.min, ALU.max), m_max)
        sh = yield from shift.take()
        DV.wait(m_max, *sh.free)
        m_h = DV.mark(partial(nc.vector.tensor_scalar, sh.t[:, 0, :].bitcast(F32R), flat, -1.0, None, ALU.mult))
        m_b = DV.mark(partial(nc.vector.tensor_scalar, sh.t[:, 2, :], flat, -1.0, -CLAMP, ALU.mult, ALU.add))
        m_l = dv(partial(nc.vector.scalar_tensor_tensor, sh.t[:, 1, :].bitcast(F32R), flat, -1.0, sh.t[:, 0, :],
                                                  ALU.mult, ALU.subtract), m_h)
        mx.release(m_l)
        yield [m_l]
        bank = yield from work_banks.take()
        PE.wait(m_l, m_b, *bank.free)
        m = PE.mark(partial(nc.tensor.transpose, bank.t[0:3 * H * TT, 0:P],
                                          sh.t[:, :, :].rearrange("p j r -> p (j r)"), ident[:, :]))
        sh.release(m)
        shT = yield from shiftT.take()
        yield [m, *shT.free]
        AC.wait(m, *shT.free)
        m = AC.mark(partial(nc.scalar.activation, shT.t[:, :], bank.t[0:3 * H * TT, 0:P], ACT.Copy))
        bank.release(m)
        yield [m]
        SP.wait(m)
        m = SP.load(shift_out[l], partial(nc.sync.dma_start, max_dram[l][b], shT.t[:, :]))
        shT.release(m)
        lower_written[b, l] = m
        yield [m]
        SP.wait(m)
        shifts_ready[b, l] = SP.load(shift_in[l], partial(nc.sync.dma_start,
            sq.t[FULL:ROWS, :, :].bitcast(F32).rearrange("j h s -> j (h s)"),
            max_dram[l][b, 0:2 * H * TT].rearrange("(j r) q -> j (r q)", j=2)))
        finished.add(("maxima", b, l))

    normal = {}

    def attend(b, l):
        yield from until(("maxima", b, l), ("value rows", b, l), *([("mean", b)] if l == 1 else []))
        lock = yield from attending.take()
        normal[b, l] = yield from attn.take()
        sq, sk, v = stack_q[l], stack_k[l], values[l]
        two = lambda t: t[:, :].rearrange("p (k s) -> p k s", k=2)

        def load_lower(h):
            low = yield from lower.take()
            yield low.free
            SP.wait(lower_written[b, l], *low.free)
            low.ready = SP.load(low.sem, partial(nc.sync.dma_start,
                low.t[:, :, :].rearrange("p h s -> p (h s)"),
                max_dram[l][b, 2 * H * TT + h * TT:2 * H * TT + (h + LB_HEADS) * TT]
                .rearrange("r q -> (r q)").partition_broadcast(P)))
            return low

        low = None
        next_low = (yield from load_lower(0)) if l == 1 else None
        clips, exps = [], []
        for h in range(H + 2):
            if h < H:
                if l == 1 and h % LB_HEADS == 0:
                    low = next_low
                    if h + LB_HEADS < H:
                        next_low = yield from load_lower(h + LB_HEADS)
                yield [shifts_ready[b, l]]
                bank = yield from work_banks.take()
                PE.wait(shifts_ready[b, l], *bank.free)
                for kt in range(2):
                    mm = partial(nc.tensor.matmul,
                        bank.t[:, kt * S:kt * S + S], sk.t[:, h, kt * P:kt * P + P], sq.t[:, h, :],
                        start=True, stop=True)
                    m = PE.mark(mm) if kt else PE.put(mm)
                yield [m]
                if l == 1:
                    c = yield from clipped.take()
                    DV.wait(m, low.ready, *c.free)
                    i = h % LB_HEADS
                    m = DV.mark(partial(nc.vector.scalar_tensor_tensor,
                        c.t[:, :, :], two(bank.t), 0.0, low.t[:, i:i + 1, :].broadcast_to([P, 2, S]),
                        ALU.min, ALU.max))
                    bank.release(m)
                    if i == LB_HEADS - 1:
                        low.release(m)
                    clips.append((h, c, c.t[:, :, :], m))
                else:
                    clips.append((h, bank, two(bank.t), m))
            if clips and (l == 0 or h >= 1):
                hc, source, view, m = clips.pop(0)
                p = yield from probs.take()
                AC.wait(m, *p.free)
                p.ready = AC.mark(partial(nc.scalar.activation, p.t[:, :, :], view, ACT.Exp))
                source.release(p.ready)
                exps.append((hc, p))
            if len(exps) > 1 or h >= H and exps:
                hv, p = exps.pop(0)
                yield [p.ready]
                if hv % 8 == 0:
                    vbank = yield from value_banks.take()
                    PE.wait(*vbank.free)
                c, half = hv % 4, (hv // 4) % 2
                PE.wait(p.ready, v.ready)
                for kt in range(2):
                    mm = partial(nc.tensor.matmul, vbank.t[32 * c:32 * c + 32, half * S:half * S + S],
                                 v.t[:, kt, hv, :], p.t[:, kt, :], start=kt == 0, stop=kt == 1)
                    m = PE.mark(mm) if kt else PE.put(mm)
                p.release(m)
                if hv % 8 == 7:
                    vbank.ready = m
                    summed_values[b, l, hv // 8] = vbank
                    finished.add(("sums", b, l, hv // 8))
        sq.free = sk.free = v.free = [m]
        finished.add(("attend", b, l))
        lock.release()

    summed_values = {}

    def value_out(b, l, pair):
        yield from until(("sums", b, l, pair))
        vbank = summed_values[b, l, pair]
        w = yield from weighted.take()
        yield [vbank.ready, *w.free]
        AC.wait(vbank.ready, *w.free)
        m = AC.mark(partial(nc.scalar.activation, w.t[:, :, :].rearrange("p g s -> p (g s)"), vbank.t[:, :], ACT.Copy))
        vbank.release(m)
        yield [m]
        bank = yield from work_banks.take()
        PE.wait(m, *bank.free)
        for t in range(TT):
            for g in range(2):
                o = (t * 2 + g) * P
                tr = partial(nc.tensor.transpose, bank.t[:, o:o + P], w.t[:, g, t * P:t * P + P], ident[:, :])
                m = PE.mark(tr) if (t, g) == (TT - 1, 1) else PE.put(tr)
        w.release(m)
        view = bank.t[:, :].rearrange("p (t h e) -> p t h e", t=TT, e=2 * HD)
        o, r = normal[b, l], (yield from recip.take())
        yield [m, *o.free]
        DV.wait(m, *r.free, *o.free)
        m = DV.mark(partial(nc.vector.reciprocal, r.t[:, :, :], view[:, :, :, HD]))
        m = dv(partial(nc.vector.tensor_tensor,
            o.t[:, :, pair * P:pair * P + P].rearrange("p t (h d) -> p t h d", d=HD), view[:, :, :, 0:HD],
            r.t[:, :, :].unsqueeze(3).broadcast_to([P, TT, 8, HD]), ALU.mult), m)
        r.release(m)
        bank.release(m)
        o.ready = m
        finished.add(("normal", b, l, pair))

    def output(b, l):
        yield from until(("normal", b, l, 0), ("normal", b, l, 1))
        o = normal[b, l]
        yield [o.ready]
        bank = yield from work_banks.take()
        PE.wait(o.ready, *bank.free)
        for k in range(KC):
            for t in range(TT):
                c = k * S + t * P
                tr = partial(nc.tensor.transpose, bank.t[:, c:c + P], o.t[:, t, k * P:k * P + P], ident[:, :])
                m = PE.mark(tr) if (k, t) == (KC - 1, TT - 1) else PE.put(tr)
        o.release(m)
        oT = yield from attnT.take()
        yield [m, *oT.free]
        AC.wait(m, *oT.free)
        m = AC.mark(partial(nc.scalar.activation, oT.t[:, :, :].rearrange("p k s -> p (k s)"), bank.t[:, :], ACT.Copy))
        bank.release(m)
        yield [m]
        bank = yield from work_banks.take()
        PE.wait(m, *bank.free)
        for t in range(TT):
            for k in range(KC):
                mm = partial(nc.tensor.matmul,
                    bank.t[:, t * D:t * D + D], oT.t[:, k, t * P:t * P + P], wo[l][:, k, :],
                    start=k == 0, stop=k == KC - 1)
                m = PE.mark(mm) if (t, k) == (TT - 1, KC - 1) else PE.put(mm)
        oT.release(m)
        s = yield from summed.take()
        yield [m, *s.free]
        DV.wait(m, *s.free)
        m = DV.mark(partial(nc.vector.tensor_tensor,
            s.t[:, :, :], bank.t[:, :].rearrange("p (t d) -> p t d", t=TT),
            ob[l][:, :].unsqueeze(1).broadcast_to([P, TT, D]), ALU.add))
        bank.release(m)
        xs = x[:, TT * b:TT * b + TT, :]
        if l == 0:
            m = dv(partial(nc.vector.scalar_tensor_tensor, xs, s.t[:, :, :], tg[:, 0:1], xs, ALU.mult, ALU.add),
                   m, tg_ready)
            x_ready[b] = m
            s.release(m)
        else:
            m = dv(partial(nc.vector.tensor_scalar, s.t[:, :, :], s.t[:, :, :], tg[:, 1:2], None, ALU.mult), m, tg_ready)
            yield [m]
            SP.wait(m)
            z_stored[b] = SP.load(z_out[b], partial(nc.sync.dma_start,
                z_dram[b].rearrange("(t p) d -> p t d", p=P), s.t[:, :, :]))
            s.release(z_stored[b])
        finished.add(("output", b, l))

    act_gate = Ring(*[sba(f"act_gate{i}", [P, S]) for i in range(2)])
    act_t = Ring(*[sba(f"act_t{i}", [P, S]) for i in range(2)])
    cwT = Ring(sba("cwT", [2 * E0, S], F32R))
    route0 = Ring(sba("rt", [P, 12, TT, 8]))
    pair0 = sba("pair0", [P, 2, TT, 8, 8])
    cw_hl = Ring(sba("cw_hl", [P, TT, 2 * E0]))

    def rank_of(values_ap, ranks, n, tiles, pa, pb, m):
        j = values_ap.unsqueeze(2).broadcast_to([P, tiles, n, n])
        i = values_ap.unsqueeze(3).broadcast_to([P, tiles, n, n])
        bef = before[:, 0:n, 0:n].unsqueeze(1).broadcast_to([P, tiles, n, n])
        aft = after[:, 0:n, 0:n].unsqueeze(1).broadcast_to([P, tiles, n, n])
        DV.wait(m, order_ready)
        m1 = DV.mark(partial(nc.vector.tensor_tensor, pa, j, i, ALU.is_ge))
        m2 = DV.mark(partial(nc.vector.tensor_tensor, pb, j, i, ALU.is_gt))
        m1 = dv(partial(nc.vector.tensor_tensor, pa, pa, bef, ALU.mult), m1)
        m2 = dv(partial(nc.vector.tensor_tensor, pb, pb, aft, ALU.mult), m2)
        m1 = dv(partial(nc.vector.tensor_tensor, pa, pa, pb, ALU.add), m1, m2)
        return dv(partial(nc.vector.tensor_reduce, ranks, pa, AX, ALU.add), m1)

    gate_wT_ready = []

    def transpose_gate():
        yield [ffn0_w]
        bank = yield from work_banks.take()
        PE.wait(ffn0_w, ident_ready, *bank.free)
        for k in range(KC):
            tr = partial(nc.tensor.transpose, bank.t[:, k * E0:k * E0 + E0], gate_rows[:, k * P:k * P + P],
                                            ident[0:E0, 0:E0])
            m = PE.mark(tr) if k else PE.put(tr)
        AC.wait(m)
        m = AC.mark(partial(nc.scalar.activation, gate_wT[:, :, :].rearrange("p k e -> p (k e)"),
                                           bank.t[:, 0:KC * E0], ACT.Copy))
        bank.release(m)
        gate_wT_ready.append(m)

    def experts0(b):
        yield from until(("output", b, 0), *([("routed0", b - 1)] if b else []))
        slot_n = yield from xn.take()
        xT = yield from xnT.take()
        yield from layer_norm(b, slot_n, xT)
        if b == 0:
            yield from transpose_gate()
        rt = yield from route0.take()
        yield [xT.ready]
        bank = yield from work_banks.take()
        PE.wait(xT.ready, *gate_wT_ready, *bank.free)
        for t in range(TT):
            for k in range(KC):
                mm = partial(nc.tensor.matmul,
                    bank.t[:, t * E0:t * E0 + E0], xT.t[:, k, t * P:t * P + P], gate_wT[:, k, :],
                    start=k == 0, stop=k == KC - 1)
                m = PE.mark(mm) if (t, k) == (TT - 1, KC - 1) else PE.put(mm)
        row = lambda i: rt.t[:, i, :, :]
        yield [m]
        AC.wait(m, *rt.free)
        m = AC.mark(partial(nc.scalar.activation, row(0), bank.t[:, 0:TT * E0].rearrange("p (t e) -> p t e", t=TT),
                                           ACT.Exp, scale=-1.0))
        bank.release(m)
        yield [m]
        m = dv(partial(nc.vector.tensor_scalar, row(1), row(0), 1.0, None, ALU.add), m)
        m_s = dv(partial(nc.vector.reciprocal, row(2), row(1)), m)
        m = dv(partial(nc.vector.tensor_tensor, row(3), row(2), corr[:, :].unsqueeze(1).broadcast_to([P, TT, E0]),
                                         ALU.add), m_s, ffn0_w)
        grp = row(3).rearrange("p t (g i) -> p t g i", i=E0 // NG)
        m = dv(partial(nc.vector.tensor_tensor, row(4)[:, :, 0:NG], grp[:, :, :, 0], grp[:, :, :, 1], ALU.add), m)
        yield []
        m = rank_of(row(4)[:, :, 0:NG], row(5)[:, :, 0:NG], NG, TT, pair0[:, 0, :, 0:NG, 0:NG],
                    pair0[:, 1, :, 0:NG, 0:NG], m)
        m = dv(partial(nc.vector.tensor_scalar, row(6)[:, :, 0:NG], row(5)[:, :, 0:NG], TKG - 0.5, None, ALU.is_lt), m)
        m = dv(partial(nc.vector.tensor_tensor, row(7).rearrange("p t (g i) -> p t g i", i=E0 // NG), grp,
                                         row(6)[:, :, 0:NG].unsqueeze(3).broadcast_to([P, TT, NG, E0 // NG]),
                                         ALU.mult), m)
        yield []
        m = rank_of(row(7), row(8), E0, TT, pair0[:, 0], pair0[:, 1], m)
        yield []
        m = dv(partial(nc.vector.scalar_tensor_tensor, row(9), row(8), TOPK0 - 0.5, row(2), ALU.is_lt, ALU.mult), m)
        m = dv(partial(nc.vector.tensor_reduce, row(10)[:, :, 0], row(9), AX, ALU.add), m)
        m = dv(partial(nc.vector.tensor_scalar, row(10)[:, :, 1], row(10)[:, :, 0], 1e-20, None, ALU.add), m)
        m = dv(partial(nc.vector.reciprocal, row(10)[:, :, 2], row(10)[:, :, 1]), m)
        m = dv(partial(nc.vector.scalar_tensor_tensor, row(11), row(9), 2.5 * 0.5,
                                                row(10)[:, :, 2:3].broadcast_to([P, TT, E0]), ALU.mult, ALU.mult),
               m)
        hl = yield from cw_hl.take()
        m = dv(partial(nc.vector.tensor_copy, hl.t[:, :, 0:E0].bitcast(F32R), row(11)), m, *hl.free)
        m = dv(partial(nc.vector.tensor_tensor, hl.t[:, :, E0:2 * E0].bitcast(F32R), row(11), hl.t[:, :, 0:E0],
                                         ALU.subtract), m)
        rt.release(m)
        yield [m]
        bank = yield from work_banks.take()
        PE.wait(m, *bank.free)
        for t in range(TT):
            tr = partial(nc.tensor.transpose, bank.t[0:2 * E0, t * P:t * P + P], hl.t[:, t, :], ident[:, :])
            m = PE.mark(tr) if t == TT - 1 else PE.put(tr)
        hl.release(m)
        cw = yield from cwT.take()
        yield [m, *cw.free]
        AC.wait(m, *cw.free)
        cw.ready = AC.mark(partial(nc.scalar.activation, cw.t[:, :], bank.t[0:2 * E0, 0:S], ACT.Copy))
        bank.release(cw.ready)
        finished.add(("routed0", b))
        y = yield from work_banks.take()
        PE.wait(*y.free)
        order = [E0] + list(range(E0))
        hiddens = []
        for n in range(E0 + 2):
            if n <= E0:
                e_ = order[n]
                gu = yield from work_banks.take()
                PE.wait(*gu.free)
                for half, w in enumerate((w_gate0, w_up0)):
                    for k in range(KC):
                        mm = partial(nc.tensor.matmul,
                            gu.t[:, half * S:half * S + S], w[:, k, e_, :], xT.t[:, k, :], start=k == 0,
                            stop=k == KC - 1)
                        m_gu = PE.mark(mm) if half and k == KC - 1 else PE.put(mm)
                    if half == 0:
                        yield []
                if n == E0:
                    xT.release(m_gu)
            if hiddens:
                yield []
                e_down, h = hiddens.pop()
                PE.wait(h.ready)
                for t in range(TT):
                    mm = partial(nc.tensor.matmul,
                        y.t[:, t * D:t * D + D], h.t[:, t * P:t * P + P], w_down0[:, e_down, :], start=n == 1 and t == 0,
                        stop=n == E0 + 1, skip_group_check=True)
                    m_y = PE.mark(mm) if t == TT - 1 else PE.put(mm)
                h.release(m_y)
            if n > E0:
                break
            th = yield from act_gate.take()
            yield [m_gu]
            AC.wait(m_gu, *th.free)
            m = AC.mark(partial(nc.scalar.activation, th.t[:, :], gu.t[:, 0:S], ACT.Tanh, scale=0.5))
            if n:
                scale = yield from work_banks.take()
                PE.wait(cw.ready, cw_sel_ready, *scale.free)
                m_w = PE.mark(partial(nc.tensor.matmul, scale.t[:, 0:S], cw_sel[:, e_, :], cw.t[:, :],
                                      start=True, stop=True))
                if n == E0:
                    cw.release(m_w)
            yield [m, m_gu]
            tmp = yield from act_t.take()
            m = dv(partial(nc.vector.scalar_tensor_tensor,
                tmp.t[:, :], th.t[:, :], 1.0, gu.t[:, 0:S], ALU.add, ALU.mult), m, *tmp.free)
            th.release(m)
            if n:
                m = dv(partial(nc.vector.tensor_tensor, tmp.t[:, :], tmp.t[:, :], scale.t[:, 0:S], ALU.mult), m, m_w)
                scale.release(m)
            h = yield from hidden0.take()
            h.ready = dv(partial(nc.vector.scalar_tensor_tensor,
                h.t[:, :], tmp.t[:, :], 1.0 if n else 0.5, gu.t[:, S:2 * S], ALU.mult, ALU.mult), m, m_gu, *h.free)
            tmp.release(h.ready)
            gu.release(h.ready)
            hiddens.append((e_, h))
        xs = x[:, TT * b:TT * b + TT, :]
        yield [m_y]
        m = dv(partial(nc.vector.scalar_tensor_tensor, xs, y.t[:, :].rearrange("p (t d) -> p t d", t=TT), tg[:, 2:3], xs,
                                                ALU.mult, ALU.add), m_y, tg_ready)
        y.release(m)
        x_ready[b] = m
        finished.add(("experts0", b))

    xs_zero = dma_sem("xs_zero")
    zero_filled = None

    def later_loads():
        nonlocal zero_filled
        yield from until(("stacking", 0, 0, 0))
        load_experts0()
        yield from until(("maxima", 0, 0))
        load_attention_weights(1)
        SP.wait(zero_ready)
        zero_filled = SP.load(xs_zero, partial(nc.sync.dma_start,
            xs_dram.rearrange("(p n) d -> p n d", p=P), zero_row[:, :].unsqueeze(1).broadcast_to([P, BLOCKS, D])))

    stages = [later_loads()]
    for b in range(NB):
        for l in range(2):
            stages += [output(b, l), value_out(b, l, 1), value_out(b, l, 0), attend(b, l), maxima(b, l),
                       queries(b, l), keys(b, l), value_rows(b, l)]
    stages += [experts0(b) for b in range(NB)]
    weave(stages, PE)

    flag = sba("flag", [P, 4])
    vm = sba("vm", [NB, D])
    vmT = sba("vmT", [P, KC, NB])
    zalt = sba("zalt", [NB, D])
    alt_in, zalt_out = dma_sem("alt_in"), dma_sem("zalt_out")
    m = dv(partial(nc.vector.tensor_reduce, flag[:, 0:1], nan_sum[:, :], AX, ALU.add), nan_marks[-1])
    m = dv(partial(nc.vector.tensor_tensor, flag[:, 1:2], flag[:, 0:1], flag[:, 0:1], ALU.is_equal), m)
    bank = work_banks.grab()
    PE.wait(m, *bank.free)
    m = PE.mark(partial(nc.tensor.matmul, bank.t[:, 0:1], ones[:, :], flag[:, 1:2], start=True, stop=True))
    m = dv(partial(nc.vector.tensor_scalar, flag[:, 2:3], bank.t[:, 0:1], P - 0.5, None, ALU.is_lt), m)
    bank.release(m)
    m_keep = dv(partial(nc.vector.tensor_scalar, keep_row[:, :], zero_row[:, :], flag[:, 2:3], None, ALU.add), m, zero_ready)
    SP.wait(*vmean_stored)
    m = SP.load(alt_in, partial(nc.sync.dma_start, vm[:, :], vmean_dram[:, :]))
    bank = work_banks.grab()
    PE.wait(m, *bank.free)
    for k in range(KC):
        tr = partial(nc.tensor.transpose, bank.t[:, k * NB:k * NB + NB], vm[:, k * P:k * P + P],
                                                   ident[0:NB, 0:NB])
        m = PE.mark(tr) if k else PE.put(tr)
    AC.wait(m)
    m = AC.mark(partial(nc.scalar.activation, vmT[:, :, :].rearrange("p k b -> p (k b)"), bank.t[:, 0:KC * NB], ACT.Copy))
    bank.release(m)
    bank2 = work_banks.grab()
    PE.wait(m, *bank2.free)
    for k in range(KC):
        mm = partial(nc.tensor.matmul, bank2.t[0:NB, 0:D], vmT[:, k, :], wo[1][:, k, :], start=k == 0, stop=k == 1)
        m = PE.mark(mm) if k else PE.put(mm)
    m = dv(partial(nc.vector.tensor_tensor, zalt[:, :], bank2.t[0:NB, 0:D], ob[1][0:NB, :], ALU.add), m)
    bank2.release(m)
    m = dv(partial(nc.vector.tensor_scalar, zalt[:, :], zalt[:, :], tg[0:NB, 1:2], None, ALU.mult), m)
    SP.wait(m)
    m_alt = SP.load(zalt_out, partial(nc.sync.dma_start, zalt_dram[:, :], zalt[:, :]))
    before_experts1 = [m_alt]

    C = es
    tail = [(q.sem, q.count) for q in (PE, DV, AC, PO)] + [m for m in z_stored if m] + [m_alt]
    tens.close()

    for q in (PE, DV, AC, PO, SP):
        q.wait(*tail)

    xn1 = sb("xn_all", [P, NT, D])
    z_in = Ring(*[sb(f"z_in{i}", [P, TT, D]) for i in range(2)])
    alt_row = Ring(*[sb(f"alt_row{i}", [P, D]) for i in range(2)])
    for i, slot in enumerate(z_in.slots):
        slot.sem = dma_sem(f"z_in{i}")
    x1T = Ring(*[sb(f"x1T{i}", [P, KC, S]) for i in range(2)])
    wr = sb("wr", [P, KC, E1])
    br = sb("br", [P, E1])
    b1_rows = sb("b1_rows", [E1 * JH, P])
    b1T = sb("b1T", [P, E1, JH])
    b2 = sb("b2", [E1, D])
    lg = sb("lg", [P, NT, E1])
    W1S = 3
    w1 = Ring(*[sb(f"w1_{i}", [P, KC, H1]) for i in range(W1S)])
    w2 = Ring(*[sb(f"w2_{i}", [P, JH, D]) for i in range(W1S)])
    router_in = dma_sem("router_in")
    for dst, src in ((wr[:, :, :], a["L1_ffn_Wr"].rearrange("(k p) e -> p k e", p=P)),
                     (br[:, :], a["L1_ffn_br"].partition_broadcast(P)),
                     (b1_rows[:, :], a["L1_ffn_b1"].rearrange("e (j p) -> (e j) p", p=P)),
                     (b2[:, :], a["L1_ffn_b2"])):
        router_w = SP.load(router_in, partial(nc.sync.dma_start, dst, src))

    def finish_attention(b):
        z, alt = (yield from z_in.take()), (yield from alt_row.take())
        SP.wait(z_stored[b], m_alt, *z.free, *alt.free)
        SP.load(z.sem, partial(nc.sync.dma_start, z.t[:, :, :], z_dram[b].rearrange("(t p) d -> p t d", p=P)))
        m = SP.load(z.sem, partial(nc.sync.dma_start, alt.t[:, :], zalt_dram[b].partition_broadcast(P)))
        yield [m]
        DV.wait(m)
        for t in range(TT):
            m = DV.mark(partial(nc.vector.copy_predicated, z.t[:, t, :], keep_row[:, :], alt.t[:, :]))
        alt.release(m)
        xs = x[:, TT * b:TT * b + TT, :]
        m = dv(partial(nc.vector.tensor_tensor, xs, xs, z.t[:, :, :], ALU.add), m)
        z.release(m)
        x_ready[b] = m
        yield [m]
        n = Slot(xn1[:, TT * b:TT * b + TT, :])
        xT = yield from x1T.take()
        yield from layer_norm(b, n, xT)
        xn_ready.append(n.ready)
        yield [xT.ready]
        bank = yield from work_banks.take()
        PE.wait(xT.ready, router_w, *bank.free)
        for t in range(TT):
            for k in range(KC):
                mm = partial(nc.tensor.matmul, 
                    bank.t[:, t * E1:t * E1 + E1], xT.t[:, k, t * P:t * P + P], wr[:, k, :],
                    start=k == 0, stop=k == KC - 1)
                m = PE.mark(mm) if (t, k) == (TT - 1, KC - 1) else PE.put(mm)
        xT.release(m)
        yield [m]
        m = dv(partial(nc.vector.tensor_tensor, 
            lg[:, TT * b:TT * b + TT, :], bank.t[:, 0:TT * E1].rearrange("p (t e) -> p t e", t=TT),
            br[:, :].unsqueeze(1).broadcast_to([P, TT, E1]), ALU.add), m, router_w)
        bank.release(m)
        lg_ready.append(m)

    xn_ready, lg_ready = [], []
    weave([finish_attention(b) for b in range(NB)], PE)

    q1 = sb("q1", [P, 8, NT, E1])
    pair1 = sb("pair1", [P, 2, NT, E1, E1])
    small = sb("small", [P, 8, NT])
    row = lambda i: q1[:, i, :, :]
    tok = lambda i: small[:, i, :]
    wide = lambda ap: ap.unsqueeze(2).broadcast_to([P, NT, E1])
    m_rank = rank_of(lg[:, :, :], row(0), E1, NT, pair1[:, 0], pair1[:, 1], lg_ready[-1])
    m_mask = dv(partial(nc.vector.tensor_scalar, row(1), row(0), TOPK1 - 0.5, None, ALU.is_lt), m_rank)

    tri = sb("tri", [P, P])
    const(partial(nc.gpsimd.memset, tri[:, :], 1.0))
    tri_ready = const(partial(nc.gpsimd.affine_select, out=tri[:, :], in_=tri[:, :], compare_op=ALU.is_gt, fill=0.0,
                                                base=0, pattern=[[1, P]], channel_multiplier=-1))
    bank = work_banks.grab()
    PE.wait(m_mask, tri_ready, *bank.free)
    PE.put(partial(nc.tensor.matmul, bank.t[:, 0:NT * E1], tri[:, :], row(1).rearrange("p t e -> p (t e)"),
                              start=True, stop=False, skip_group_check=True))
    for t in range(NT):
        n = NT - 1 - t
        if n:
            PE.put(partial(nc.tensor.matmul, 
                bank.t[:, (t + 1) * E1:NT * E1].rearrange("p (t e) -> p t e", e=E1), ones[:, :],
                row(1)[:, t:t + 1, :].broadcast_to([P, n, E1]), start=False, stop=False, skip_group_check=True))
        mm = partial(nc.tensor.matmul, bank.t[:, NT * E1:NT * E1 + E1], ones[:, :], row(1)[:, t, :], start=False,
                                     stop=t == NT - 1, skip_group_check=True)
        m_count = PE.mark(mm) if t == NT - 1 else PE.put(mm)
    m_max = dv(partial(nc.vector.tensor_reduce, tok(0), lg[:, :, :], AX, ALU.max), m_mask)
    m = dv(partial(nc.vector.tensor_tensor, row(2), lg[:, :, :], row(1), ALU.mult), m_mask)
    m1 = dv(partial(nc.vector.tensor_scalar, row(3), row(1), -NEG_INF, NEG_INF, ALU.mult, ALU.add), m_mask)
    m = dv(partial(nc.vector.tensor_tensor, row(2), row(2), row(3), ALU.add), m, m1)
    m = dv(partial(nc.vector.tensor_tensor, row(2), row(2), wide(tok(0)), ALU.subtract), m, m_max)
    AC.wait(m)
    m = AC.mark(partial(nc.scalar.activation, row(3), row(2), ACT.Exp))
    m = dv(partial(nc.vector.tensor_reduce, tok(1), row(3), AX, ALU.add), m)
    m = dv(partial(nc.vector.reciprocal, tok(2), tok(1)), m)
    m = dv(partial(nc.vector.tensor_scalar, tok(2), tok(2), tg[:, 3:4], None, ALU.mult), m)
    m_w = dv(partial(nc.vector.tensor_tensor, row(4), row(3), wide(tok(2)), ALU.mult), m)
    TB = NB * S // P
    steps = sb("steps", [P, E1, TB])
    steps_ready = const(partial(nc.gpsimd.iota, steps[:, :, :], [[0, E1], [P, TB]], base=0, channel_multiplier=0,
                                         allow_small_or_imprecise_dtypes=True))
    cnt = sb("cnt", [P, 6, E1])
    c = lambda i: cnt[:, i, :]
    m = dv(partial(nc.vector.tensor_copy, c(0), bank.t[:, NT * E1:NT * E1 + E1]), m_count)
    m = dv(partial(nc.vector.tensor_tensor, steps[:, :, :], c(0).unsqueeze(2).broadcast_to([P, E1, TB]), steps[:, :, :],
                                     ALU.is_gt), m, steps_ready)
    m = dv(partial(nc.vector.tensor_reduce, c(1), steps[:, :, :], AX, ALU.add), m)
    cum = sb("cum", [P, E1, E1])
    m = dv(partial(nc.vector.tensor_tensor, cum[:, :, :], before[:, :, :], c(1).unsqueeze(1).broadcast_to([P, E1, E1]),
                                     ALU.mult), m)
    m = dv(partial(nc.vector.tensor_reduce, c(2), cum[:, :, :], AX, ALU.add), m)
    m_end = dv(partial(nc.vector.tensor_tensor, c(3), c(2), c(1), ALU.add), m)
    m = dv(partial(nc.vector.tensor_scalar, c(4), c(2), float(P), None, ALU.mult), m)
    m_slot = dv(partial(nc.vector.tensor_tensor, 
        row(5), bank.t[:, 0:NT * E1].rearrange("p (t e) -> p t e", e=E1),
        c(4).unsqueeze(1).broadcast_to([P, NT, E1]), ALU.add), m)
    bank.release(m_slot)
    slot_i = sb("slot_i", [P, TOPK1, NT], I32)
    slot_ready = []
    for r in range(TOPK1):
        m = dv(partial(nc.vector.tensor_scalar, row(6), row(0), float(r), None, ALU.is_equal), m_rank, m_slot, m_w)
        m1 = dv(partial(nc.vector.tensor_tensor, row(7), row(6), row(5), ALU.mult), m)
        m1 = dv(partial(nc.vector.tensor_reduce, tok(3 + r), row(7), AX, ALU.add), m1)
        slot_ready.append(dv(partial(nc.vector.tensor_copy, slot_i[:, r, :], tok(3 + r)), m1))
        m1 = dv(partial(nc.vector.tensor_tensor, row(7), row(6), row(4), ALU.mult), m, m1)
        w_ready = dv(partial(nc.vector.tensor_reduce, tok(5 + r), row(7), AX, ALU.add), m1)
        m_slot = w_ready
    block_no = sb("block_no", [P, BLOCKS, E1])
    block_e = sb("block_e", [P, BLOCKS])
    block_i = sb("block_i", [P, BLOCKS], I32)
    m_no = const(partial(nc.gpsimd.iota, block_no[:, :, :], [[1, BLOCKS], [0, E1]], base=0, channel_multiplier=0,
                                  allow_small_or_imprecise_dtypes=True))
    m = dv(partial(nc.vector.tensor_tensor, block_no[:, :, :], block_no[:, :, :],
                                     c(3).unsqueeze(1).broadcast_to([P, BLOCKS, E1]), ALU.is_ge), m_end, m_no)
    m = dv(partial(nc.vector.tensor_reduce, block_e[:, :], block_no[:, :, :], AX, ALU.add), m)
    m_be = dv(partial(nc.vector.tensor_scalar, block_e[:, :], block_e[:, :], E1 - 1.0, None, ALU.min), m)
    block_ready = dv(partial(nc.vector.tensor_copy, block_i[:, :], block_e[:, :]), m_be)

    scatter_sem = dma_sem("scatter_sem")
    PO.wait(zero_filled, xn_ready[-1], *slot_ready)
    for r in range(TOPK1):
        for t in range(NT):
            scattered = PO.load(scatter_sem, partial(nc.gpsimd.indirect_dma_start, 
                xs_dram[:, :], bass.IndirectOffsetOnAxis(ap=slot_i[:, r, t:t + 1].bitcast(U32), axis=0),
                xn1[:, t, :], None))

    bank = work_banks.grab()
    PE.wait(router_w, *bank.free)
    m = PE.mark(partial(nc.tensor.transpose, bank.t[:, 0:E1 * JH], b1_rows[:, :], ident[0:E1 * JH, 0:E1 * JH]))
    AC.wait(m)
    m_b1 = AC.mark(partial(nc.scalar.activation, b1T[:, :, :].rearrange("p e j -> p (e j)"), bank.t[:, 0:E1 * JH],
                                          ACT.Copy))
    bank.release(m_b1)
    expert_no = sb("expert_no", [P, E1])
    part_no = sb("part_no", [P, 1])
    const(partial(nc.gpsimd.iota, expert_no[:, :], [[1, E1]], base=0, channel_multiplier=0,
                           allow_small_or_imprecise_dtypes=True))
    no_ready = const(partial(nc.gpsimd.iota, part_no[:, :], [[0, 1]], base=0, channel_multiplier=1,
                                      allow_small_or_imprecise_dtypes=True))
    onehot = sb("onehot", [P, BLOCKS, E1])
    onehotT = sb("onehotT", [P, BLOCKS])
    m = dv(partial(nc.vector.tensor_tensor, onehot[:, :, :], expert_no[:, :].unsqueeze(1).broadcast_to([P, BLOCKS, E1]),
                                     block_e[:, :].unsqueeze(2).broadcast_to([P, BLOCKS, E1]), ALU.is_equal),
           m_be, no_ready)
    onehotT_ready = dv(partial(nc.vector.tensor_scalar, onehotT[:, :], block_e[:, :], part_no[:, 0:1], None,
                                                 ALU.is_equal), m_be, no_ready)
    b1_all = sb("b1_all", [P, BLOCKS, JH])
    b1_tmp = sb("b1_tmp", [P, BLOCKS, JH])
    m = dv(partial(nc.vector.tensor_tensor, 
        b1_all[:, :, :], onehot[:, :, 0:1].broadcast_to([P, BLOCKS, JH]),
        b1T[:, 0:1, :].broadcast_to([P, BLOCKS, JH]), ALU.mult), m, m_b1)
    for ex in range(1, E1):
        m = dv(partial(nc.vector.tensor_tensor, 
            b1_tmp[:, :, :], onehot[:, :, ex:ex + 1].broadcast_to([P, BLOCKS, JH]),
            b1T[:, ex:ex + 1, :].broadcast_to([P, BLOCKS, JH]), ALU.mult), m)
        m = dv(partial(nc.vector.tensor_tensor, b1_all[:, :, :], b1_all[:, :, :], b1_tmp[:, :, :], ALU.add), m)
    b1_ready = m

    W_AHEAD = W1S - 1
    for i, slot in enumerate(w2.slots):
        slot.sem = dma_sem(f"w_in{i}")
    xs_in = Ring(*[sb(f"xs_in{i}", [P, D]) for i in range(3)])
    for i, slot in enumerate(xs_in.slots):
        slot.sem = dma_sem(f"xs_in{i}")
    xsT = Ring(*[sb(f"xsT{i}", [P, KC, P]) for i in range(2)])
    hT = Ring(*[sb(f"hT{i}", [P, JH, P]) for i in range(2)])
    ysb = Ring(*[sb(f"ysb{i}", [P, D]) for i in range(2)])
    for i, slot in enumerate(ysb.slots):
        slot.sem = dma_sem(f"ysb{i}")
    last = [m for s in (*value_banks.slots, *work_banks.slots) for m in s.free]
    PE.wait(*last)
    AC.wait(*last)
    DV.wait(*last)
    h_banks = Ring(*[banks[i] for i in range(4)])
    y_banks = Ring(*banks[4:6])
    t_banks = Ring(*banks[6:8])
    weights = {}

    def load_weights(i):
        a1, a2 = w1.grab(), w2.grab()
        SP.wait(block_ready, *a1.free, *a2.free)

        def start():
            no = nc.sync.value_load(block_i[0:1, i:i + 1], min_val=0, max_val=E1 - 1)
            nc.sync.dma_start(a1.t[:, :, :], a["L1_ffn_W1"][bass.ds(no, 1)].rearrange("e (k p) n -> p (e k) n", p=P))\
                .then_inc(a2.sem.sem, 16)
            return nc.sync.dma_start(a2.t[:, :, :],
                               a["L1_ffn_W2"][bass.ds(no, 1)].rearrange("e (j p) n -> p (e j) n", p=P))
        a2.sem.total += 16
        weights[i] = (a1, a2, SP.load(a2.sem, start))

    xs_slots = {}

    def load_slots(i):
        s = xs_in.grab()
        SP.wait(scattered, *s.free)
        s.ready = SP.load(s.sem, partial(nc.sync.dma_start, s.t[:, :], xs_dram[i * P:i * P + P, :]))
        xs_slots[i] = s

    def up(i):
        s, xT, bank = xs_slots.pop(i), xsT.grab(), t_banks.grab()
        PE.wait(s.ready, *bank.free)
        for k in range(KC):
            tr = partial(nc.tensor.transpose, bank.t[:, k * P:k * P + P], s.t[:, k * P:k * P + P], ident[:, :])
            m = PE.mark(tr) if k else PE.put(tr)
        s.release(m)
        AC.wait(m, *xT.free)
        m = AC.mark(partial(nc.scalar.activation, xT.t[:, :, :].rearrange("p k s -> p (k s)"), bank.t[:, 0:KC * P],
                                           ACT.Copy))
        bank.release(m)
        xT.ready = m
        return xT

    def up2(i, xT):
        a1, _, w_ready_ = weights[i]
        hb, h = (h_banks.grab(), h_banks.grab()), hT.grab()
        for half in range(2):
            PE.wait(xT.ready, w_ready_, *hb[half].free)
            for j in range(half * JH // 2, (half + 1) * JH // 2):
                o = (j % (JH // 2)) * P
                for k in range(KC):
                    mm = partial(nc.tensor.matmul, 
                        hb[half].t[:, o:o + P], a1.t[:, k, j * P:j * P + P], xT.t[:, k, :], start=k == 0,
                        stop=k == KC - 1)
                    m = PE.mark(mm) if k == KC - 1 and j % (JH // 2) == JH // 2 - 1 else PE.put(mm)
            q = AC if half == 0 else DV
            q.wait(m, b1_ready, *h.free)
            for j in range(half * JH // 2, (half + 1) * JH // 2):
                o = (j % (JH // 2)) * P
                if q is AC:
                    mh = q.mark(partial(nc.scalar.activation, 
                        h.t[:, j, :], hb[half].t[:, o:o + P], ACT.Relu, bias=b1_all[:, i, j:j + 1]))
                else:
                    mh = q.mark(partial(nc.vector.tensor_scalar, 
                        h.t[:, j, :], hb[half].t[:, o:o + P], b1_all[:, i, j:j + 1], 0.0, ALU.add, ALU.max))
            hb[half].release(mh)
            h.ready = (h.ready if half else []) + [mh]
        xT.release(m)
        a1.release(m)
        return h

    ys_written = []

    def down(i, h):
        _, a2, w_ready_ = weights.pop(i)
        bank, y = y_banks.grab(), ysb.grab()
        PE.wait(onehotT_ready, router_w, w_ready_, *bank.free)
        PE.put(partial(nc.tensor.matmul, bank.t[:, 0:D], onehotT[0:E1, i:i + 1].broadcast_to([E1, P]), b2[:, :],
                                  start=True, stop=False))
        PE.wait(*h.ready)
        for j in range(JH):
            mm = partial(nc.tensor.matmul, bank.t[:, 0:D], h.t[:, j, :], a2.t[:, j, :], start=False,
                                         stop=j == JH - 1)
            m = PE.mark(mm) if j == JH - 1 else PE.put(mm)
        h.release(m)
        a2.release(m)
        DV.wait(m, *y.free)
        m = DV.mark(partial(nc.vector.tensor_copy, y.t[:, :], bank.t[:, 0:D]))
        bank.release(m)
        SP.wait(m)
        m = SP.load(y.sem, partial(nc.sync.dma_start, ys_dram[i * P:i * P + P, :], y.t[:, :]))
        y.release(m)
        ys_written.append(m)

    for i in range(W_AHEAD):
        load_weights(i)
    for i in range(2):
        load_slots(i)
    xTs = {0: up(0)}
    held = None
    for i in range(BLOCKS):
        if i + 2 < BLOCKS:
            load_slots(i + 2)
        if i + 1 < BLOCKS:
            xTs[i + 1] = up(i + 1)
        h = up2(i, xTs.pop(i))
        if held is not None:
            down(*held)
        if i + W_AHEAD < BLOCKS:
            load_weights(i + W_AHEAD)
        held = (i, h)
    down(*held)

    picked = Ring(*[sb(f"picked{i}", [P, TOPK1, D]) for i in range(4)])
    for i, slot in enumerate(picked.slots):
        slot.sem = dma_sem(f"picked{i}")
    out_sem = dma_sem("out_sem")
    PO.wait(*ys_written[-2:])
    for t in range(NT):
        g = picked.grab()
        PO.wait(*g.free)
        for r in range(TOPK1):
            m = PO.load(g.sem, partial(nc.gpsimd.indirect_dma_start, 
                g.t[:, r, :], None, ys_dram[:, :],
                bass.IndirectOffsetOnAxis(ap=slot_i[:, r, t:t + 1].bitcast(U32), axis=0)))
        for r in range(TOPK1):
            m = dv(partial(nc.vector.scalar_tensor_tensor, 
                x[:, t, :], g.t[:, r, :], small[:, 5 + r, t:t + 1], x[:, t, :], ALU.mult, ALU.add), m, w_ready)
        g.release(m)
        SP.wait(m)
        done = SP.load(out_sem, partial(nc.sync.dma_start, 
            out[t // TT, (t % TT) * P:(t % TT) * P + P, :], x[:, t, :]))
    SP.wait(done)

    block = es.enter_context(nc.Block())

    @block.sync
    def _(_engine):
        SP.play()

    @block.tensor
    def _(_engine):
        PE.play()

    @block.vector
    def _(_engine):
        DV.play()

    @block.scalar
    def _(_engine):
        AC.play()

    @block.gpsimd
    def _(_engine):
        PO.play()

    es.close()


def kernel(**inputs):
    import numpy as np
    import concourse.bacc as bacc
    from concourse.bass_utils import run_bass_kernel_spmd

    nc = bacc.Bacc("TRN2", target_bir_lowering=False, num_devices=1)
    arrays, aps = {}, {}
    for name, value in inputs.items():
        v = np.ascontiguousarray(value)
        arrays[f"in_{name}"] = v
        aps[name] = nc.dram_tensor(f"in_{name}", v.shape, mybir.dt.from_np(v.dtype), kind="ExternalInput").ap()
    out = nc.dram_tensor("out_x", (NB, S, D), F32, kind="ExternalOutput").ap()
    build(nc, aps, out)
    r = run_bass_kernel_spmd(nc, [arrays], core_ids=[0])
    return r.results[0]["out_x"]
```

```python
from contextlib import ExitStack
from functools import partial
from math import prod

import concourse.bass as bass
from concourse import mybir

F32 = mybir.dt.float32
F32R = mybir.dt.float32r
I32 = mybir.dt.int32
BF16 = mybir.dt.bfloat16
U32 = mybir.dt.uint32
ALU = mybir.AluOpType
ACT = mybir.ActivationFunctionType
AX = mybir.AxisListType.X

P = 128
LOG_P = 7
NB, S, D = 8, 256, 256
CTX = 192
H, HD = 16, 16
TT = S // P
NT = NB * TT
KC = D // P
E0, I0 = 8, 128
NG, TKG, TOPK0 = 4, 2, 4
E1, H1, TOPK1 = 8, 1024, 2
JH = H1 // P
BLOCKS = NB * S * TOPK1 // P + E1 - 1
CLAMP = 10000.0
EPS = 1e-5
QSCALE = HD ** -0.5
NEG_INF = -1e9

STACK = 4 * HD
FULL = 96
ROWS = FULL + 2


PE_COLUMN = 0.42
PASSES = 4
PE_STRIP = 32
DVE_NS, DVE_COLUMN = 60, 1.04
ACT_NS, ACT_COLUMN = 50, 0.83
POOL_NS, POOL_COLUMN = 100, 1.3
SP_NS, SP_COLUMN = 60, 0.0
SIGNAL_NS = 150
DMA_START, DMA_END, DMA_BYTE = 1400, 900, 1 / 360


def columns(fn):
    return max((prod(v.shape[1:]) for v in (*fn.args, *fn.keywords.values()) if isinstance(v, bass.AP)), default=0)


class Queue:

    due = {}
    dma_free = 0.0

    def __init__(self, eng, sem, fixed, per_column):
        self.eng, self.sem, self.ops, self.count, self.seen = eng, sem, [], 0, {}
        self.fixed, self.per_column, self.now = fixed, per_column, 0.0

    def wait(self, *marks):
        for mark in marks:
            if mark is None:
                continue
            sem, value = mark
            if self.seen.get(sem.name, 0) < value:
                self.seen[sem.name] = value
                self.ops.append(partial(self.eng.wait_ge, sem, value))
                self.now = max(self.now, when([mark]))

    def put(self, fn):
        self.ops.append(fn)
        self.now += self.cost(fn)

    def cost(self, fn):
        return self.fixed + self.per_column * columns(fn)

    def mark(self, fn):
        self.count += 1
        self.ops.append(lambda: fn().then_inc(self.sem, 1))
        self.now += self.cost(fn)
        self.due[self.sem.name, self.count] = self.now + SIGNAL_NS
        return (self.sem, self.count)

    def load(self, sem, fn):
        sem.total += 16
        self.ops.append(lambda: fn().then_inc(sem.sem, 16))
        self.now += self.fixed
        start = max(self.now + DMA_START, Queue.dma_free)
        ap = fn.args[0] if isinstance(fn, partial) else None
        Queue.dma_free = start + DMA_BYTE * (4 * prod(ap.shape) if ap is not None and isinstance(ap, bass.AP) else 0)
        self.due[sem.sem.name, sem.total] = Queue.dma_free + DMA_END
        return (sem.sem, sem.total)

    def play(self):
        for op in self.ops:
            op()


class TensorQueue(Queue):

    def cost(self, fn):
        out, weights = fn.args[0:2]
        n = prod(out.shape[1:]) * (PASSES if weights.dtype == F32 else 1)
        return self.fixed + self.per_column * n * (out.shape[0] / P if out.shape[0] == PE_STRIP else 1)


def when(marks):
    return max((Queue.due.get((m[0].name, m[1]), 0.0) for m in marks if m), default=0.0)


class DmaSem:
    def __init__(self, sem):
        self.sem, self.total = sem, 0


class Slot:

    def __init__(self, t):
        self.t, self.free, self.held, self.ready = t, [], False, None

    def release(self, *marks):
        self.free, self.held = list(marks), False


BUSY = "busy"


class Ring:

    def __init__(self, *tensors):
        self.slots = [Slot(t) for t in tensors]

    def take(self):
        while all(s.held for s in self.slots):
            yield BUSY
        slot = min((s for s in self.slots if not s.held), key=lambda s: when(s.free))
        slot.held = True
        return slot

    def grab(self):
        slot = min((s for s in self.slots if not s.held), key=lambda s: when(s.free))
        slot.held = True
        return slot


def weave(stages, clock):
    turn = {n: 0.0 for n in range(len(stages))}
    busy = set()
    while turn:
        n = min((n for n in turn if n not in busy), key=lambda n: max(turn[n], clock.now))
        marks = next(stages[n], None)
        if marks == BUSY:
            busy.add(n)
            continue
        if marks is None:
            del turn[n]
        else:
            turn[n] = when(marks)
        busy.clear()


def build(nc, a, out):
    es = ExitStack()
    tens = ExitStack()

    def sem(name):
        return es.enter_context(nc.semaphore(name))

    def sb(name, shape, dt=F32, scope=None):
        return (scope or es).enter_context(nc.sbuf_tensor(name, shape, dt))

    def dma_sem(name):
        return DmaSem(sem(name))

    PE = TensorQueue(nc.tensor, sem("pe_done"), 0, PE_COLUMN)
    DV = Queue(nc.vector, sem("dve_done"), DVE_NS, DVE_COLUMN)
    AC = Queue(nc.scalar, sem("act_done"), ACT_NS, ACT_COLUMN)
    PO = Queue(nc.gpsimd, sem("pool_done"), POOL_NS, POOL_COLUMN)
    SP = Queue(nc.sync, sem("sp_done"), SP_NS, SP_COLUMN)

    qk_dram = [nc.dram_tensor(f"qk_{l}", (NB, 4, D, S), F32).ap() for l in range(2)]
    max_dram = [nc.dram_tensor(f"max_{l}", (NB, 3 * H * TT, P), F32).ap() for l in range(2)]
    ctxT_dram = nc.dram_tensor("ctx_t", (NB, 2, P, S), F32).ap()
    z_dram = nc.dram_tensor("z_rows", (NB, S, D), F32).ap()
    vmean_dram = nc.dram_tensor("vmean", (NB, D), F32).ap()
    zalt_dram = nc.dram_tensor("zalt_rows", (NB, D), F32).ap()
    xn1_dram = nc.dram_tensor("rows1", (NB * S + P, D + E1), F32).ap()

    banks = [es.enter_context(nc.psum_tensor(f"bank{i}", [P, 512], F32)) for i in range(8)]
    value_banks = Ring(banks[0])
    work_banks = Ring(*banks[1:8])

    x = sb("x", [P, NT, D])
    ident = sb("ident", [P, P])
    ones = sb("ones", [P, P])
    tg = sb("tg", [P, 4])
    zero_row = sb("zero_row", [P, D + E1])
    g_raw = sb("g_raw", [P, 4])
    norm_small = Ring(*[(sb(f"stats{i}", [P, TT, 6]), sb(f"moments{i}", [P, TT, 2]), sb(f"rstd{i}", [P, 4, TT]))
                        for i in range(3)])
    minus_half = sb("minus_half", [P, TT])
    before = sb("before", [P, 8, 8])
    after = sb("after", [P, 8, 8])
    keep_row = sb("keep_row", [P, 1], I32)
    mask = sb("mask", [P, NT, E1], BF16)
    picks = sb("picks", [P, TOPK1, NT, E1])
    tri = sb("tri", [P, P], BF16)
    ones_bf = sb("ones_bf", [P, P], BF16)
    steps = sb("steps", [P, E1, NB * S // P])
    block_no = sb("block_no", [P, BLOCKS, E1])
    block_row = sb("block_row", [P, BLOCKS])
    place_row = sb("place_row", [P, P])
    expert_row = sb("expert_row", [P, E1])
    part_no = sb("part_no", [P, 1])
    spare_row = sb("spare_row", [P, 1])
    tile_start = sb("tile_start", [P, TOPK1 * NT])
    row_no = sb("row_no", [P, 1])
    x_ready = [None] * NB

    wait_const = []

    def const(fn):
        PO.wait(*wait_const[-1:])
        m = PO.mark(fn)
        wait_const.append(m)
        return m

    const(partial(nc.gpsimd.memset, ident[:, :], 0.0))
    ident_ready = const(partial(nc.gpsimd.affine_select, out=ident[:, :], in_=ident[:, :], compare_op=ALU.not_equal,
                                                  fill=1.0, base=0, pattern=[[-1, P]], channel_multiplier=1))
    const(partial(nc.gpsimd.memset, ones[:, :], 1.0))
    zero_ready = const(partial(nc.gpsimd.memset, zero_row[:, :], 0.0))

    gates_in = dma_sem("gates_in")
    SP.load(gates_in, partial(nc.sync.dma_start, g_raw[:, 0:2], a["g_xattn"].partition_broadcast(P)))
    m = SP.load(gates_in, partial(nc.sync.dma_start, g_raw[:, 2:4], a["g_ffn"].partition_broadcast(P)))
    AC.wait(m)
    tg_ready = AC.mark(partial(nc.scalar.activation, tg[:, :], g_raw[:, :], ACT.Tanh))

    A = tens

    def sba(name, shape, dt=F32):
        return sb(name, shape, dt, A)

    x_in = [dma_sem(f"x_in{b}") for b in range(NB)]

    def load_x(b):
        m = SP.load(x_in[b], partial(nc.sync.dma_start, 
            x[:, TT * b:TT * b + TT, :], a["x"][b].rearrange("(t p) d -> p t d", p=P)))
        x_ready[b] = m

    ctx_tok = Ring(*[sba(f"ctx_tok{i}", [P, TT, CTX]) for i in range(2)])
    for i, slot in enumerate(ctx_tok.slots):
        slot.sem = dma_sem(f"ctx_in{i}")

    wq = [sba(f"wq{l}", [P, KC, D]) for l in range(2)]
    wkv = [sba(f"wkv{l}", [P, 2, 2 * D]) for l in range(2)]
    wo = [sba(f"wo{l}", [P, KC, D]) for l in range(2)]
    qkb = [sba(f"qkb{l}", [P, 2, KC]) for l in range(2)]
    vb = [sba(f"vb{l}", [P, D]) for l in range(2)]
    ob = [sba(f"ob{l}", [P, D]) for l in range(2)]
    attn_w_in = [dma_sem(f"attn_w_in{l}") for l in range(2)]
    attn_w_loaded, attn_w_ready = [None, None], [None, None]

    def load_attention_weights(l):
        if l == 0:
            q_w, q_b, o_w, o_b = a["L0_xattn_q_w"], a["L0_xattn_q_b"], a["L0_xattn_proj_w"], a["L0_xattn_proj_b"]
            k_w, v_w = a["L0_xattn_kv_w"][:, 0:D], a["L0_xattn_kv_w"][:, D:2 * D]
            k_b, v_b = a["L0_xattn_kv_b"][0:D], a["L0_xattn_kv_b"][D:2 * D]
        else:
            q_w, q_b, o_w, o_b = a["L1_xattn_Wq"], a["L1_xattn_bq"], a["L1_xattn_Wo"], a["L1_xattn_bo"]
            k_w, v_w, k_b, v_b = a["L1_xattn_Wk"], a["L1_xattn_Wv"], a["L1_xattn_bk"], a["L1_xattn_bv"]
        q_col, k_col = q_b.rearrange("(k p) -> p k", p=P), k_b.rearrange("(k p) -> p k", p=P)
        for dst, src in (
            (wq[l][:, :, :], q_w.rearrange("(k p) n -> p k n", p=P)),
            (qkb[l][:, 0, :], q_col),
            (qkb[l][:, 1, :], k_col),
            (wkv[l][:, 0, 0:D], k_w[0:P, :]),
            (wkv[l][0:CTX - P, 1, 0:D], k_w[P:CTX, :]),
            (wkv[l][:, 0, D:2 * D], v_w[0:P, :]),
            (wkv[l][0:CTX - P, 1, D:2 * D], v_w[P:CTX, :]),
            (vb[l][:, :], v_b.partition_broadcast(P)),
            (wo[l][:, :, :], o_w.rearrange("(k p) n -> p k n", p=P)),
            (ob[l][:, :], o_b.partition_broadcast(P)),
        ):
            columns = src is q_col or src is k_col
            m = SP.load(attn_w_in[l], partial(nc.sync.dma_start, 
                dst, src, allow_slow_non_contiguous=columns))
        attn_w_loaded[l] = m

    def scale_queries(l):
        DV.wait(attn_w_loaded[l])
        DV.mark(partial(nc.vector.tensor_scalar, qkb[l][:, 0, :], qkb[l][:, 0, :], QSCALE, None, ALU.mult))
        attn_w_ready[l] = DV.mark(partial(nc.vector.tensor_scalar, wq[l][:, :, :], wq[l][:, :, :], QSCALE, None, ALU.mult))

    def load_ctx(b):
        slot = yield from ctx_tok.take()
        SP.wait(*slot.free)
        slot.ready = SP.load(slot.sem, partial(nc.sync.dma_start, 
            slot.t[:, :, :], a["ctx_768"][b].rearrange("(t p) d -> p t d", p=P)))
        return slot

    load_x(0)
    load_attention_weights(0)

    w_gate0 = sba("w_gate0", [P, KC, E0 + 1, I0])
    w_up0 = sba("w_up0", [P, KC, E0 + 1, I0])
    w_down0 = sba("w_down0", [P, E0 + 1, D])
    gate_rows = sba("gate_rows", [E0, D])
    gate_wT = sba("gate_wT", [P, KC, E0])
    corr = sba("corr", [P, E0])
    ffn0_in = dma_sem("ffn0_in")
    ffn0_w = None
    loads0 = [(gate_rows[:, :], a["L0_ffn_gate_w"]),
              (corr[:, :], a["L0_ffn_correction_bias"].partition_broadcast(P))]
    for k in range(KC):
        rows = slice(k * P, k * P + P)
        for t, w, shared in ((w_gate0, a["L0_ffn_Wg"], a["L0_ffn_Wg_s"]), (w_up0, a["L0_ffn_Wu"], a["L0_ffn_Wu_s"])):
            loads0.append((t[:, k, 0:E0, :], w[:, rows, :].rearrange("e p i -> p e i")))
            loads0.append((t[:, k, E0, :], shared[rows, :]))
    loads0.append((w_down0[:, 0:E0, :], a["L0_ffn_Wd"].rearrange("e i d -> i e d")))
    loads0.append((w_down0[:, E0, :], a["L0_ffn_Wd_s"]))

    def load_experts0():
        nonlocal ffn0_w
        for dst, src in loads0:
            ffn0_w = SP.load(ffn0_in, partial(nc.sync.dma_start, dst, src))

    stack_q = [Slot(sba(f"stack_q{l}", [ROWS, H, S], F32R)) for l in range(2)]
    stack_k = [Slot(sba(f"stack_k{l}", [ROWS, H, S], F32R)) for l in range(2)]
    values = [Slot(sba(f"values{l}", [P, 2, H, 2 * HD])) for l in range(2)]
    xn = Ring(*[sba(f"xn{i}", [P, TT, D]) for i in range(2)])
    xnT = Ring(*[sba(f"xnT{i}", [P, KC, S]) for i in range(3)])
    ctxT = Ring(*[sba(f"ctxT{i}", [P, 2, S]) for i in range(2)])
    for i, slot in enumerate(ctxT.slots):
        slot.sem = dma_sem(f"ctxT_in{i}")
    split = Ring(*[(sba(f"hi{i}", [P, KC, S], F32R), sba(f"lo{i}", [P, KC, S], F32R)) for i in range(2)])
    rowmax = Ring(*[sba(f"rowmax{i}", [P, H, TT]) for i in range(2)])
    shift = Ring(sba("shift", [P, 3, H * TT]))
    shiftT = Ring(sba("shiftT", [3 * H * TT, P]))
    clipped = Ring(*[sba(f"clipped{i}", [P, 2, S]) for i in range(2)])
    LB_HEADS = 2
    lower = Ring(*[sba(f"lower{i}", [P, LB_HEADS, S]) for i in range(2)])
    for i, slot in enumerate(lower.slots):
        slot.sem = dma_sem(f"lower_in{i}")
    probs = Ring(*[sba(f"probs{i}", [P, 2, S]) for i in range(3)])
    weighted = Ring(sba("weighted", [P, 2, S]))
    recip = Ring(sba("recip", [P, TT, 8]))
    attn = Ring(sba("attn", [P, TT, D]))
    attnT = Ring(sba("attnT", [P, KC, S]))
    summed = Ring(*[sba(f"summed{i}", [P, TT, D]) for i in range(1)])
    attending = Ring(None)
    nan_sum = sba("nan_sum", [P, 2 * NB])
    vmean_row = Slot(sba("vmean_row", [1, D]))
    inv_s = sba("inv_s", [P, 32])

    half_ready = const(partial(nc.gpsimd.memset, minus_half[:, :], -0.5))
    inv_ready = const(partial(nc.gpsimd.memset, inv_s[:, :], 1.0 / S))
    stacks_ready = []
    for l in range(2):
        fills = (stack_q[l].t[STACK:FULL, :, :], 0.0), (stack_k[l].t[STACK:ROWS, :, :], 1.0)
        for t, value in fills:
            fill = partial((nc.vector if l == 0 else nc.gpsimd).memset, t.bitcast(F32), value)
            m = DV.mark(fill) if l == 0 else const(fill)
        stacks_ready.append(m)
    values_ready = [DV.mark(partial(nc.vector.memset, values[l].t[:, :, :, HD:2 * HD], 1.0)) for l in range(2)]

    scale_queries(0)

    hidden0 = Ring(*[sba(f"hidden0_{i}", [P, S]) for i in range(3)])
    cw_sel_f = sba("cw_sel_f", [2 * E0, E0])
    cw_sel = sba("cw_sel", [2 * E0, E0], F32R)
    const(partial(nc.gpsimd.memset, cw_sel_f[:, :], 0.0))
    for half in range(2):
        m = const(partial(nc.gpsimd.affine_select, out=cw_sel_f[:, :], in_=cw_sel_f[:, :], compare_op=ALU.not_equal,
                          fill=1.0, base=-half * E0, pattern=[[-1, E0]], channel_multiplier=1))
    DV.wait(m)
    cw_sel_ready = DV.mark(partial(nc.vector.tensor_copy, cw_sel[:, :], cw_sel_f[:, :]))
    const(partial(nc.gpsimd.memset, before[:, :, :], 1.0))
    const(partial(nc.gpsimd.affine_select, out=before[:, :, :], in_=before[:, :, :], compare_op=ALU.is_gt, fill=0.0,
                                    base=0, pattern=[[1, 8], [-1, 8]], channel_multiplier=0))
    const(partial(nc.gpsimd.memset, after[:, :, :], 1.0))
    order_ready = const(partial(nc.gpsimd.affine_select, out=after[:, :, :], in_=after[:, :, :], compare_op=ALU.is_gt,
                                                  fill=0.0, base=0, pattern=[[-1, 8], [1, 8]],
                                                  channel_multiplier=0))

    const(partial(nc.gpsimd.memset, tri[:, :], 1.0))
    const(partial(nc.gpsimd.affine_select, out=tri[:, :], in_=tri[:, :], compare_op=ALU.is_gt, fill=0.0,
                  base=0, pattern=[[1, P]], channel_multiplier=-1))
    tri_ready = const(partial(nc.gpsimd.memset, ones_bf[:, :], 1.0))
    for t, pattern, base, by_partition in (
        (steps[:, :, :], [[0, E1], [P, NB * S // P]], 0, 0),
        (block_no[:, :, :], [[1, BLOCKS], [0, E1]], 0, 0),
        (block_row[:, :], [[1, BLOCKS]], 0, 0),
        (place_row[:, :], [[1, P]], 0, 0),
        (expert_row[:, :], [[1, E1]], 0, 0),
        (part_no[:, :], [[0, 1]], 0, 1),
        (spare_row[:, :], [[0, 1]], NB * S + 1, 1),
        (tile_start[:, :], [[0, TOPK1], [P, NT]], 0, 0),
        (row_no[:, :], [[0, 1]], 1, 1),
    ):
        no_ready = const(partial(nc.gpsimd.iota, t, pattern, base=base, channel_multiplier=by_partition,
                                 allow_small_or_imprecise_dtypes=True))

    def dv(fn, *waits):
        DV.wait(*waits)
        return DV.mark(fn)

    finished = set()

    def until(*names):
        while not finished.issuperset(names):
            yield BUSY

    def layer_norm(b, slot_n, slot_t):
        yield [x_ready[b]]
        s = yield from norm_small.take()
        stats, moments, r = s.t
        DV.wait(*s.free, x_ready[b])
        for t in range(TT):
            m = DV.mark(partial(nc.vector.bn_stats, stats[:, t, :], x[:, TT * b + t, :]))
        DV.wait(m)
        for t in range(TT):
            m_mom = DV.mark(partial(nc.vector.bn_aggr, moments[:, t, :], stats[:, t, :]))
        PO.wait(m_mom, half_ready)
        m = PO.mark(partial(nc.gpsimd.tensor_scalar, r[:, 0, :], moments[:, :, 1], EPS, None, ALU.add))
        for fn in (
            partial(nc.gpsimd.tensor_tensor, r[:, 1, :], r[:, 0, :], minus_half[:, :], ALU.pow),
            partial(nc.gpsimd.tensor_tensor, r[:, 2, :], r[:, 1, :], r[:, 1, :], ALU.mult),
            partial(nc.gpsimd.tensor_tensor, r[:, 2, :], r[:, 2, :], r[:, 0, :], ALU.mult),
            partial(nc.gpsimd.tensor_scalar, r[:, 2, :], r[:, 2, :], -0.5, 1.5, ALU.mult, ALU.add),
            partial(nc.gpsimd.tensor_tensor, r[:, 3, :], r[:, 1, :], r[:, 2, :], ALU.mult),
        ):
            PO.wait(m)
            m = PO.mark(fn)
        yield [m, *slot_n.free]
        DV.wait(m, *slot_n.free)
        for t in range(TT):
            m_n = DV.mark(partial(nc.vector.tensor_scalar,
                slot_n.t[:, t, :], x[:, TT * b + t, :], moments[:, t, 0:1], r[:, 3, t:t + 1],
                ALU.subtract, ALU.mult))
        s.release(m_n)
        slot_n.ready = m_n
        yield [m_n]
        bank = yield from work_banks.take()
        PE.wait(m_n, ident_ready, *bank.free)
        for k in range(KC):
            for t in range(TT):
                o = k * S + t * P
                tr = partial(nc.tensor.transpose,
                    bank.t[:, o:o + P], slot_n.t[:, t, k * P:k * P + P], ident[:, :])
                m = PE.mark(tr) if (k, t) == (KC - 1, TT - 1) else PE.put(tr)
        slot_n.release(m)
        yield [m, *slot_t.free]
        AC.wait(m, *slot_t.free)
        slot_t.ready = AC.mark(partial(nc.scalar.activation,
            slot_t.t[:, :, :].rearrange("p k s -> p (k s)"), bank.t[:, :], ACT.Copy))
        bank.release(slot_t.ready)

    hilo_out = [[dma_sem(f"hilo_out{l}{w}") for w in range(2)] for l in range(2)]
    stack_in = [[dma_sem(f"stack_in{l}{w}") for w in range(2)] for l in range(2)]
    ctxT_out = [dma_sem(f"ctxT_out{i}") for i in range(NB)]
    shift_out = [dma_sem(f"shift_out{l}") for l in range(2)]
    shift_in = [dma_sem(f"shift_in{l}") for l in range(2)]
    z_out = [dma_sem(f"z_out{i}") for i in range(NB)]
    vmean_out = dma_sem("vmean_out")
    ctxT_stored = [None] * NB
    z_stored = [None] * NB
    vmean_stored = [None] * NB
    nan_marks = []
    shifts_ready = {}
    lower_written = {}

    def context(b, l):
        cT = yield from ctxT.take()
        if l == 0:
            slot = yield from load_ctx(b)
            yield [slot.ready]
            bank = yield from work_banks.take()
            PE.wait(slot.ready, ident_ready, *bank.free)
            for t in range(TT):
                PE.put(partial(nc.tensor.transpose, bank.t[:, t * P:t * P + P], slot.t[:, t, 0:P], ident[:, :]))
            for t in range(TT):
                tr = partial(nc.tensor.transpose, bank.t[0:CTX - P, S + t * P:S + t * P + P],
                                                slot.t[:, t, P:CTX], ident[:, :])
                m = PE.mark(tr) if t == TT - 1 else PE.put(tr)
            slot.release(m)
            yield [m, *cT.free]
            AC.wait(m, *cT.free)
            AC.mark(partial(nc.scalar.activation, cT.t[:, 0, :], bank.t[:, 0:S], ACT.Copy))
            cT.ready = AC.mark(partial(nc.scalar.activation, cT.t[0:CTX - P, 1, :], bank.t[0:CTX - P, S:2 * S], ACT.Copy))
            bank.release(cT.ready)
            yield [cT.ready]
            SP.wait(cT.ready)
            SP.load(ctxT_out[b], partial(nc.sync.dma_start, ctxT_dram[b, 0], cT.t[:, 0, :]))
            ctxT_stored[b] = SP.load(ctxT_out[b], partial(nc.sync.dma_start,
                ctxT_dram[b, 1, 0:CTX - P], cT.t[0:CTX - P, 1, :]))
        else:
            yield [ctxT_stored[b], *cT.free]
            SP.wait(ctxT_stored[b], *cT.free)
            SP.load(cT.sem, partial(nc.sync.dma_start, cT.t[:, 0, :], ctxT_dram[b, 0]))
            cT.ready = SP.load(cT.sem, partial(nc.sync.dma_start,
                cT.t[0:CTX - P, 1, :], ctxT_dram[b, 1, 0:CTX - P]))
        return cT

    CTX_CHUNKS = ((0, P), (1, CTX - P))

    def hi_lo(b, l, which, source, weights, rows):
        yield [source.ready, attn_w_ready[l]]
        bank = yield from work_banks.take()
        PE.wait(source.ready, attn_w_ready[l], *bank.free)
        for mt in range(KC):
            for n, (k, r) in enumerate(rows):
                mm = partial(nc.tensor.matmul,
                    bank.t[:, mt * S:mt * S + S], weights[0:r, k, mt * P:mt * P + P], source.t[0:r, k, :],
                    start=n == 0, stop=n == len(rows) - 1)
                m_mm = PE.mark(mm) if mt == KC - 1 and n == len(rows) - 1 else PE.put(mm)
        if which == 0:
            source.release(m_mm)
        else:
            finished.add(("k product", b, l))
        s = yield from split.take()
        hs, ls = s.t
        yield [m_mm, *s.free]
        AC.wait(m_mm, *s.free)
        for mt in range(KC):
            m_h = AC.mark(partial(nc.scalar.activation, hs[:, mt, :], bank.t[:, mt * S:mt * S + S], ACT.Identity,
                                  bias=qkb[l][:, which, mt:mt + 1]))
        yield [m_h]
        DV.wait(m_h, *s.free)
        for mt in range(KC):
            m_l = DV.mark(partial(nc.vector.scalar_tensor_tensor, ls[:, mt, :], bank.t[:, mt * S:mt * S + S],
                                  qkb[l][:, which, mt:mt + 1], hs[:, mt, :].bitcast(F32), ALU.add, ALU.subtract))
        bank.release(m_l)
        yield [m_l]
        dram = qk_dram[l][b]
        SP.wait(m_h, m_l)
        for part, t in enumerate((hs, ls)):
            m_out = SP.load(hilo_out[l][which], partial(nc.sync.dma_start,
                dram[2 * which + part].rearrange("(k p) s -> p k s", p=P), t[:, :, :].bitcast(F32)))
        m_nan = None
        if l == 1:
            scratch = yield from clipped.take()
            lo_flat = ls[:, :, :].bitcast(F32).rearrange("p k s -> p (k s)")
            AC.wait(m_l, *scratch.free)
            m_nan = AC.mark(partial(nc.scalar.activation, scratch.t[:, :, :].rearrange("p k s -> p (k s)"), lo_flat,
                                    ACT.Copy, accum_out=nan_sum[:, 2 * b + which:2 * b + which + 1]))
            scratch.release(m_nan)
            nan_marks.append(m_nan)
        s.release(m_out, m_nan)
        dst = (stack_q if which == 0 else stack_k)[l]
        if b:
            yield from until(("attend", b - 1, l))
        yield [m_out, *dst.free]
        SP.wait(m_out, stacks_ready[l], *dst.free)
        for blk in range(STACK // HD):
            part = (blk // 2) if which == 0 else (blk % 2)
            src = dram[2 * which + part].rearrange("(h d) s -> d h s", d=HD)
            finished.add(("stacking", which, b, l))
            dst.ready = SP.load(stack_in[l][which], partial(nc.sync.dma_start,
                dst.t[blk * HD:blk * HD + HD, :, :].bitcast(F32), src))

    contexts = {}

    def keys(b, l):
        yield from until(*([("keys", b - 1, l)] if b else []), *([("output", b, 0), "weights 1"] if l == 1 else []))
        cT = contexts[b, l] = yield from context(b, l)
        finished.add(("context", b, l))
        yield from hi_lo(b, l, 1, cT, wkv[l], CTX_CHUNKS)
        finished.add(("keys", b, l))

    def queries(b, l):
        yield from until(*([("queries", b - 1, l)] if b else []), *([("experts0", b), "weights 1"] if l == 1 else []))
        if l == 0 and b + 1 < NB:
            load_x(b + 1)
        slot_n = yield from xn.take()
        xT = yield from xnT.take()
        yield from layer_norm(b, slot_n, xT)
        yield from hi_lo(b, l, 0, xT, wq[l], ((0, P), (1, P)))
        finished.add(("queries", b, l))

    def value_rows(b, l):
        yield from until(("k product", b, l), *([("value rows", b - 1, l)] if b else []))
        cT = contexts[b, l]
        bank = yield from work_banks.take()
        PE.wait(cT.ready, attn_w_ready[l], *bank.free)
        for kt in range(2):
            for k, r in CTX_CHUNKS:
                mm = partial(nc.tensor.matmul,
                    bank.t[:, kt * D:kt * D + D], cT.t[0:r, k, kt * P:kt * P + P], wkv[l][0:r, k, D:2 * D],
                    start=k == 0, stop=k == 1)
                m = PE.mark(mm) if (kt, k) == (1, 1) else PE.put(mm)
        cT.release(m, ctxT_stored[b] if l == 0 else None)
        if b:
            yield from until(("attend", b - 1, l))
        v = values[l]
        yield [m, *v.free]
        DV.wait(values_ready[l], m, attn_w_ready[l], *v.free)
        v.ready = DV.mark(partial(nc.vector.tensor_tensor,
            v.t[:, :, :, 0:HD], bank.t[:, :].rearrange("p (k h d) -> p k h d", k=2, d=HD),
            vb[l][:, :].rearrange("p (h d) -> p h d", d=HD).unsqueeze(1).broadcast_to([P, 2, H, HD]), ALU.add))
        bank.release(v.ready)
        finished.add(("value rows", b, l))
        if l == 1:
            yield [v.ready]
            bank = yield from work_banks.take()
            PE.wait(v.ready, inv_ready, *bank.free)
            for kt in range(2):
                mm = partial(nc.tensor.matmul, bank.t[0:32, 0:D].rearrange("p (h d) -> p h d", d=HD),
                                               inv_s[:, :], v.t[:, kt, :, 0:HD], start=kt == 0, stop=kt == 1)
                m = PE.mark(mm) if kt else PE.put(mm)
            finished.add(("mean", b))
            yield [m, *vmean_row.free]
            AC.wait(m, *vmean_row.free)
            m = AC.mark(partial(nc.scalar.activation, vmean_row.t[0:1, :], bank.t[0:1, 0:D], ACT.Copy))
            bank.release(m)
            yield [m]
            SP.wait(m)
            vmean_stored[b] = SP.load(vmean_out, partial(nc.sync.dma_start, vmean_dram[b:b + 1, :], vmean_row.t[0:1, :]))
            vmean_row.free = [vmean_stored[b]]

    def maxima(b, l):
        yield from until(("keys", b, l), ("queries", b, l))
        sq, sk = stack_q[l], stack_k[l]
        mx = yield from rowmax.take()
        before_last = None
        for h in range(H + 1):
            yield [sq.ready, sk.ready]
            if h < H:
                bank = yield from work_banks.take()
                PE.wait(sq.ready, sk.ready, *bank.free)
                for t in range(TT):
                    mm = partial(nc.tensor.matmul, bank.t[:, t * S:t * S + S], sq.t[0:FULL, h, t * P:t * P + P],
                                                      sk.t[0:FULL, h, :], start=True, stop=True)
                    m = PE.mark(mm) if t == TT - 1 else PE.put(mm)
            if h:
                last_bank, last_m = before_last
                DV.wait(last_m, *mx.free)
                m_max = DV.mark(partial(nc.vector.tensor_reduce,
                    mx.t[:, h - 1, :], last_bank.t[:, :].rearrange("p (t s) -> p t s", t=TT), AX, ALU.max))
                last_bank.release(m_max)
            before_last = (bank, m)
        flat = mx.t[:, :, :].rearrange("p h t -> p (h t)")
        if l == 1:
            m_max = dv(partial(nc.vector.tensor_scalar, flat, flat, CLAMP, -CLAMP, ALU.min, ALU.max), m_max)
        sh = yield from shift.take()
        DV.wait(m_max, *sh.free)
        m_h = DV.mark(partial(nc.vector.tensor_scalar, sh.t[:, 0, :].bitcast(F32R), flat, -1.0, None, ALU.mult))
        m_b = DV.mark(partial(nc.vector.tensor_scalar, sh.t[:, 2, :], flat, -1.0, -CLAMP, ALU.mult, ALU.add))
        m_l = dv(partial(nc.vector.scalar_tensor_tensor, sh.t[:, 1, :].bitcast(F32R), flat, -1.0, sh.t[:, 0, :],
                                                  ALU.mult, ALU.subtract), m_h)
        mx.release(m_l)
        yield [m_l]
        bank = yield from work_banks.take()
        PE.wait(m_l, m_b, *bank.free)
        m = PE.mark(partial(nc.tensor.transpose, bank.t[0:3 * H * TT, 0:P],
                                          sh.t[:, :, :].rearrange("p j r -> p (j r)"), ident[:, :]))
        sh.release(m)
        shT = yield from shiftT.take()
        yield [m, *shT.free]
        AC.wait(m, *shT.free)
        m = AC.mark(partial(nc.scalar.activation, shT.t[:, :], bank.t[0:3 * H * TT, 0:P], ACT.Copy))
        bank.release(m)
        yield [m]
        SP.wait(m)
        m = SP.load(shift_out[l], partial(nc.sync.dma_start, max_dram[l][b], shT.t[:, :]))
        shT.release(m)
        lower_written[b, l] = m
        yield [m]
        SP.wait(m)
        shifts_ready[b, l] = SP.load(shift_in[l], partial(nc.sync.dma_start,
            sq.t[FULL:ROWS, :, :].bitcast(F32).rearrange("j h s -> j (h s)"),
            max_dram[l][b, 0:2 * H * TT].rearrange("(j r) q -> j (r q)", j=2)))
        finished.add(("maxima", b, l))

    normal = {}

    def attend(b, l):
        yield from until(("maxima", b, l), ("value rows", b, l), *([("mean", b)] if l == 1 else []))
        lock = yield from attending.take()
        normal[b, l] = yield from attn.take()
        sq, sk, v = stack_q[l], stack_k[l], values[l]
        two = lambda t: t[:, :].rearrange("p (k s) -> p k s", k=2)

        def load_lower(h):
            low = yield from lower.take()
            yield low.free
            SP.wait(lower_written[b, l], *low.free)
            low.ready = SP.load(low.sem, partial(nc.sync.dma_start,
                low.t[:, :, :].rearrange("p h s -> p (h s)"),
                max_dram[l][b, 2 * H * TT + h * TT:2 * H * TT + (h + LB_HEADS) * TT]
                .rearrange("r q -> (r q)").partition_broadcast(P)))
            return low

        low = None
        next_low = (yield from load_lower(0)) if l == 1 else None
        clips, exps = [], []
        for h in range(H + 2):
            if h < H:
                if l == 1 and h % LB_HEADS == 0:
                    low = next_low
                    if h + LB_HEADS < H:
                        next_low = yield from load_lower(h + LB_HEADS)
                yield [shifts_ready[b, l]]
                bank = yield from work_banks.take()
                PE.wait(shifts_ready[b, l], *bank.free)
                for kt in range(2):
                    mm = partial(nc.tensor.matmul,
                        bank.t[:, kt * S:kt * S + S], sk.t[:, h, kt * P:kt * P + P], sq.t[:, h, :],
                        start=True, stop=True)
                    m = PE.mark(mm) if kt else PE.put(mm)
                yield [m]
                if l == 1:
                    c = yield from clipped.take()
                    DV.wait(m, low.ready, *c.free)
                    i = h % LB_HEADS
                    m = DV.mark(partial(nc.vector.scalar_tensor_tensor,
                        c.t[:, :, :], two(bank.t), 0.0, low.t[:, i:i + 1, :].broadcast_to([P, 2, S]),
                        ALU.min, ALU.max))
                    bank.release(m)
                    if i == LB_HEADS - 1:
                        low.release(m)
                    clips.append((h, c, c.t[:, :, :], m))
                else:
                    clips.append((h, bank, two(bank.t), m))
            if clips and (l == 0 or h >= 1):
                hc, source, view, m = clips.pop(0)
                p = yield from probs.take()
                AC.wait(m, *p.free)
                p.ready = AC.mark(partial(nc.scalar.activation, p.t[:, :, :], view, ACT.Exp))
                source.release(p.ready)
                exps.append((hc, p))
            if len(exps) > 1 or h >= H and exps:
                hv, p = exps.pop(0)
                yield [p.ready]
                if hv % 8 == 0:
                    vbank = yield from value_banks.take()
                    PE.wait(*vbank.free)
                c, half = hv % 4, (hv // 4) % 2
                PE.wait(p.ready, v.ready)
                for kt in range(2):
                    mm = partial(nc.tensor.matmul, vbank.t[32 * c:32 * c + 32, half * S:half * S + S],
                                 v.t[:, kt, hv, :], p.t[:, kt, :], start=kt == 0, stop=kt == 1)
                    m = PE.mark(mm) if kt else PE.put(mm)
                p.release(m)
                if hv % 8 == 7:
                    vbank.ready = m
                    summed_values[b, l, hv // 8] = vbank
                    finished.add(("sums", b, l, hv // 8))
        sq.free = sk.free = v.free = [m]
        finished.add(("attend", b, l))
        lock.release()

    summed_values = {}

    def value_out(b, l, pair):
        yield from until(("sums", b, l, pair))
        vbank = summed_values[b, l, pair]
        w = yield from weighted.take()
        yield [vbank.ready, *w.free]
        AC.wait(vbank.ready, *w.free)
        m = AC.mark(partial(nc.scalar.activation, w.t[:, :, :].rearrange("p g s -> p (g s)"), vbank.t[:, :], ACT.Copy))
        vbank.release(m)
        yield [m]
        bank = yield from work_banks.take()
        PE.wait(m, *bank.free)
        for t in range(TT):
            for g in range(2):
                o = (t * 2 + g) * P
                tr = partial(nc.tensor.transpose, bank.t[:, o:o + P], w.t[:, g, t * P:t * P + P], ident[:, :])
                m = PE.mark(tr) if (t, g) == (TT - 1, 1) else PE.put(tr)
        w.release(m)
        view = bank.t[:, :].rearrange("p (t h e) -> p t h e", t=TT, e=2 * HD)
        o, r = normal[b, l], (yield from recip.take())
        yield [m, *o.free]
        DV.wait(m, *r.free, *o.free)
        m = DV.mark(partial(nc.vector.reciprocal, r.t[:, :, :], view[:, :, :, HD]))
        m = dv(partial(nc.vector.tensor_tensor,
            o.t[:, :, pair * P:pair * P + P].rearrange("p t (h d) -> p t h d", d=HD), view[:, :, :, 0:HD],
            r.t[:, :, :].unsqueeze(3).broadcast_to([P, TT, 8, HD]), ALU.mult), m)
        r.release(m)
        bank.release(m)
        o.ready = m
        finished.add(("normal", b, l, pair))

    def output(b, l):
        yield from until(("normal", b, l, 0), ("normal", b, l, 1))
        o = normal[b, l]
        yield [o.ready]
        bank = yield from work_banks.take()
        PE.wait(o.ready, *bank.free)
        for k in range(KC):
            for t in range(TT):
                c = k * S + t * P
                tr = partial(nc.tensor.transpose, bank.t[:, c:c + P], o.t[:, t, k * P:k * P + P], ident[:, :])
                m = PE.mark(tr) if (k, t) == (KC - 1, TT - 1) else PE.put(tr)
        o.release(m)
        oT = yield from attnT.take()
        yield [m, *oT.free]
        AC.wait(m, *oT.free)
        m = AC.mark(partial(nc.scalar.activation, oT.t[:, :, :].rearrange("p k s -> p (k s)"), bank.t[:, :], ACT.Copy))
        bank.release(m)
        yield [m]
        bank = yield from work_banks.take()
        PE.wait(m, *bank.free)
        for t in range(TT):
            for k in range(KC):
                mm = partial(nc.tensor.matmul,
                    bank.t[:, t * D:t * D + D], oT.t[:, k, t * P:t * P + P], wo[l][:, k, :],
                    start=k == 0, stop=k == KC - 1)
                m = PE.mark(mm) if (t, k) == (TT - 1, KC - 1) else PE.put(mm)
        oT.release(m)
        s = yield from summed.take()
        yield [m, *s.free]
        DV.wait(m, *s.free)
        m = DV.mark(partial(nc.vector.tensor_tensor,
            s.t[:, :, :], bank.t[:, :].rearrange("p (t d) -> p t d", t=TT),
            ob[l][:, :].unsqueeze(1).broadcast_to([P, TT, D]), ALU.add))
        bank.release(m)
        xs = x[:, TT * b:TT * b + TT, :]
        if l == 0:
            m = dv(partial(nc.vector.scalar_tensor_tensor, xs, s.t[:, :, :], tg[:, 0:1], xs, ALU.mult, ALU.add),
                   m, tg_ready)
            x_ready[b] = m
            s.release(m)
        else:
            m = dv(partial(nc.vector.tensor_scalar, s.t[:, :, :], s.t[:, :, :], tg[:, 1:2], None, ALU.mult), m, tg_ready)
            yield [m]
            SP.wait(m)
            z_stored[b] = SP.load(z_out[b], partial(nc.sync.dma_start,
                z_dram[b].rearrange("(t p) d -> p t d", p=P), s.t[:, :, :]))
            s.release(z_stored[b])
        finished.add(("output", b, l))

    act_gate = Ring(*[sba(f"act_gate{i}", [P, S]) for i in range(2)])
    act_t = Ring(*[sba(f"act_t{i}", [P, S]) for i in range(2)])
    cwT = Ring(sba("cwT", [2 * E0, S], F32R))
    route0 = Ring(sba("rt", [P, 12, TT, 8]))
    pairs = Slot(sba("pairs", [P, 2, TT, 8, 8]))
    cw_hl = Ring(sba("cw_hl", [P, TT, 2 * E0]))

    def rank_of(values_ap, ranks, n, m):
        j = values_ap.unsqueeze(2).broadcast_to([P, TT, n, n])
        i = values_ap.unsqueeze(3).broadcast_to([P, TT, n, n])
        bef = before[:, 0:n, 0:n].unsqueeze(1).broadcast_to([P, TT, n, n])
        aft = after[:, 0:n, 0:n].unsqueeze(1).broadcast_to([P, TT, n, n])
        pa, pb = (pairs.t[:, side, :, 0:n, 0:n] for side in range(2))
        DV.wait(m, order_ready, *pairs.free)
        m1 = DV.mark(partial(nc.vector.tensor_tensor, pa, j, i, ALU.is_ge))
        m2 = DV.mark(partial(nc.vector.tensor_tensor, pb, j, i, ALU.is_gt))
        m1 = dv(partial(nc.vector.tensor_tensor, pa, pa, bef, ALU.mult), m1)
        m2 = dv(partial(nc.vector.tensor_tensor, pb, pb, aft, ALU.mult), m2)
        m1 = dv(partial(nc.vector.tensor_tensor, pa, pa, pb, ALU.add), m1, m2)
        m = dv(partial(nc.vector.tensor_reduce, ranks, pa, AX, ALU.add), m1)
        pairs.free = [m]
        return m

    gate_wT_ready = []

    def transpose_gate():
        yield [ffn0_w]
        bank = yield from work_banks.take()
        PE.wait(ffn0_w, ident_ready, *bank.free)
        for k in range(KC):
            tr = partial(nc.tensor.transpose, bank.t[:, k * E0:k * E0 + E0], gate_rows[:, k * P:k * P + P],
                                            ident[0:E0, 0:E0])
            m = PE.mark(tr) if k else PE.put(tr)
        AC.wait(m)
        m = AC.mark(partial(nc.scalar.activation, gate_wT[:, :, :].rearrange("p k e -> p (k e)"),
                                           bank.t[:, 0:KC * E0], ACT.Copy))
        bank.release(m)
        gate_wT_ready.append(m)

    experts0_done = []

    def experts0(b):
        yield from until(("output", b, 0), *([("routed0", b - 1)] if b else []))
        slot_n = yield from xn.take()
        xT = yield from xnT.take()
        yield from layer_norm(b, slot_n, xT)
        if b == 0:
            yield from transpose_gate()
        rt = yield from route0.take()
        yield [xT.ready]
        bank = yield from work_banks.take()
        PE.wait(xT.ready, *gate_wT_ready, *bank.free)
        for t in range(TT):
            for k in range(KC):
                mm = partial(nc.tensor.matmul,
                    bank.t[:, t * E0:t * E0 + E0], xT.t[:, k, t * P:t * P + P], gate_wT[:, k, :],
                    start=k == 0, stop=k == KC - 1)
                m = PE.mark(mm) if (t, k) == (TT - 1, KC - 1) else PE.put(mm)
        row = lambda i: rt.t[:, i, :, :]
        yield [m]
        AC.wait(m, *rt.free)
        m = AC.mark(partial(nc.scalar.activation, row(0), bank.t[:, 0:TT * E0].rearrange("p (t e) -> p t e", t=TT),
                                           ACT.Exp, scale=-1.0))
        bank.release(m)
        yield [m]
        m = dv(partial(nc.vector.tensor_scalar, row(1), row(0), 1.0, None, ALU.add), m)
        m_s = dv(partial(nc.vector.reciprocal, row(2), row(1)), m)
        m = dv(partial(nc.vector.tensor_tensor, row(3), row(2), corr[:, :].unsqueeze(1).broadcast_to([P, TT, E0]),
                                         ALU.add), m_s, ffn0_w)
        grp = row(3).rearrange("p t (g i) -> p t g i", i=E0 // NG)
        m = dv(partial(nc.vector.tensor_tensor, row(4)[:, :, 0:NG], grp[:, :, :, 0], grp[:, :, :, 1], ALU.add), m)
        yield []
        m = rank_of(row(4)[:, :, 0:NG], row(5)[:, :, 0:NG], NG, m)
        m = dv(partial(nc.vector.tensor_scalar, row(6)[:, :, 0:NG], row(5)[:, :, 0:NG], TKG - 0.5, None, ALU.is_lt), m)
        m = dv(partial(nc.vector.tensor_tensor, row(7).rearrange("p t (g i) -> p t g i", i=E0 // NG), grp,
                                         row(6)[:, :, 0:NG].unsqueeze(3).broadcast_to([P, TT, NG, E0 // NG]),
                                         ALU.mult), m)
        yield []
        m = rank_of(row(7), row(8), E0, m)
        yield []
        m = dv(partial(nc.vector.scalar_tensor_tensor, row(9), row(8), TOPK0 - 0.5, row(2), ALU.is_lt, ALU.mult), m)
        m = dv(partial(nc.vector.tensor_reduce, row(10)[:, :, 0], row(9), AX, ALU.add), m)
        m = dv(partial(nc.vector.tensor_scalar, row(10)[:, :, 1], row(10)[:, :, 0], 1e-20, None, ALU.add), m)
        m = dv(partial(nc.vector.reciprocal, row(10)[:, :, 2], row(10)[:, :, 1]), m)
        m = dv(partial(nc.vector.scalar_tensor_tensor, row(11), row(9), 2.5 * 0.5,
                                                row(10)[:, :, 2:3].broadcast_to([P, TT, E0]), ALU.mult, ALU.mult),
               m)
        hl = yield from cw_hl.take()
        m = dv(partial(nc.vector.tensor_copy, hl.t[:, :, 0:E0].bitcast(F32R), row(11)), m, *hl.free)
        m = dv(partial(nc.vector.tensor_tensor, hl.t[:, :, E0:2 * E0].bitcast(F32R), row(11), hl.t[:, :, 0:E0],
                                         ALU.subtract), m)
        rt.release(m)
        yield [m]
        bank = yield from work_banks.take()
        PE.wait(m, *bank.free)
        for t in range(TT):
            tr = partial(nc.tensor.transpose, bank.t[0:2 * E0, t * P:t * P + P], hl.t[:, t, :], ident[:, :])
            m = PE.mark(tr) if t == TT - 1 else PE.put(tr)
        hl.release(m)
        cw = yield from cwT.take()
        yield [m, *cw.free]
        AC.wait(m, *cw.free)
        cw.ready = AC.mark(partial(nc.scalar.activation, cw.t[:, :], bank.t[0:2 * E0, 0:S], ACT.Copy))
        bank.release(cw.ready)
        finished.add(("routed0", b))
        y = yield from work_banks.take()
        PE.wait(*y.free)
        order = [E0] + list(range(E0))
        hiddens = []
        for n in range(E0 + 2):
            if n <= E0:
                e_ = order[n]
                gu = yield from work_banks.take()
                PE.wait(*gu.free)
                for half, w in enumerate((w_gate0, w_up0)):
                    for k in range(KC):
                        mm = partial(nc.tensor.matmul,
                            gu.t[:, half * S:half * S + S], w[:, k, e_, :], xT.t[:, k, :], start=k == 0,
                            stop=k == KC - 1)
                        m_gu = PE.mark(mm) if half and k == KC - 1 else PE.put(mm)
                    if half == 0:
                        yield []
                if n == E0:
                    xT.release(m_gu)
            if hiddens:
                yield []
                e_down, h = hiddens.pop()
                PE.wait(h.ready)
                for t in range(TT):
                    mm = partial(nc.tensor.matmul,
                        y.t[:, t * D:t * D + D], h.t[:, t * P:t * P + P], w_down0[:, e_down, :], start=n == 1 and t == 0,
                        stop=n == E0 + 1, skip_group_check=True)
                    m_y = PE.mark(mm) if t == TT - 1 else PE.put(mm)
                h.release(m_y)
            if n > E0:
                break
            th = yield from act_gate.take()
            yield [m_gu]
            AC.wait(m_gu, *th.free)
            m = AC.mark(partial(nc.scalar.activation, th.t[:, :], gu.t[:, 0:S], ACT.Tanh, scale=0.5))
            if n:
                scale = yield from work_banks.take()
                PE.wait(cw.ready, cw_sel_ready, *scale.free)
                m_w = PE.mark(partial(nc.tensor.matmul, scale.t[:, 0:S], cw_sel[:, e_:e_ + 1].broadcast_to([2 * E0, P]), cw.t[:, :],
                                      start=True, stop=True))
                if n == E0:
                    cw.release(m_w)
            yield [m, m_gu]
            tmp = yield from act_t.take()
            m = dv(partial(nc.vector.scalar_tensor_tensor,
                tmp.t[:, :], th.t[:, :], 1.0, gu.t[:, 0:S], ALU.add, ALU.mult), m, *tmp.free)
            th.release(m)
            if n:
                m = dv(partial(nc.vector.tensor_tensor, tmp.t[:, :], tmp.t[:, :], scale.t[:, 0:S], ALU.mult), m, m_w)
                scale.release(m)
            h = yield from hidden0.take()
            h.ready = dv(partial(nc.vector.scalar_tensor_tensor,
                h.t[:, :], tmp.t[:, :], 1.0 if n else 0.5, gu.t[:, S:2 * S], ALU.mult, ALU.mult), m, m_gu, *h.free)
            tmp.release(h.ready)
            gu.release(h.ready)
            hiddens.append((e_, h))
        xs = x[:, TT * b:TT * b + TT, :]
        yield [m_y]
        m = dv(partial(nc.vector.scalar_tensor_tensor, xs, y.t[:, :].rearrange("p (t d) -> p t d", t=TT), tg[:, 2:3], xs,
                                                ALU.mult, ALU.add), m_y, tg_ready)
        y.release(m)
        x_ready[b] = m
        experts0_done.append(m_y)
        finished.add(("experts0", b))

    flag = sba("flag", [P, 4])
    vmT = sba("vmT", [P, KC, NB])
    alt_in, zalt_out = dma_sem("alt_in"), dma_sem("zalt_out")
    alt_ready = {}

    def guard():
        yield from until(("keys", NB - 1, 1), ("queries", NB - 1, 1))
        yield nan_marks
        m = dv(partial(nc.vector.tensor_reduce, flag[:, 0:1], nan_sum[:, :], AX, ALU.add), *nan_marks)
        m = dv(partial(nc.vector.tensor_tensor, flag[:, 1:2], flag[:, 0:1], flag[:, 0:1], ALU.is_equal), m)
        yield [m]
        bank = yield from work_banks.take()
        PE.wait(m, *bank.free)
        m = PE.mark(partial(nc.tensor.matmul, bank.t[:, 0:1], ones[:, :], flag[:, 1:2], start=True, stop=True))
        yield [m]
        m = dv(partial(nc.vector.tensor_scalar, flag[:, 2:3], bank.t[:, 0:1], P - 0.5, None, ALU.is_lt), m)
        bank.release(m)
        alt_ready["keep"] = dv(partial(nc.vector.tensor_scalar, keep_row[:, :], zero_row[:, 0:1], flag[:, 2:3], None,
                                       ALU.add), m, zero_ready)
        room = yield from clipped.take()
        vm, zalt = room.t[0:NB, 0, :], room.t[0:NB, 1, :]
        yield vmean_stored
        SP.wait(*vmean_stored, *room.free)
        m = SP.load(alt_in, partial(nc.sync.dma_start, vm, vmean_dram[:, :]))
        yield [m]
        bank = yield from work_banks.take()
        PE.wait(m, *bank.free)
        for k in range(KC):
            tr = partial(nc.tensor.transpose, bank.t[:, k * NB:k * NB + NB], vm[:, k * P:k * P + P],
                                                       ident[0:NB, 0:NB])
            m = PE.mark(tr) if k else PE.put(tr)
        yield [m]
        AC.wait(m)
        m = AC.mark(partial(nc.scalar.activation, vmT[:, :, :].rearrange("p k b -> p (k b)"), bank.t[:, 0:KC * NB],
                            ACT.Copy))
        bank.release(m)
        yield [m]
        bank = yield from work_banks.take()
        PE.wait(m, *bank.free)
        for k in range(KC):
            mm = partial(nc.tensor.matmul, bank.t[0:NB, 0:D], vmT[:, k, :], wo[1][:, k, :], start=k == 0, stop=k == 1)
            m = PE.mark(mm) if k else PE.put(mm)
        yield [m]
        m = dv(partial(nc.vector.tensor_tensor, zalt, bank.t[0:NB, 0:D], ob[1][0:NB, :], ALU.add), m)
        bank.release(m)
        m = dv(partial(nc.vector.tensor_scalar, zalt, zalt, tg[0:NB, 1:2], None, ALU.mult), m)
        yield [m]
        SP.wait(m)
        alt_ready["zalt"] = SP.load(zalt_out, partial(nc.sync.dma_start, zalt_dram[:, :], zalt))
        room.release(alt_ready["zalt"])
        for slot in (*xn1.slots, *z_in.slots, *alt_row.slots):
            slot.free = [experts0_done[-1]]
        finished.add("guard")

    WIDE = D + E1
    FINISHING = 4

    def in_place_of(t, i, width):
        dims = "p a b c -> p (a b c)" if len(t.shape) == 4 else "p a b -> p (a b)"
        flat = t[(slice(None),) * len(t.shape)].rearrange(dims)
        return flat[:, i * TT * width:(i + 1) * TT * width].rearrange("p (t d) -> p t d", t=TT)

    xn1 = Ring(*[in_place_of(w_gate0, i, WIDE) for i in range(FINISHING)])
    z_in = Ring(*[in_place_of(w_up0, i, D) for i in range(FINISHING)])
    alt_row = Ring(*[in_place_of(w_down0, i, D)[:, 0, :] for i in range(FINISHING)])
    for i, slot in enumerate(z_in.slots):
        slot.sem = dma_sem(f"z_in{i}")
    route1 = Ring(*[sba(f"route1_{i}", [P, 8, TT, E1]) for i in range(2)])
    wr = sba("wr", [P, KC, E1])
    br = sba("br", [P, E1])
    router_in = dma_sem("router_in")
    router_w = None
    xn1_out = [dma_sem(f"xn1_out{b}") for b in range(NB)]
    x_out = [dma_sem(f"x_out{b}") for b in range(NB)]
    pad_out = dma_sem("pad_out")
    prefix = {}
    rows_written = []
    routed = []

    def load_router():
        nonlocal router_w
        for dst, src in ((wr[:, :, :], a["L1_ffn_Wr"].rearrange("(k p) e -> p k e", p=P)),
                         (br[:, :], a["L1_ffn_br"].partition_broadcast(P))):
            router_w = SP.load(router_in, partial(nc.sync.dma_start, dst, src))
        SP.wait(zero_ready)
        SP.load(pad_out, partial(nc.sync.dma_start, xn1_dram[NB * S:NB * S + P, :], zero_row[:, :]))
        rows_written.append(SP.load(pad_out, partial(nc.sync.dma_start, out[NB * S:NB * S + P, :], zero_row[:, 0:D])))
        finished.add("router")

    def finish(b):
        yield from until("guard", "router", ("output", b, 1), *([("finish", b - 1)] if b else []))
        z, alt = (yield from z_in.take()), (yield from alt_row.take())
        yield [z_stored[b], alt_ready["zalt"], *z.free, *alt.free]
        SP.wait(z_stored[b], alt_ready["zalt"], *z.free, *alt.free)
        SP.load(z.sem, partial(nc.sync.dma_start, z.t[:, :, :], z_dram[b].rearrange("(t p) d -> p t d", p=P)))
        m = SP.load(z.sem, partial(nc.sync.dma_start, alt.t, zalt_dram[b].partition_broadcast(P)))
        finished.add(("finish", b))
        yield [m, alt_ready["keep"]]
        DV.wait(m, alt_ready["keep"])
        for t in range(TT):
            m = DV.mark(partial(nc.vector.copy_predicated, z.t[:, t, :], keep_row[:, 0:1].broadcast_to([P, D]), alt.t))
        alt.release(m)
        xs = x[:, TT * b:TT * b + TT, :]
        m = dv(partial(nc.vector.tensor_tensor, xs, xs, z.t[:, :, :], ALU.add), m)
        z.release(m)
        x_ready[b] = m
        yield [m]
        SP.wait(m)
        rows_written.append(SP.load(x_out[b], partial(nc.sync.dma_start,
            out[b * S:b * S + S, :].rearrange("(t p) d -> p t d", p=P), xs)))
        wide_rows = yield from xn1.take()
        n = Slot(wide_rows.t[:, :, 0:D])
        n.free = wide_rows.free
        xT = yield from xnT.take()
        yield from layer_norm(b, n, xT)
        yield [xT.ready]
        bank = yield from work_banks.take()
        PE.wait(xT.ready, router_w, *bank.free)
        for t in range(TT):
            for k in range(KC):
                mm = partial(nc.tensor.matmul,
                    bank.t[:, t * E1:t * E1 + E1], xT.t[:, k, t * P:t * P + P], wr[:, k, :],
                    start=k == 0, stop=k == KC - 1)
                m = PE.mark(mm) if (t, k) == (TT - 1, KC - 1) else PE.put(mm)
        xT.release(m)
        rt = yield from route1.take()
        row = lambda i: rt.t[:, i, :, :]
        wide = lambda ap: ap.broadcast_to([P, TT, E1])
        yield [m, *rt.free]
        lg = row(0)
        m = dv(partial(nc.vector.tensor_tensor,
            lg, bank.t[:, 0:TT * E1].rearrange("p (t e) -> p t e", t=TT),
            br[:, :].unsqueeze(1).broadcast_to([P, TT, E1]), ALU.add), m, router_w, *rt.free)
        bank.release(m)
        m_rank = rank_of(lg, row(1), E1, m)
        yield []
        tiles = slice(TT * b, TT * b + TT)
        m_mask = dv(partial(nc.vector.tensor_scalar, mask[:, tiles, :], row(1), TOPK1 - 0.5, None, ALU.is_lt), m_rank)
        DV.wait(m_rank)
        for r in range(TOPK1):
            m_pick = DV.mark(partial(nc.vector.tensor_scalar, picks[:, r, tiles, :], row(1), float(r), None, ALU.is_equal))
        m_max = dv(partial(nc.vector.tensor_reduce, row(7)[:, :, 0], lg, AX, ALU.max))
        m = dv(partial(nc.vector.tensor_tensor, row(2), lg, mask[:, tiles, :], ALU.mult), m_mask)
        m1 = dv(partial(nc.vector.tensor_scalar, row(3), mask[:, tiles, :], -NEG_INF, NEG_INF, ALU.mult, ALU.add), m_mask)
        m = dv(partial(nc.vector.tensor_tensor, row(2), row(2), row(3), ALU.add), m, m1)
        m = dv(partial(nc.vector.tensor_tensor, row(2), row(2), wide(row(7)[:, :, 0:1]), ALU.subtract), m, m_max)
        yield [m]
        AC.wait(m)
        m = AC.mark(partial(nc.scalar.activation, row(3), row(2), ACT.Exp))
        if b == 0:
            prefix["bank"] = yield from work_banks.take()
            PE.wait(*prefix["bank"].free)
        else:
            yield from until(("counted", b - 1))
        counts = prefix["bank"]
        PE.wait(m_mask, tri_ready)
        for t in range(TT * b, TT * b + TT):
            PE.put(partial(nc.tensor.matmul, counts.t[:, t * E1:t * E1 + E1], tri[:, :], mask[:, t, :],
                           start=t == 0, stop=False, skip_group_check=True))
            later = NT - 1 - t
            if later:
                PE.put(partial(nc.tensor.matmul,
                    counts.t[:, (t + 1) * E1:NT * E1].rearrange("p (t e) -> p t e", e=E1), ones_bf[:, :],
                    mask[:, t:t + 1, :].broadcast_to([P, later, E1]), start=False, stop=False, skip_group_check=True))
            counts.ready = PE.mark(partial(nc.tensor.matmul, counts.t[:, NT * E1:NT * E1 + E1], ones_bf[:, :],
                                           mask[:, t, :], start=False, stop=t == NT - 1, skip_group_check=True))
        finished.add(("counted", b))
        yield [m]
        m = dv(partial(nc.vector.tensor_reduce, row(7)[:, :, 1], row(3), AX, ALU.add), m)
        m = dv(partial(nc.vector.reciprocal, row(7)[:, :, 2], row(7)[:, :, 1]), m)
        m = dv(partial(nc.vector.tensor_scalar, row(7)[:, :, 3], row(7)[:, :, 2], tg[:, 3:4], None, ALU.mult), m)
        m = dv(partial(nc.vector.tensor_tensor, row(4), row(3), wide(row(7)[:, :, 3:4]), ALU.mult), m)
        m = dv(partial(nc.vector.tensor_tensor, wide_rows.t[:, :, D:WIDE], row(4), mask[:, tiles, :], ALU.mult), m)
        rt.release(m, m_pick)
        routed.append(m)
        yield [m]
        SP.wait(m, n.ready)
        rows_written.append(SP.load(xn1_out[b], partial(nc.sync.dma_start,
            xn1_dram[b * S:b * S + S, :].rearrange("(t p) d -> p t d", p=P), wide_rows.t[:, :, :])))
        wide_rows.release(rows_written[-1], *n.free)

    def later_loads():
        yield from until(("stacking", 0, 0, 0))
        load_experts0()
        yield from until(("maxima", 0, 0))
        load_attention_weights(1)
        yield [attn_w_loaded[1]]
        scale_queries(1)
        finished.add("weights 1")
        yield from until(("experts0", 0))
        load_router()

    stages = [later_loads()]
    for b in range(NB):
        for l in range(2):
            stages += [output(b, l), value_out(b, l, 1), value_out(b, l, 0), attend(b, l), maxima(b, l),
                       queries(b, l), keys(b, l), value_rows(b, l)]
    stages += [experts0(b) for b in range(NB)]
    stages += [guard()] + [finish(b) for b in range(NB)]
    weave(stages, PE)

    m_counts = prefix["bank"].ready
    counts_bank = prefix["bank"]
    tail = [(q.sem, q.count) for q in (PE, DV, AC, PO)] + rows_written
    tens.close()

    for q in (PE, DV, AC, PO, SP):
        q.wait(*tail)

    b1 = sb("b1", [E1, H1])
    b2 = sb("b2", [E1, D])
    biases_in = dma_sem("biases_in")
    SP.load(biases_in, partial(nc.sync.dma_start, b1[:, :], a["L1_ffn_b1"]))
    biases = SP.load(biases_in, partial(nc.sync.dma_start, b2[:, :], a["L1_ffn_b2"]))
    W1S = 3
    w1 = Ring(*[sb(f"w1_{i}", [P, KC, H1]) for i in range(W1S)])
    w2 = Ring(*[sb(f"w2_{i}", [P, JH, D]) for i in range(W1S)])
    PICKS = TOPK1 * NT

    cnt = sb("cnt", [P, 6, E1])
    c = lambda i: cnt[:, i, :]
    over = sb("over", [P, E1, NB * S // P])
    cum = sb("cum", [P, E1, E1])
    m = dv(partial(nc.vector.tensor_copy, c(0), counts_bank.t[:, NT * E1:NT * E1 + E1]), m_counts)
    m = dv(partial(nc.vector.tensor_tensor, over[:, :, :], c(0).unsqueeze(2).broadcast_to([P, E1, NB * S // P]),
                   steps[:, :, :], ALU.is_gt), m, no_ready)
    m = dv(partial(nc.vector.tensor_reduce, c(1), over[:, :, :], AX, ALU.add), m)
    m = dv(partial(nc.vector.tensor_tensor, cum[:, :, :], before[:, :, :], c(1).unsqueeze(1).broadcast_to([P, E1, E1]),
                                     ALU.mult), m)
    m = dv(partial(nc.vector.tensor_reduce, c(2), cum[:, :, :], AX, ALU.add), m)
    m_first = dv(partial(nc.vector.tensor_scalar, c(4), c(2), float(P), None, ALU.mult), m)
    m_end = dv(partial(nc.vector.tensor_tensor, c(3), c(2), c(1), ALU.add), m)
    ended = sb("ended", [P, BLOCKS, E1])
    block_e = sb("block_e", [P, BLOCKS])
    block_i = sb("block_i", [P, BLOCKS], I32)
    m = dv(partial(nc.vector.tensor_tensor, ended[:, :, :], block_no[:, :, :],
                                     c(3).unsqueeze(1).broadcast_to([P, BLOCKS, E1]), ALU.is_ge), m_end, no_ready)
    m = dv(partial(nc.vector.tensor_reduce, block_e[:, :], ended[:, :, :], AX, ALU.add), m)
    m_be = dv(partial(nc.vector.tensor_scalar, block_e[:, :], block_e[:, :], E1 - 1.0, None, ALU.min), m)
    block_ready = dv(partial(nc.vector.tensor_copy, block_i[:, :], block_e[:, :]), m_be)

    slots_all = sb("slots_all", [P, NT, E1])
    slots_pick = sb("slots_pick", [P, TOPK1, NT, E1])
    slot_f = sb("slot_f", [P, PICKS])
    slot_i = sb("slot_i", [P, 3, PICKS], I32)
    place_block = sb("place_block", [P, 2, PICKS])
    at_place = sb("at_place", [P, PICKS, P], BF16)
    in_block = sb("in_block", [P, PICKS, BLOCKS])
    in_block_no = sb("in_block_no", [P, PICKS, 2, BLOCKS], BF16)
    m = dv(partial(nc.vector.tensor_tensor, slots_all[:, :, :],
        counts_bank.t[:, 0:NT * E1].rearrange("p (t e) -> p t e", e=E1),
        c(4).unsqueeze(1).broadcast_to([P, NT, E1]), ALU.add), m_first)
    counts_bank.release(m)
    m = dv(partial(nc.vector.tensor_tensor, slots_pick[:, :, :, :], picks[:, :, :, :],
                   slots_all[:, :, :].unsqueeze(1).broadcast_to([P, TOPK1, NT, E1]), ALU.mult), m)
    m = dv(partial(nc.vector.tensor_reduce, slot_f[:, :], slots_pick[:, :, :, :].rearrange("p r t e -> p (r t) e"),
                   AX, ALU.add), m)
    m = dv(partial(nc.vector.tensor_copy, slot_i[:, 0, :], slot_f[:, :]), m)
    m1 = dv(partial(nc.vector.tensor_scalar, slot_i[:, 1, :], slot_i[:, 0, :], P - 1, None, ALU.bitwise_and), m)
    m2 = dv(partial(nc.vector.tensor_scalar, slot_i[:, 2, :], slot_i[:, 0, :], LOG_P, None, ALU.logical_shift_right), m)
    m_split = dv(partial(nc.vector.tensor_copy, place_block[:, :, :], slot_i[:, 1:3, :]), m1, m2)

    onehot = sb("onehot", [P, BLOCKS, E1])
    onehotT = sb("onehotT", [P, BLOCKS])
    b1_all = sb("b1_all", [P, JH, BLOCKS])
    onehotT_ready = dv(partial(nc.vector.tensor_scalar, onehotT[:, :], block_e[:, :], part_no[:, 0:1], None,
                                                 ALU.is_equal), m_be, no_ready)
    onehot_ready = dv(partial(nc.vector.tensor_tensor, onehot[:, :, :],
        expert_row[:, :].unsqueeze(1).broadcast_to([P, BLOCKS, E1]),
        block_e[:, :].unsqueeze(2).broadcast_to([P, BLOCKS, E1]), ALU.is_equal), m_be, no_ready)
    b1_bank = work_banks.grab()
    PE.wait(biases, onehotT_ready, *b1_bank.free)
    for j in range(JH):
        mm = partial(nc.tensor.matmul, b1_bank.t[:, j * BLOCKS:j * BLOCKS + BLOCKS], b1[:, j * P:j * P + P],
                     onehotT[0:E1, :], start=True, stop=True)
        m_b1 = PE.mark(mm) if j == JH - 1 else PE.put(mm)

    m = dv(partial(nc.vector.tensor_tensor, in_block[:, :, :],
                   place_block[:, 1, :].unsqueeze(2).broadcast_to([P, PICKS, BLOCKS]),
                   block_row[:, :].unsqueeze(1).broadcast_to([P, PICKS, BLOCKS]), ALU.is_equal), m_split, no_ready)
    PO.wait(m)
    m0 = PO.mark(partial(nc.gpsimd.tensor_tensor, in_block_no[:, :, 0, :], in_block[:, :, :],
                         tile_start[:, :].unsqueeze(2).broadcast_to([P, PICKS, BLOCKS]), ALU.mult))
    AC.wait(m)
    m1 = AC.mark(partial(nc.scalar.activation, in_block_no[:, :, 1, :], in_block[:, :, :], ACT.Copy,
                         scale=row_no[:, 0:1]))
    AC.wait(m_b1)
    b1_ready = AC.mark(partial(nc.scalar.activation, b1_all[:, :, :].rearrange("p j b -> p (j b)"),
                               b1_bank.t[:, 0:JH * BLOCKS], ACT.Copy))
    b1_bank.release(b1_ready)
    in_block_ready = [m0, m1]
    bank = work_banks.grab()
    PE.wait(*in_block_ready, *bank.free)
    QUARTER = PICKS // 4
    for q in range(4):
        part = slice(q * QUARTER, (q + 1) * QUARTER)
        m = dv(partial(nc.vector.tensor_tensor, at_place[:, part, :],
                       place_block[:, 0, part].unsqueeze(2).broadcast_to([P, QUARTER, P]),
                       place_row[:, :].unsqueeze(1).broadcast_to([P, QUARTER, P]), ALU.is_equal), m_split, no_ready)
        PE.wait(m)
        for i in range(q * QUARTER, (q + 1) * QUARTER):
            mm = partial(nc.tensor.matmul, bank.t[:, 0:2 * BLOCKS], at_place[:, i, :],
                         in_block_no[:, i, :, :].rearrange("p a b -> p (a b)"), start=i == 0, stop=i == PICKS - 1)
            m_tok = PE.mark(mm) if i == PICKS - 1 else PE.put(mm)
    tok = sb("tok", [P, 3, BLOCKS])
    token_i = sb("token_i", [P, BLOCKS], I32)
    spare = dv(partial(nc.vector.tensor_scalar, tok[:, 0, :], bank.t[:, BLOCKS:2 * BLOCKS], 0.0, spare_row[:, 0:1],
                       ALU.is_equal, ALU.mult), m_tok, no_ready)
    m = dv(partial(nc.vector.tensor_copy, tok[:, 1, :], bank.t[:, 0:BLOCKS]), m_tok)
    m = dv(partial(nc.vector.scalar_tensor_tensor, tok[:, 2, :], bank.t[:, BLOCKS:2 * BLOCKS], -1.0, tok[:, 1, :],
                   ALU.add, ALU.add), m)
    bank.release(m)
    tokens_ready = dv(partial(nc.vector.tensor_tensor, token_i[:, :], tok[:, 2, :], tok[:, 0, :], ALU.add), m, spare)

    W_AHEAD = W1S - 1
    for i, slot in enumerate(w2.slots):
        slot.sem = dma_sem(f"w_in{i}")
    xs_in = Ring(*[sb(f"xs_in{i}", [P, WIDE]) for i in range(4)])
    for i, slot in enumerate(xs_in.slots):
        slot.sem = dma_sem(f"xs_in{i}")
    xsT = Ring(*[sb(f"xsT{i}", [P, KC, P]) for i in range(2)])
    hT = Ring(*[sb(f"hT{i}", [P, JH, P]) for i in range(2)])
    ysb = Ring(*[sb(f"ysb{i}", [P, D]) for i in range(3)])
    own = Ring(*[sb(f"own{i}", [P, 2, E1]) for i in range(3)])
    added = dma_sem("added")
    last = [m for s in (*value_banks.slots, *work_banks.slots) for m in s.free]
    PE.wait(*last)
    AC.wait(*last)
    DV.wait(*last)
    h_banks = Ring(*[banks[i] for i in range(4)])
    y_banks = Ring(*banks[4:6])
    t_banks = Ring(*banks[6:8])
    weights = {}

    def load_weights(i):
        a1, a2 = w1.grab(), w2.grab()
        SP.wait(block_ready, *a1.free, *a2.free)

        def start():
            no = nc.sync.value_load(block_i[0:1, i:i + 1], min_val=0, max_val=E1 - 1)
            nc.sync.dma_start(a1.t[:, :, :], a["L1_ffn_W1"][bass.ds(no, 1)].rearrange("e (k p) n -> p (e k) n", p=P))\
                .then_inc(a2.sem.sem, 16)
            return nc.sync.dma_start(a2.t[:, :, :],
                               a["L1_ffn_W2"][bass.ds(no, 1)].rearrange("e (j p) n -> p (e j) n", p=P))
        a2.sem.total += 16
        weights[i] = (a1, a2, SP.load(a2.sem, start))

    xs_slots = {}

    def load_slots(i):
        s = xs_in.grab()
        PO.wait(tokens_ready, *rows_written, *s.free)
        s.ready = PO.load(s.sem, partial(nc.gpsimd.indirect_dma_start, s.t[:, :], None, xn1_dram[:, :],
            bass.IndirectOffsetOnAxis(ap=token_i[:, i:i + 1].bitcast(U32), axis=0)))
        xs_slots[i] = s

    def turn(i):
        s, xT, bank, w = xs_slots.pop(i), xsT.grab(), t_banks.grab(), own.grab()
        PE.wait(s.ready, *bank.free)
        for k in range(KC):
            tr = partial(nc.tensor.transpose, bank.t[:, k * P:k * P + P], s.t[:, k * P:k * P + P], ident[:, :])
            m_t = PE.mark(tr) if k else PE.put(tr)
        AC.wait(m_t, *xT.free)
        m = AC.mark(partial(nc.scalar.activation, xT.t[:, :, :].rearrange("p k s -> p (k s)"), bank.t[:, 0:KC * P],
                                           ACT.Copy))
        bank.release(m)
        xT.ready = m
        m = dv(partial(nc.vector.tensor_tensor, w.t[:, 0, :], s.t[:, D:WIDE], onehot[:, i, :], ALU.mult),
               s.ready, onehot_ready, *w.free)
        w.ready = dv(partial(nc.vector.tensor_reduce, w.t[:, 1, 0:1], w.t[:, 0, :], AX, ALU.add), m)
        s.release(m_t, m)
        return xT, w

    def up(i, xT):
        a1, _, w_ready_ = weights[i]
        hb, h = (h_banks.grab(), h_banks.grab()), hT.grab()
        for half in range(2):
            PE.wait(xT.ready, w_ready_, *hb[half].free)
            for j in range(half * JH // 2, (half + 1) * JH // 2):
                o = (j % (JH // 2)) * P
                for k in range(KC):
                    mm = partial(nc.tensor.matmul,
                        hb[half].t[:, o:o + P], a1.t[:, k, j * P:j * P + P], xT.t[:, k, :], start=k == 0,
                        stop=k == KC - 1)
                    m = PE.mark(mm) if k == KC - 1 and j % (JH // 2) == JH // 2 - 1 else PE.put(mm)
            q = AC if half == 0 else DV
            q.wait(m, b1_ready, *h.free)
            for j in range(half * JH // 2, (half + 1) * JH // 2):
                o = (j % (JH // 2)) * P
                if q is AC:
                    mh = q.mark(partial(nc.scalar.activation,
                        h.t[:, j, :], hb[half].t[:, o:o + P], ACT.Relu, bias=b1_all[:, j, i:i + 1]))
                else:
                    mh = q.mark(partial(nc.vector.tensor_scalar,
                        h.t[:, j, :], hb[half].t[:, o:o + P], b1_all[:, j, i:i + 1], 0.0, ALU.add, ALU.max))
            hb[half].release(mh)
            h.ready = (h.ready if half else []) + [mh]
        xT.release(m)
        a1.release(m)
        return h

    def down(i, h, w):
        _, a2, w_ready_ = weights.pop(i)
        bank, y = y_banks.grab(), ysb.grab()
        PE.wait(onehotT_ready, biases, w_ready_, *bank.free)
        PE.put(partial(nc.tensor.matmul, bank.t[:, 0:D], onehotT[0:E1, i:i + 1].broadcast_to([E1, P]), b2[:, :],
                                  start=True, stop=False))
        PE.wait(*h.ready)
        for j in range(JH):
            mm = partial(nc.tensor.matmul, bank.t[:, 0:D], h.t[:, j, :], a2.t[:, j, :], start=False,
                                         stop=j == JH - 1)
            m = PE.mark(mm) if j == JH - 1 else PE.put(mm)
        h.release(m)
        a2.release(m)
        DV.wait(m, w.ready, *y.free)
        m = DV.mark(partial(nc.vector.tensor_scalar, y.t[:, :], bank.t[:, 0:D], w.t[:, 1, 0:1], None, ALU.mult))
        bank.release(m)
        w.release(m)
        y.ready = m
        return y

    def add(i, y):
        PO.wait(y.ready, (added.sem, added.total) if i else None)
        m = PO.load(added, partial(nc.gpsimd.indirect_dma_start, out[:, :],
            bass.IndirectOffsetOnAxis(ap=token_i[:, i:i + 1].bitcast(U32), axis=0), y.t[:, :], None,
            compute_op=ALU.add))
        y.release(m)
        return m

    for i in range(W_AHEAD):
        load_weights(i)
    SLOTS_AHEAD = 3
    for i in range(SLOTS_AHEAD):
        load_slots(i)
    turned = {0: turn(0)}
    held = None
    for i in range(BLOCKS):
        if i + SLOTS_AHEAD < BLOCKS:
            load_slots(i + SLOTS_AHEAD)
        if i + 1 < BLOCKS:
            turned[i + 1] = turn(i + 1)
        xT, w = turned.pop(i)
        h = up(i, xT)
        if held is not None:
            done = add(held[0], down(*held))
        if i + W_AHEAD < BLOCKS:
            load_weights(i + W_AHEAD)
        held = (i, h, w)
    done = add(held[0], down(*held))
    SP.wait(done)

    block = es.enter_context(nc.Block())

    @block.sync
    def _(_engine):
        SP.play()

    @block.tensor
    def _(_engine):
        PE.play()

    @block.vector
    def _(_engine):
        DV.play()

    @block.scalar
    def _(_engine):
        AC.play()

    @block.gpsimd
    def _(_engine):
        PO.play()

    es.close()


def kernel(**inputs):
    import numpy as np
    import concourse.bacc as bacc
    from concourse.bass_utils import run_bass_kernel_spmd

    nc = bacc.Bacc("TRN2", target_bir_lowering=False, num_devices=1)
    arrays, aps = {}, {}
    for name, value in inputs.items():
        v = np.ascontiguousarray(value)
        arrays[f"in_{name}"] = v
        aps[name] = nc.dram_tensor(f"in_{name}", v.shape, mybir.dt.from_np(v.dtype), kind="ExternalInput").ap()
    out = nc.dram_tensor("out_x", (NB * S + P, D), F32, kind="ExternalOutput").ap()
    build(nc, aps, out)
    r = run_bass_kernel_spmd(nc, [arrays], core_ids=[0])
    return r.results[0]["out_x"][0:NB * S].reshape(NB, S, D)
```
